# Optimizing a Trainium2 kernel written in Bass

```python
import numpy as np
import jax
import jax.numpy as jnp

def _softmax(x, axis=-1):
    return jax.nn.softmax(x, axis=axis)

def _gelu(x):
    return jax.nn.gelu(x, approximate=True)

def _silu(x):
    return jax.nn.silu(x)

def _sigmoid(x):
    return jax.nn.sigmoid(x)

def _layernorm(x, axis=-1, eps=1e-05):
    m = jnp.mean(x, axis=axis, keepdims=True)
    v = jnp.var(x, axis=axis, keepdims=True)
    return (x - m) / jnp.sqrt(v + eps)

def _scatter_add(tgt, idx, src, axis=0):
    return tgt.at[idx].add(src)

def _segment_sum(src, seg, n):
    return jax.ops.segment_sum(src, seg, n)
kernel_name = 'mk_adaln_d2_jaxref_r8_dfc85b'

def setup_inputs(seed: int=0):
    np.random.seed(seed)
    _w = jnp.asarray

    def _L0_attn_setup():
        import jax, jax.numpy as jnp
        import numpy as np
        D_MODEL = 256
        N_HEADS = 16
        D_HEAD = D_MODEL // N_HEADS
        B, S = (2, 256)
        EPS = 1e-05

        def _mhsa(X, ln_g, ln_b, Wq, bq, Wk, bk, Wv, bv, Wo, bo):
            n_ctx = X.shape[-2]
            mu = jnp.mean(X, axis=-1, keepdims=True)
            var = jnp.mean(jnp.square(X - mu), axis=-1, keepdims=True)
            Xn = (X - mu) * jax.lax.rsqrt(var + EPS) * ln_g + ln_b

            def split_heads(t):
                return t.reshape(t.shape[:-1] + (N_HEADS, D_HEAD)).swapaxes(-2, -3)
            Q = split_heads(Xn @ Wq + bq)
            K = split_heads(Xn @ Wk + bk)
            V = split_heads(Xn @ Wv + bv)
            scores = jnp.einsum('bhqd,bhkd->bhqk', Q, K) / jnp.sqrt(jnp.float32(D_HEAD))
            causal = jnp.tril(jnp.ones((n_ctx, n_ctx), dtype=bool))
            scores = jnp.where(causal, scores, jnp.float32(-jnp.inf))
            A = jax.nn.softmax(scores, axis=-1)
            AV = jnp.einsum('bhqk,bhkd->bhqd', A, V)
            AV = AV.swapaxes(-2, -3).reshape(X.shape[:-1] + (D_MODEL,))
            return AV @ Wo + bo
        key = jax.random.key(seed)
        ks = jax.random.split(key, 10)
        sd = 1.0 / np.sqrt(D_MODEL)
        inp = {'X': jax.random.normal(ks[0], (B, S, D_MODEL), dtype=jnp.float32), 'ln_g': jnp.ones((D_MODEL,), jnp.float32), 'ln_b': jnp.zeros((D_MODEL,), jnp.float32), 'Wq': jax.random.uniform(ks[1], (D_MODEL, D_MODEL), jnp.float32, -sd, sd), 'bq': jax.random.uniform(ks[2], (D_MODEL,), jnp.float32, -sd, sd), 'Wk': jax.random.uniform(ks[3], (D_MODEL, D_MODEL), jnp.float32, -sd, sd), 'bk': jax.random.uniform(ks[4], (D_MODEL,), jnp.float32, -sd, sd), 'Wv': jax.random.uniform(ks[5], (D_MODEL, D_MODEL), jnp.float32, -sd, sd), 'bv': jax.random.uniform(ks[6], (D_MODEL,), jnp.float32, -sd, sd), 'Wo': jax.random.uniform(ks[7], (D_MODEL, D_MODEL), jnp.float32, -sd, sd), 'bo': jax.random.uniform(ks[8], (D_MODEL,), jnp.float32, -sd, sd)}
        return inp
    _L0_attn_in = _L0_attn_setup()

    def _L0_ffn_setup():
        import jax, jax.numpy as jnp
        import numpy as np
        HIDDEN = 256
        EXPERT_FF = 176
        NUM_EXPERTS = 16
        NUM_SHARED = 2
        SHARED_FF = EXPERT_FF * NUM_SHARED
        TOP_K = 4
        SCALE = 1.0
        BATCH, SEQ = (1, 256)

        def _moe_forward(hidden_states, Wg, W1, W2, W3, W1s, W2s, W3s):
            B, S, D = hidden_states.shape
            x = hidden_states.reshape(-1, D)
            T = x.shape[0]
            E = Wg.shape[0]
            shared = jax.nn.silu(x @ W1s.T) * (x @ W3s.T) @ W2s.T
            logits = x @ Wg.T
            probs = jax.nn.softmax(logits.astype(jnp.float32), axis=-1)
            topk_w, sel = jax.lax.top_k(probs, TOP_K)
            topk_w = topk_w.astype(x.dtype) * SCALE
            combine = jnp.zeros((T, E), x.dtype).at[jnp.arange(T)[:, None], sel].add(topk_w)
            h = jax.nn.silu(jnp.einsum('td,efd->etf', x, W1)) * jnp.einsum('td,efd->etf', x, W3)
            routed = jnp.einsum('etf,edf->td', h * combine.T[:, :, None], W2)
            return (shared + routed).reshape(B, S, D)
        key = jax.random.key(seed)
        ks = jax.random.split(key, 8)
        std = 0.02
        return {'hidden_states': jax.random.normal(ks[0], (BATCH, SEQ, HIDDEN), dtype=jnp.float32), 'Wg': jax.random.normal(ks[1], (NUM_EXPERTS, HIDDEN), dtype=jnp.float32) * std, 'W1': jax.random.normal(ks[2], (NUM_EXPERTS, EXPERT_FF, HIDDEN), dtype=jnp.float32) * std, 'W2': jax.random.normal(ks[3], (NUM_EXPERTS, HIDDEN, EXPERT_FF), dtype=jnp.float32) * std, 'W3': jax.random.normal(ks[4], (NUM_EXPERTS, EXPERT_FF, HIDDEN), dtype=jnp.float32) * std, 'W1s': jax.random.normal(ks[5], (SHARED_FF, HIDDEN), dtype=jnp.float32) * std, 'W2s': jax.random.normal(ks[6], (HIDDEN, SHARED_FF), dtype=jnp.float32) * std, 'W3s': jax.random.normal(ks[7], (SHARED_FF, HIDDEN), dtype=jnp.float32) * std}
    _L0_ffn_in = _L0_ffn_setup()
    _L0_c = _w((lambda *s: np.random.randn(*s).astype(np.float32) * 0.05)(4, 256))
    _L0_wmod = _w((lambda *s: np.random.randn(*s).astype(np.float32) * 0.05)(256, 6 * 256) * 256 ** (-0.5))

    def _L1_attn_setup():
        import jax, jax.numpy as jnp
        import numpy as np
        from jax import lax
        D_MODEL = 256
        D_INNER = 512
        D_CONV = 4
        B, T = (4, 256)

        def _rmsnorm(h):
            n = jnp.sqrt(jnp.sum(h * h, axis=-1, keepdims=True))
            return h / jnp.maximum(n, 1e-12) * h.shape[-1] ** 0.5

        def _mamba_fallback(h, W_in, conv_w, conv_b, W_out):
            xz = jnp.einsum('btd,ed->bte', h, W_in)
            xp, z = jnp.split(xz, 2, axis=-1)
            xc = lax.conv_general_dilated(xp.transpose(0, 2, 1), conv_w, window_strides=(1,), padding=[(D_CONV - 1, 0)], dimension_numbers=('NCH', 'OIH', 'NCH'), feature_group_count=D_INNER) + conv_b[None, :, None]
            xc = xc.transpose(0, 2, 1)
            y = jax.nn.silu(xc) * jax.nn.silu(z)
            return jnp.einsum('bte,de->btd', y, W_out)
        key = jax.random.key(seed)
        ks = jax.random.split(key, 7)
        std = 0.02
        return {'x': jax.random.normal(ks[0], (B, T, D_MODEL), jnp.float32), 'W_in': jax.random.normal(ks[1], (2 * D_INNER, D_MODEL), jnp.float32) * std, 'conv_w': jax.random.normal(ks[2], (D_INNER, 1, D_CONV), jnp.float32) * std, 'conv_b': jnp.zeros((D_INNER,), jnp.float32), 'W_out': jax.random.normal(ks[3], (D_MODEL, D_INNER), jnp.float32) * std, 'W_mlp1': jax.random.normal(ks[4], (4 * D_MODEL, D_MODEL), jnp.float32) * std, 'W_mlp2': jax.random.normal(ks[5], (D_MODEL, 4 * D_MODEL), jnp.float32) * std}
    _L1_attn_in = _L1_attn_setup()

    def _L1_ffn_setup():
        import jax, jax.numpy as jnp
        import numpy as np
        B, S, D, FF, E = (4, 256, 256, 1024, 2)
        key = jax.random.key(seed)
        k0, k1, k2, k3, k4 = jax.random.split(key, 5)
        s = 0.02
        return {'hidden_states': jax.random.normal(k0, (B, S, D), jnp.float32), 'gate_w': jax.random.normal(k1, (E, D), jnp.float32) * s, 'w_gate': jax.random.normal(k2, (E, FF, D), jnp.float32) * s, 'w_up': jax.random.normal(k3, (E, FF, D), jnp.float32) * s, 'w_down': jax.random.normal(k4, (E, D, FF), jnp.float32) * s}
    _L1_ffn_in = _L1_ffn_setup()
    _L1_c = _w((lambda *s: np.random.randn(*s).astype(np.float32) * 0.05)(4, 256))
    _L1_wmod = _w((lambda *s: np.random.randn(*s).astype(np.float32) * 0.05)(256, 6 * 256) * 256 ** (-0.5))
    _d = {'L0_attn_X': _L0_attn_in['X'], 'L0_attn_ln_g': _L0_attn_in['ln_g'], 'L0_attn_ln_b': _L0_attn_in['ln_b'], 'L0_attn_Wq': _L0_attn_in['Wq'], 'L0_attn_bq': _L0_attn_in['bq'], 'L0_attn_Wk': _L0_attn_in['Wk'], 'L0_attn_bk': _L0_attn_in['bk'], 'L0_attn_Wv': _L0_attn_in['Wv'], 'L0_attn_bv': _L0_attn_in['bv'], 'L0_attn_Wo': _L0_attn_in['Wo'], 'L0_attn_bo': _L0_attn_in['bo'], 'L0_ffn_Wg': _L0_ffn_in['Wg'], 'L0_ffn_W1': _L0_ffn_in['W1'], 'L0_ffn_W2': _L0_ffn_in['W2'], 'L0_ffn_W3': _L0_ffn_in['W3'], 'L0_ffn_W1s': _L0_ffn_in['W1s'], 'L0_ffn_W2s': _L0_ffn_in['W2s'], 'L0_ffn_W3s': _L0_ffn_in['W3s'], 'L0_c': _L0_c, 'L0_wmod': _L0_wmod, 'L1_attn_W_in': _L1_attn_in['W_in'], 'L1_attn_conv_w': _L1_attn_in['conv_w'], 'L1_attn_conv_b': _L1_attn_in['conv_b'], 'L1_attn_W_out': _L1_attn_in['W_out'], 'L1_attn_W_mlp1': _L1_attn_in['W_mlp1'], 'L1_attn_W_mlp2': _L1_attn_in['W_mlp2'], 'L1_ffn_gate_w': _L1_ffn_in['gate_w'], 'L1_ffn_w_gate': _L1_ffn_in['w_gate'], 'L1_ffn_w_up': _L1_ffn_in['w_up'], 'L1_ffn_w_down': _L1_ffn_in['w_down'], 'L1_c': _L1_c, 'L1_wmod': _L1_wmod}
    _x0 = _d['L0_attn_X']
    _d['L0_attn_X'] = jax.random.normal(jax.random.fold_in(jax.random.key(seed), 1), (4, 512, 256), dtype=_x0.dtype)
    del _x0
    return _d

def reference(L0_attn_X, L0_attn_ln_g, L0_attn_ln_b, L0_attn_Wq, L0_attn_bq, L0_attn_Wk, L0_attn_bk, L0_attn_Wv, L0_attn_bv, L0_attn_Wo, L0_attn_bo, L0_ffn_Wg, L0_ffn_W1, L0_ffn_W2, L0_ffn_W3, L0_ffn_W1s, L0_ffn_W2s, L0_ffn_W3s, L0_c, L0_wmod, L1_attn_W_in, L1_attn_conv_w, L1_attn_conv_b, L1_attn_W_out, L1_attn_W_mlp1, L1_attn_W_mlp2, L1_ffn_gate_w, L1_ffn_w_gate, L1_ffn_w_up, L1_ffn_w_down, L1_c, L1_wmod):

    def _L0_attn_ref(X, ln_g, ln_b, Wq, bq, Wk, bk, Wv, bv, Wo, bo):
        import jax, jax.numpy as jnp
        import numpy as np
        D_MODEL = 256
        N_HEADS = 16
        D_HEAD = D_MODEL // N_HEADS
        B, S = (2, 256)
        EPS = 1e-05

        def _mhsa(X, ln_g, ln_b, Wq, bq, Wk, bk, Wv, bv, Wo, bo):
            n_ctx = X.shape[-2]
            mu = jnp.mean(X, axis=-1, keepdims=True)
            var = jnp.mean(jnp.square(X - mu), axis=-1, keepdims=True)
            Xn = (X - mu) * jax.lax.rsqrt(var + EPS) * ln_g + ln_b

            def split_heads(t):
                return t.reshape(t.shape[:-1] + (N_HEADS, D_HEAD)).swapaxes(-2, -3)
            Q = split_heads(Xn @ Wq + bq)
            K = split_heads(Xn @ Wk + bk)
            V = split_heads(Xn @ Wv + bv)
            scores = jnp.einsum('bhqd,bhkd->bhqk', Q, K) / jnp.sqrt(jnp.float32(D_HEAD))
            causal = jnp.tril(jnp.ones((n_ctx, n_ctx), dtype=bool))
            scores = jnp.where(causal, scores, jnp.float32(-jnp.inf))
            A = jax.nn.softmax(scores, axis=-1)
            AV = jnp.einsum('bhqk,bhkd->bhqd', A, V)
            AV = AV.swapaxes(-2, -3).reshape(X.shape[:-1] + (D_MODEL,))
            return AV @ Wo + bo
        return _mhsa(X, ln_g, ln_b, Wq, bq, Wk, bk, Wv, bv, Wo, bo)

    def _L0_ffn_ref(hidden_states, Wg, W1, W2, W3, W1s, W2s, W3s):
        import jax, jax.numpy as jnp
        import numpy as np
        HIDDEN = 256
        EXPERT_FF = 176
        NUM_EXPERTS = 16
        NUM_SHARED = 2
        SHARED_FF = EXPERT_FF * NUM_SHARED
        TOP_K = 4
        SCALE = 1.0
        BATCH, SEQ = (1, 256)

        def _moe_forward(hidden_states, Wg, W1, W2, W3, W1s, W2s, W3s):
            B, S, D = hidden_states.shape
            x = hidden_states.reshape(-1, D)
            T = x.shape[0]
            E = Wg.shape[0]
            shared = jax.nn.silu(x @ W1s.T) * (x @ W3s.T) @ W2s.T
            logits = x @ Wg.T
            probs = jax.nn.softmax(logits.astype(jnp.float32), axis=-1)
            topk_w, sel = jax.lax.top_k(probs, TOP_K)
            topk_w = topk_w.astype(x.dtype) * SCALE
            combine = jnp.zeros((T, E), x.dtype).at[jnp.arange(T)[:, None], sel].add(topk_w)
            h = jax.nn.silu(jnp.einsum('td,efd->etf', x, W1)) * jnp.einsum('td,efd->etf', x, W3)
            routed = jnp.einsum('etf,edf->td', h * combine.T[:, :, None], W2)
            return (shared + routed).reshape(B, S, D)
        return _moe_forward(hidden_states, Wg, W1, W2, W3, W1s, W2s, W3s)

    def _L1_attn_ref(x, W_in, conv_w, conv_b, W_out, W_mlp1, W_mlp2):
        import jax, jax.numpy as jnp
        import numpy as np
        from jax import lax
        D_MODEL = 256
        D_INNER = 512
        D_CONV = 4
        B, T = (4, 256)

        def _rmsnorm(h):
            n = jnp.sqrt(jnp.sum(h * h, axis=-1, keepdims=True))
            return h / jnp.maximum(n, 1e-12) * h.shape[-1] ** 0.5

        def _mamba_fallback(h, W_in, conv_w, conv_b, W_out):
            xz = jnp.einsum('btd,ed->bte', h, W_in)
            xp, z = jnp.split(xz, 2, axis=-1)
            xc = lax.conv_general_dilated(xp.transpose(0, 2, 1), conv_w, window_strides=(1,), padding=[(D_CONV - 1, 0)], dimension_numbers=('NCH', 'OIH', 'NCH'), feature_group_count=D_INNER) + conv_b[None, :, None]
            xc = xc.transpose(0, 2, 1)
            y = jax.nn.silu(xc) * jax.nn.silu(z)
            return jnp.einsum('bte,de->btd', y, W_out)
        h = _rmsnorm(x)
        x = x + _mamba_fallback(h, W_in, conv_w, conv_b, W_out)
        h = _rmsnorm(x)
        m = jnp.einsum('bte,de->btd', jax.nn.relu(jnp.einsum('btd,ed->bte', h, W_mlp1)), W_mlp2)
        return x + m

    def _L1_ffn_ref(hidden_states, gate_w, w_gate, w_up, w_down):
        import jax, jax.numpy as jnp
        import numpy as np
        B, S, D, FF, E = (4, 256, 256, 1024, 2)
        b, s, d = hidden_states.shape
        x = hidden_states.reshape(-1, d)
        logits = x @ gate_w.T
        probs = jax.nn.softmax(logits.astype(jnp.float32), axis=-1)
        sel = jnp.argmax(probs, axis=-1)
        top_w = jnp.take_along_axis(probs, sel[:, None], axis=-1)
        onehot = jax.nn.one_hot(sel, gate_w.shape[0], dtype=x.dtype)
        g = jnp.einsum('td,efd->etf', x, w_gate)
        u = jnp.einsum('td,efd->etf', x, w_up)
        h = jax.nn.silu(g) * u
        y = jnp.einsum('etf,edf->etd', h, w_down)
        out = jnp.einsum('etd,te->td', y, onehot * top_w)
        return out.reshape(b, s, d)
    x = L0_attn_X
    mod = (_silu(L0_c) @ L0_wmod).reshape(L0_c.shape[0], 6, 1, -1)
    sa, ca, ga, sb, cb, gb = (mod[:, 0], mod[:, 1], mod[:, 2], mod[:, 3], mod[:, 4], mod[:, 5])
    ga = (2 * (ga >= 0) - 1) * jnp.maximum(jnp.abs(ga), 0.25)
    gb = (2 * (gb >= 0) - 1) * jnp.maximum(jnp.abs(gb), 0.25)
    h = _layernorm(x, axis=-1) * (1 + ca) + sa
    x = x + ga * _L0_attn_ref(h, L0_attn_ln_g, L0_attn_ln_b, L0_attn_Wq, L0_attn_bq, L0_attn_Wk, L0_attn_bk, L0_attn_Wv, L0_attn_bv, L0_attn_Wo, L0_attn_bo)
    h = _layernorm(x, axis=-1) * (1 + cb) + sb
    x = x + gb * _L0_ffn_ref(h, L0_ffn_Wg, L0_ffn_W1, L0_ffn_W2, L0_ffn_W3, L0_ffn_W1s, L0_ffn_W2s, L0_ffn_W3s)
    mod = (_silu(L1_c) @ L1_wmod).reshape(L1_c.shape[0], 6, 1, -1)
    sa, ca, ga, sb, cb, gb = (mod[:, 0], mod[:, 1], mod[:, 2], mod[:, 3], mod[:, 4], mod[:, 5])
    ga = (2 * (ga >= 0) - 1) * jnp.maximum(jnp.abs(ga), 0.25)
    gb = (2 * (gb >= 0) - 1) * jnp.maximum(jnp.abs(gb), 0.25)
    h = _layernorm(x, axis=-1) * (1 + ca) + sa
    x = x + ga * _L1_attn_ref(h, L1_attn_W_in, L1_attn_conv_w, L1_attn_conv_b, L1_attn_W_out, L1_attn_W_mlp1, L1_attn_W_mlp2)
    h = _layernorm(x, axis=-1) * (1 + cb) + sb
    x = x + gb * _L1_ffn_ref(h, L1_ffn_gate_w, L1_ffn_w_gate, L1_ffn_w_up, L1_ffn_w_down)
    return x

_drawn_inputs = setup_inputs


def setup_inputs(seed=0):
    import zlib

    import numpy as np

    out = dict(_drawn_inputs(seed))
    spreads = {'L0_attn_ln_g': (1.0, 0.6), 'L0_attn_ln_b': (0.0, 0.8), 'L1_attn_conv_b': (0.0, 0.8)}
    factors = {'L0_attn_Wq': 8.0,
     'L0_attn_bq': 8.0,
     'L0_attn_Wk': 8.0,
     'L0_attn_bk': 8.0,
     'L0_attn_Wv': 4.009,
     'L0_attn_bv': 8.0,
     'L0_attn_Wo': 3.742,
     'L0_attn_bo': 6.464,
     'L0_ffn_Wg': 8.0,
     'L0_ffn_W1': 8.0,
     'L0_ffn_W2': 8.0,
     'L0_ffn_W3': 8.0,
     'L0_ffn_W1s': 8.0,
     'L0_ffn_W2s': 8.0,
     'L0_ffn_W3s': 8.0,
     'L0_c': 3.335,
     'L0_wmod': 3.222,
     'L1_attn_W_in': 8.0,
     'L1_attn_conv_w': 8.0,
     'L1_attn_W_out': 8.0,
     'L1_ffn_gate_w': 8.0,
     'L1_ffn_w_gate': 8.0,
     'L1_ffn_w_up': 8.0,
     'L1_ffn_w_down': 8.0}
    for name, (base, spread) in spreads.items():
        noise = np.random.default_rng([zlib.crc32(name.encode()), seed]).standard_normal(out[name].shape)
        drawn = base * np.exp(spread * noise) if base else spread * noise
        out[name] = jnp.asarray(drawn.astype(out[name].dtype))
    for name, factor in factors.items():
        out[name] = (out[name] * factor).astype(out[name].dtype)
    return out
```

```python
from contextlib import ExitStack

import concourse.bass as bass
from concourse import mybir

F32 = mybir.dt.float32
F32R = mybir.dt.float32r
BF16 = mybir.dt.bfloat16
ALU = mybir.AluOpType
ACT = mybir.ActivationFunctionType
AX_X = mybir.AxisListType.X

P = 128
D = 256
DM = D // P
B, T = 4, 512
NT = B * T // P
TT = T // P
HEADS, DH = 16, 16
QUADS = HEADS // 4
EPS = 1e-5
L0_EXPERTS, L0_TOPK, L0_FF, L0_SHARED = 16, 4, 176, 352
L0_TILES = -(-(L0_EXPERTS * L0_FF + L0_SHARED) // P)
L1_EXPERTS, L1_FF = 2, 1024
L1_TILES = L1_EXPERTS * L1_FF // P
INNER, TAPS = 512, 4
IT = INNER // P
MLP_T = 4 * D // P
GROW = 32
ONE = 16
MASKED = -3.0e38
SA, CA, GA, SB, CB, GB = range(6)


def f32(ap):
    return ap.bitcast(F32)


def split3(pe, out, w_hi, w_lo, x_hi, x_lo, first, last):
    pe.matmul(out, w_hi, x_lo, start=first, stop=False)
    pe.matmul(out, w_lo, x_hi, start=False, stop=False)
    return pe.matmul(out, w_hi, x_hi, start=False, stop=last)


def wait(eng, sem, n):
    if not isinstance(n, int) or n > 0:
        eng.wait_ge(sem, n)


def over_batches(eng, batch):
    batch(0)
    with eng.Fori(1, B) as b:
        batch(b)


class Chain:

    def __init__(self, eng, sem, start=0):
        self.eng, self.sem, self.n = eng, sem, start

    def link(self, ins):
        ins.then_inc(self.sem, 1)
        self.n = self.n + 1
        return self.n

    def wait(self, n=None):
        self.eng.wait_ge(self.sem, self.n if n is None else n)


class Core:

    def __init__(self, nc, ctx):
        self.nc, self.ctx, self.sems = nc, ctx, []
        sb, dram = self.sb, self.dram
        self.PS = ctx.enter_context(nc.psum_tensor("PS", [P, 8, 512], F32))
        self.X = sb("X", [P, NT, D], F32)
        self.ident = sb("ident", [P, P], F32)
        self.identb = sb("identb", [P, P], BF16)
        self.mhalf = sb("mhalf", [P, TT], F32)
        self.maskb = sb("maskb", [P, P], BF16)
        self.modc = sb("modc", [P, 2, 6, DM, B], F32)
        self.rows = sb("rows", [P, 2, 3, B, D], F32)
        self.q_parts = dram("q_parts", [B, QUADS, 4, 2, DH, T])
        self.k_parts = dram("k_parts", [B, QUADS, 4, 2, DH, T])
        self.v_parts = dram("v_parts", [B, TT, P, HEADS, 2 * DH])

    def sb(self, name, shape, dt, ctx=None):
        return (ctx or self.ctx).enter_context(self.nc.sbuf_tensor(name, shape, dt))

    def dram(self, name, shape):
        return self.nc.dram_tensor(name, shape, F32, kind="Internal").ap()

    def sem(self, name):
        sem = self.nc.alloc_semaphore(name=name)
        self.sems.append(sem)
        return sem

    def recycle(self):
        self.nc.clear_and_free_semaphores(self.sems)
        self.nc.all_engine_barrier()
        self.sems = []


def setup(k, x, cT, wmod0, wmod1):
    nc = k.nc
    with ExitStack() as c:
        cs = k.sb("cs", [P, 2, DM, B], F32, c)
        scT = k.sb("scT", [P, 2, DM, B], F32, c)
        scB = k.sb("scB", [P, 2, DM, B, P], F32, c)
        wm = k.sb("wm", [P, 2, DM, 6 * D], F32, c)
        sgn = k.sb("sgn", [P, B, D], F32, c)
        mag = k.sb("mag", [P, B, D], F32, c)
        zero = k.sb("zero", [P, P], F32, c)
        x_in, c_in, w_in = k.sem("x_in"), k.sem("c_in"), k.sem("wm_in")
        silu_done, cols_ready, rows_ready = k.sem("silu_done"), k.sem("cols_ready"), k.sem("rows_ready")
        rows_taken, pool_own, dve_own = k.sem("rows_taken"), k.sem("setup_pool"), k.sem("setup_dve")
        cols = k.PS[:, 0, 0:2 * 12 * B].rearrange("p (l j b) -> p l j b", l=2, j=12)
        block = c.enter_context(nc.Block())

        @block.sync
        def _(sp):
            sp.dma_start(cs[:], cT).then_inc(c_in, 16)
            for l, w in enumerate((wmod0, wmod1)):
                sp.dma_start(wm[:, l], w.rearrange("(m p) n -> p m n", p=P)).then_inc(w_in, 16)
            sp.dma_start(k.X[:], x.rearrange("(t p) d -> p t d", p=P)).then_inc(x_in, 16)
            sp.wait_ge(x_in, 16)

        @block.gpsimd
        def _(pool):
            own = Chain(pool, pool_own)
            own.link(pool.memset(k.ident[:], 0.0))
            own.link(pool.memset(k.maskb[:], 0.0))
            own.link(pool.memset(k.mhalf[:], -0.5))
            own.wait()
            own.link(pool.affine_select(out=k.ident[:], in_=k.ident[:], compare_op=ALU.not_equal, fill=1.0,
                                        base=0, pattern=[[-1, P]], channel_multiplier=1))
            own.link(pool.affine_select(out=k.maskb[:], in_=k.maskb[:], compare_op=ALU.is_ge, fill=MASKED,
                                        base=0, pattern=[[-1, P]], channel_multiplier=1))
            own.wait()
            own.link(pool.tensor_copy(k.identb[:], k.ident[:]))
            own.wait()

        @block.scalar
        def _(act):
            act.wait_ge(c_in, 16)
            act.activation(scT[:], cs[:], ACT.Silu).then_inc(silu_done, 1)

        @block.tensor
        def _(pe):
            pe.wait_ge(silu_done, 1)
            pe.wait_ge(w_in, 32)
            for l in range(2):
                for j in range(12):
                    for m in range(DM):
                        last = pe.matmul(cols[:, l, j, :], wm[:, l, m, j * P:(j + 1) * P], scT[:, l, m, :],
                                         start=(m == 0), stop=(m == DM - 1))
            last.then_inc(cols_ready, 1)
            pe.wait_ge(dve_own, 1)
            n = 0
            for l in range(2):
                for b in range(B):
                    for lo, hi in ((0, 2 * D), (2 * D, 3 * D))[:1 + l]:
                        if n >= 4:
                            pe.wait_ge(rows_taken, n - 3)
                        for m in range(DM):
                            last = pe.matmul(k.PS[:, 1 + n % 4, 0:hi - lo], scB[:, l, m, b, :], wm[:, l, m, lo:hi],
                                             start=(m == 0), stop=(m == DM - 1))
                        last.then_inc(rows_ready, 1)
                        n += 1

        @block.vector
        def _(dve):
            own = Chain(dve, dve_own)
            dve.wait_ge(silu_done, 1)
            own.link(dve.tensor_copy(scB[:], scT[:].unsqueeze(4).to_broadcast([P, 2, DM, B, P])))
            dve.wait_ge(cols_ready, 1)
            own.link(dve.tensor_copy(k.modc[:].rearrange("p l c m b -> p (l c m b)"),
                                     cols.rearrange("p l j b -> p (l j b)")))
            own.wait()
            for l in range(2):
                for part in (CA, CB):
                    own.link(dve.tensor_scalar(k.modc[:, l, part], k.modc[:, l, part], 1.0, None, ALU.add))

            def gate(v, s, a):
                own.link(dve.tensor_scalar(s, v, 0.0, 2.0, ALU.is_ge, ALU.mult))
                own.link(dve.scalar_tensor_tensor(out=a, in0=v, scalar=-1.0, in1=v, op0=ALU.mult, op1=ALU.max))
                own.wait()
                own.link(dve.tensor_scalar(s, s, -1.0, None, ALU.add))
                own.wait()
                own.link(dve.scalar_tensor_tensor(out=v, in0=a, scalar=0.25, in1=s, op0=ALU.max, op1=ALU.mult))
                own.wait()

            for l in range(2):
                for part in (GA, GB):
                    gate(k.modc[:, l, part], sgn[:, 0, 0:DM * B].rearrange("p (m b) -> p m b", m=DM),
                         mag[:, 0, 0:DM * B].rearrange("p (m b) -> p m b", m=DM))
            n = 0
            for l in range(2):
                for b in range(B):
                    for parts in ((SA, CA), (GA,))[:1 + l]:
                        dve.wait_ge(rows_ready, n + 1)
                        for i, part in enumerate(parts):
                            src = k.PS[:, 1 + n % 4, i * D:(i + 1) * D]
                            last = dve.tensor_scalar(k.rows[:, l, part, b, :], src,
                                                     1.0 if part == CA else 0.0, None, ALU.add)
                        last.then_inc(rows_taken, 1)
                        n += 1
            dve.wait_ge(rows_taken, n)
            gate(k.rows[:, 1, GA], sgn[:], mag[:])


def row_stats(own, dve, src, stats, mv):
    for t in range(TT):
        own.link(dve.bn_stats(stats[:, t, :], src(t)))
    own.wait()
    own.link(dve.tensor_copy(stats[:, TT, 0:1], stats[:, 0, 0:1]))
    for t in range(TT):
        own.link(dve.bn_aggr(mv[:, t, :], stats[:, t, :]))
    own.wait()


STATS_OPS = 2 * TT + 1


def attention_inputs(k, w, ln_gb, bqk, bv_row):
    nc = k.nc
    with ExitStack() as c:
        wst = k.sb("wst", [P, 3, DM, D], F32, c)
        whi = k.sb("whi", [P, 3, DM, D], F32R, c)
        wlo = k.sb("wlo", [P, 3, DM, D], F32R, c)
        gb = k.sb("gb", [P, 2, DM], F32, c)
        bq = k.sb("bq", [P, 2, DM], F32, c)
        bv = k.sb("bv", [P, D], F32, c)
        stats = k.sb("stats", [P, TT + 1, 6], F32, c)
        mv = k.sb("mv", [P, TT, 2], F32, c)
        var = k.sb("var", [P, TT], F32, c)
        rs = k.sb("rs", [P, TT], F32, c)
        xh = k.sb("xh", [P, TT, D], F32, c)
        h = k.sb("h", [P, TT, D], F32, c)
        hn = k.sb("hn", [P, TT, D], F32, c)
        hf = k.sb("hf", [P, DM, T], F32, c)
        hhi = k.sb("hhi", [P, DM, T], F32R, c)
        hlo = k.sb("hlo", [P, DM, T], F32R, c)
        qf = k.sb("qf", [P, 4, T], F32, c)
        qhi = k.sb("qhi", [P, 4, T], F32R, c)
        qlo = k.sb("qlo", [P, 4, T], F32R, c)
        vf = k.sb("vf", [P, TT, D], F32, c)
        vp = k.sb("vp", [P, TT, HEADS, 2, DH], F32R, c)
        S = lambda n: k.sem("a1_" + n)
        par_in, w_split, own_dve, own_act = S("par_in"), S("w_split"), S("dve"), S("act")
        var_ready, root_done, hn_ready, hT_ready = S("var_ready"), S("root_done"), S("hn_ready"), S("hT_ready")
        hf_done, hhi_done, hlo_done = S("hf_done"), S("hhi_done"), S("hlo_done")
        q_ready, q_done, qhi_done, qlo_done = S("q_ready"), S("q_done"), S("qhi_done"), S("qlo_done")
        v_ready, vf_done, vhi_done, vlo_done = S("v_ready"), S("vf_done"), S("vhi_done"), S("vlo_done")
        q_out, v_out = S("q_out"), S("v_out")
        block = c.enter_context(nc.Block())

        @block.sync
        def _(sp):
            sp.dma_start(gb[:], ln_gb).then_inc(par_in, 16)
            sp.dma_start(bq[:], bqk).then_inc(par_in, 16)
            sp.dma_start(bv[:], bv_row.partition_broadcast(P)).then_inc(par_in, 16)
            for i in range(3):
                sp.dma_start(wst[:, i], w[i].rearrange("(m p) n -> p m n", p=P)).then_inc(par_in, 16)
            def batch(b):
                for j in range(4):
                    wait(sp, qhi_done, b * 4 + j + 1)
                    wait(sp, qlo_done, b * 4 + j + 1)
                    dst = (k.q_parts, k.k_parts)[j // 2]
                    for part, tile in enumerate((qhi, qlo)):
                        sp.dma_start(dst[b, 2 * (j % 2):2 * (j % 2) + 2, :, part].rearrange("q s r t -> (q s) r t"),
                                     f32(tile[:, j, :])).then_inc(q_out, 16)
                wait(sp, vhi_done, (b + 1) * 2)
                wait(sp, vlo_done, (b + 1) * 2)
                sp.dma_start(k.v_parts[b].rearrange("t p h d -> p t (h d)"),
                             f32(vp[:].rearrange("p t h a d -> p t (h a d)"))).then_inc(v_out, 16)
            over_batches(sp, batch)
            sp.wait_ge(q_out, B * 8 * 16)
            sp.wait_ge(v_out, B * 16)

        @block.gpsimd
        def _(pool):
            def batch(b):
                for i in range(2):
                    wait(pool, var_ready, b * 2 + i + 1)
                    pool.tensor_tensor(rs[:], var[:], k.mhalf[:, 0:TT], ALU.pow).then_inc(root_done, 1)
            over_batches(pool, batch)

        @block.scalar
        def _(act):
            act.wait_ge(par_in, 96)
            act.activation(whi[:], wst[:], ACT.Copy).then_inc(w_split, 1)
            act.mul(bq[:, 0], bq[:, 0], 0.25).then_inc(own_act, 1)
            act.wait_ge(own_act, 1)
            def batch(b):
                for m in range(DM):
                    wait(act, hT_ready, b * DM + m + 1)
                    wait(act, hlo_done, b * DM)
                    act.activation(hf[:, m, :], k.PS[:, m, :], ACT.Identity, scale=gb[:, 0, m:m + 1],
                                   bias=gb[:, 1, m:m + 1]).then_inc(hf_done, 1)
                for m in range(DM):
                    wait(act, hf_done, b * DM + m + 1)
                    wait(act, v_ready, b * 2)
                    act.activation(hhi[:, m, :], hf[:, m, :], ACT.Copy).then_inc(hhi_done, 1)
                for j in range(4):
                    wait(act, q_ready, b * 4 + j + 1)
                    wait(act, q_out, b * 128)
                    act.activation(qf[:, j, :], k.PS[:, 2 + j, :], ACT.Identity, scale=(0.25 if j < 2 else 1.0),
                                   bias=bq[:, j // 2, j % 2:j % 2 + 1]).then_inc(q_done, 1)
                    wait(act, q_done, b * 4 + j + 1)
                    act.activation(qhi[:, j, :], qf[:, j, :], ACT.Copy).then_inc(qhi_done, 1)
                for g in range(2):
                    wait(act, vf_done, b * 2 + g + 1)
                    wait(act, v_out, b * 16)
                    for t in (2 * g, 2 * g + 1):
                        last = act.activation(vp[:, t, :, 0, :], vf[:, t, :].rearrange("p (h d) -> p h d", d=DH), ACT.Copy)
                    last.then_inc(vhi_done, 1)
            over_batches(act, batch)

        @block.vector
        def _(dve):
            dve.wait_ge(par_in, 96)
            dve.wait_ge(w_split, 1)
            dve.tensor_tensor(wlo[:], wst[:], f32(whi[:]), ALU.subtract).then_inc(w_split, 1)
            per = 2 * STATS_OPS + TT + 2
            def batch(b):
                own = Chain(dve, own_dve, b * per)
                row_stats(own, dve, lambda t: k.X[:, b * TT + t, :], stats, mv)
                dve.tensor_scalar(var[:], mv[:, :, 1], EPS, None, ALU.add).then_inc(var_ready, 1)
                wait(dve, root_done, b * 2 + 1)
                for t in range(TT):
                    own.link(dve.tensor_scalar(xh[:, t, :], k.X[:, b * TT + t, :], mv[:, t, 0:1], rs[:, t:t + 1],
                                               ALU.subtract, ALU.mult))
                own.wait()
                row = lambda part: k.rows[:, 0, part, b, :].unsqueeze(1).to_broadcast([P, TT, D])
                own.link(dve.tensor_tensor(h[:], xh[:], row(CA), ALU.mult))
                own.wait()
                own.link(dve.tensor_tensor(h[:], h[:], row(SA), ALU.add))
                own.wait()
                row_stats(own, dve, lambda t: h[:, t, :], stats, mv)
                dve.tensor_scalar(var[:], mv[:, :, 1], EPS, None, ALU.add).then_inc(var_ready, 1)
                wait(dve, root_done, b * 2 + 2)
                wait(dve, hT_ready, b * DM)
                for t in range(TT):
                    dve.tensor_scalar(hn[:, t, :], h[:, t, :], mv[:, t, 0:1], rs[:, t:t + 1],
                                      ALU.subtract, ALU.mult).then_inc(hn_ready, 1)
                for m in range(DM):
                    wait(dve, hhi_done, b * DM + m + 1)
                    dve.tensor_tensor(hlo[:, m, :], hf[:, m, :], f32(hhi[:, m, :]), ALU.subtract).then_inc(hlo_done, 1)
                for j in range(4):
                    wait(dve, qhi_done, b * 4 + j + 1)
                    dve.tensor_tensor(qlo[:, j, :], qf[:, j, :], f32(qhi[:, j, :]), ALU.subtract).then_inc(qlo_done, 1)
                for g in range(2):
                    wait(dve, v_ready, b * 2 + g + 1)
                    wait(dve, vlo_done, b * 2)
                    dve.tensor_tensor(vf[:, 2 * g:2 * g + 2, :], k.PS[:, 6 + g, :].rearrange("p (t d) -> p t d", t=2),
                                      bv[:].unsqueeze(1).to_broadcast([P, 2, D]), ALU.add).then_inc(vf_done, 1)
                for g in range(2):
                    wait(dve, vhi_done, b * 2 + g + 1)
                    for t in (2 * g, 2 * g + 1):
                        last = dve.tensor_tensor(vp[:, t, :, 1, :], vf[:, t, :].rearrange("p (h d) -> p h d", d=DH),
                                                 f32(vp[:, t, :, 0, :]), ALU.subtract)
                    last.then_inc(vlo_done, 1)
            over_batches(dve, batch)

        @block.tensor
        def _(pe):
            pe.wait_ge(w_split, 2)
            def batch(b):
                for m in range(DM):
                    wait(pe, hf_done, b * DM)
                    for t in range(TT):
                        wait(pe, hn_ready, b * TT + t + 1)
                        last = pe.transpose(k.PS[:, m, t * P:(t + 1) * P], hn[:, t, m * P:(m + 1) * P], k.ident[:])
                    last.then_inc(hT_ready, 1)
                wait(pe, hlo_done, (b + 1) * DM)
                wait(pe, q_done, b * 4)
                for j in range(4):
                    i, m = j // 2, j % 2
                    for d in range(DM):
                        last = split3(pe, k.PS[:, 2 + j, :], whi[:, i, d, m * P:(m + 1) * P], wlo[:, i, d, m * P:(m + 1) * P],
                                      hhi[:, d, :], hlo[:, d, :], d == 0, d == DM - 1)
                    last.then_inc(q_ready, 1)
                wait(pe, vf_done, b * 2)
                for g in range(2):
                    for t in (2 * g, 2 * g + 1):
                        out = k.PS[:, 6 + g, (t % 2) * D:(t % 2 + 1) * D]
                        for d in range(DM):
                            last = split3(pe, out, hhi[:, d, t * P:(t + 1) * P], hlo[:, d, t * P:(t + 1) * P],
                                          whi[:, 2, d, :], wlo[:, 2, d, :], d == 0, d == DM - 1)
                    last.then_inc(v_ready, 1)
            over_batches(pe, batch)


PT_AT = (0, 4 * P, 8 * P, 7 * P)
PT_BANKS = ((0, 4 * P), (4 * P, 4 * P), (8 * P, 2 * P))


def attention(k, OT, free):
    nc = k.nc
    NQ = B * QUADS
    with ExitStack() as c:
        Q4 = [k.sb(f"Q4_{u}", [P, 2, T], F32R, c) for u in range(2)]
        K4 = [k.sb(f"K4_{u}", [P, 4, T], F32R, c) for u in range(2)]
        V4 = [k.sb(f"V4_{u}", [P, TT, 4, P], F32R, c) for u in range(2)]
        PR = k.sb("PR", [P, 4, TT, T], F32, c)
        PThi = k.sb("PThi", [P, 2, 10 * P], F32R, c)
        PTlo = k.sb("PTlo", [P, 2, 10 * P], F32R, c)
        nmax = k.sb("nmax", [P, 4, TT], F32, c)
        rsum = k.sb("rsum", [P, 4, TT], F32, c)
        rinv = k.sb("rinv", [P, 4, TT], F32, c)
        carry = k.sb("carry", [P, 8], F32, c)
        S = lambda n: k.sem("a2_" + n)
        zeroed = S("zeroed")
        k_in, q_in, v_in = ([S(f"{n}_in{u}") for u in range(2)] for n in "kqv")
        s_ready, max_done, exp_done, inv_done, norm_done = S("s_ready"), S("max_done"), S("exp_done"), S("inv_done"), S("norm_done")
        t_ready, hi_done, lo_done, av_done, o_hi, o_lo = S("t_ready"), S("hi_done"), S("lo_done"), S("av_done"), S("o_hi"), S("o_lo")
        O = k.PS[:, 7, :]
        block = c.enter_context(nc.Block())
        LT, LA = 2, 3
        ITERS = NQ // 2

        @block.sync
        def _(sp):
            sp.wait_ge(zeroed, 4)
            def batch(b):
                for qp in range(QUADS // 2):
                    it = b * (QUADS // 2) + qp
                    for u in range(2):
                        wait(sp, s_ready, it * 32)
                        for s in range(4):
                            r = 64 * (s % 2)
                            src = k.k_parts[b, qp * 2 + u, s].rearrange("a r t -> (a r) t")
                            for dup in range(2):
                                sp.dma_start(f32(K4[u][r + 32 * dup:r + 32 * dup + 32, s, :]), src).then_inc(k_in[u], 16)
                            src = k.q_parts[b, qp * 2 + u, s]
                            sp.dma_start(f32(Q4[u][r:r + 32, s // 2, :]), src.rearrange("a r t -> (a r) t")).then_inc(q_in[u], 16)
                            for dup in range(2):
                                sp.dma_start(f32(Q4[u][r + 32 + 16 * dup:r + 48 + 16 * dup, s // 2, :]), src[1 - dup]).then_inc(q_in[u], 16)
                    for u in range(2):
                        wait(sp, av_done, it * 8)
                        for s in range(4):
                            sp.dma_start(f32(V4[u][:, :, s, 32 * s:32 * s + 32]),
                                         k.v_parts[b].rearrange("t p h d -> p t h d")[:, :, (qp * 2 + u) * 4 + s, :]).then_inc(v_in[u], 16)
            over_batches(sp, batch)

        @block.gpsimd
        def _(pool):
            for u in range(2):
                pool.memset(f32(K4[u][:]), 0.0).then_inc(zeroed, 1)
                pool.memset(f32(V4[u][:]), 0.0).then_inc(zeroed, 1)
            with pool.Fori(0, ITERS) as it:
                for e in range(8):
                    pool.wait_ge(inv_done, it * 8 + e + 1)
                    pool.tensor_tensor(carry[:, e:e + 1], rinv[:, e % 4, 0:1], rinv[:, e % 4, 0:1], ALU.mult)
                    for i in range(TT):
                        w = P * (i + 1)
                        pool.tensor_scalar(PR[:, e % 4, i, 0:w], PR[:, e % 4, i, 0:w], rinv[:, e % 4, i:i + 1], 1.0,
                                           ALU.mult, ALU.mult).then_inc(norm_done, 1)

        def loop(eng, body):
            body(0, True, False)
            with eng.Fori(1, ITERS) as it:
                body(it, False, False)
            body(ITERS, False, True)

        @block.tensor
        def _(pe):
            def body(it, first, last):
                for e in range(8):
                    h = it * 8 + e
                    u, s = e // 4, e % 4
                    if not last:
                        if s == 0:
                            pe.wait_ge(k_in[u], it * 128 + 128)
                            pe.wait_ge(q_in[u], it * 192 + 192)
                        for i in range(TT):
                            w = P * (i + 1)
                            if not (first and e == 0):
                                pe.wait_ge(exp_done, (h - 1) * TT + i + 1)
                            pe.matmul(k.PS[:, i, 0:w], Q4[u][:, s // 2, P * i:P * i + P], K4[u][:, s, 0:w], start=True, stop=False)
                            pe.matmul(k.PS[:, i, w - P:w], k.identb[:], k.maskb[:], start=False, stop=True).then_inc(s_ready, 1)
                    if (not last or e < LT) and not (first and e < LT):
                        g = h - LT
                        for i in range(TT):
                            pe.wait_ge(norm_done, g * TT + i + 1)
                            for j in (0, 1, 3, 2):
                                if j > i:
                                    continue
                                if not (first and e == LT) and i == j:
                                    bank = (0, 1, 2, 1)[j]
                                    pe.wait_ge(lo_done, (g - 1) * 3 + bank + 1)
                                at = PT_AT[j] + P * (i - j)
                                ins = pe.transpose(k.PS[:, 4 + at // 512, at % 512:at % 512 + P],
                                                   PR[:, (e - LT) % 4, i, P * j:P * j + P], k.ident[:])
                                if i == 3 and j != 1:
                                    ins.then_inc(t_ready, 1)
                    if (not last or e < LA) and not (first and e < LA):
                        g, ge = h - LA, (e - LA) % 8
                        u, s = ge // 4, ge % 4
                        if s == 0:
                            pe.wait_ge(v_in[u], (it if e >= LA else it - 1) * 64 + 64)
                            if not (first and e == LA):
                                pe.wait_ge(o_lo, (it * 2 + u) if e >= LA else (it - 1) * 2 + u)
                        for j in (0, 1, 3, 2):
                            bank = (0, 1, 2, 1)[j]
                            pe.wait_ge(lo_done, g * 3 + bank + 1)
                            w = T - P * j
                            for part, pt in enumerate((PThi, PTlo)):
                                ins = pe.matmul(O[:, P * j:T], V4[u][:, j, s, :], pt[:, ge % 2, PT_AT[j]:PT_AT[j] + w],
                                                start=(s == 0 and j == 0 and part == 0), stop=(s == 3 and j == 2 and part == 1))
                        ins.then_inc(av_done, 1)
            loop(pe, body)

        @block.scalar
        def _(act):
            def body(it, first, last):
                for e in range(8):
                    h = it * 8 + e
                    if not last:
                        if not (first and e < 4):
                            act.wait_ge(t_ready, (h - 4) * 3 + 3)
                        for i in range(TT):
                            w = P * (i + 1)
                            act.wait_ge(max_done, h * TT + i + 1)
                            act.activation(PR[:, e % 4, i, 0:w], k.PS[:, i, 0:w], ACT.Exp, bias=nmax[:, e % 4, i:i + 1],
                                           accum_out=rsum[:, e % 4, i:i + 1]).then_inc(exp_done, 1)
                    if (not last or e < LT) and not (first and e < LT):
                        g = h - LT
                        if not (first and e < LT + 2):
                            act.wait_ge(av_done, g - 1)
                        for n, (at, w) in enumerate(PT_BANKS):
                            act.wait_ge(t_ready, g * 3 + n + 1)
                            act.activation(PThi[:, e % 2, at:at + w], k.PS[:, 4 + n, 0:w], ACT.Copy).then_inc(hi_done, 1)
                    if (not last or e < LA) and not (first and e < LA) and (e - LA) % 4 == 3:
                        q = it * 2 + (0 if e == 6 else -1)
                        act.wait_ge(av_done, (q + 1) * 4)
                        act.activation(OT[0][:, q, :], O, ACT.Copy).then_inc(o_hi, 1)
            loop(act, body)

        @block.vector
        def _(dve):
            def body(it, first, last):
                for e in range(8):
                    h = it * 8 + e
                    if not last:
                        for i in range(TT):
                            w = P * (i + 1)
                            dve.wait_ge(s_ready, h * TT + i + 1)
                            dve.tensor_reduce(nmax[:, e % 4, i:i + 1], k.PS[:, i, 0:w], AX_X, ALU.max, negate=True).then_inc(max_done, 1)
                    if (not last or e < LT) and not (first and e < LT):
                        g = h - LT
                        if not (first and e < LT + 2):
                            dve.wait_ge(av_done, g - 1)
                        for n, (at, w) in enumerate(PT_BANKS):
                            dve.wait_ge(hi_done, g * 3 + n + 1)
                            dve.tensor_tensor(PTlo[:, e % 2, at:at + w], k.PS[:, 4 + n, 0:w], f32(PThi[:, e % 2, at:at + w]),
                                              ALU.subtract).then_inc(lo_done, 1)
                    if not last:
                        dve.wait_ge(exp_done, h * TT + TT)
                        if not (first and e < 4):
                            dve.wait_ge(norm_done, (h - 4) * TT + TT)
                        dve.reciprocal(rinv[:, e % 4, :], rsum[:, e % 4, :]).then_inc(inv_done, 1)
                    if (not last or e < LA) and not (first and e < LA) and (e - LA) % 4 == 3:
                        q = it * 2 + (0 if e == 6 else -1)
                        dve.wait_ge(o_hi, q + 1)
                        dve.tensor_tensor(OT[1][:, q, :], O, f32(OT[0][:, q, :]), ALU.subtract).then_inc(o_lo, 1)
            loop(dve, body)


def attention_output(k, OT, wo, bo_col):
    nc = k.nc
    with ExitStack() as c:
        wst = k.sb("wo_st", [P, QUADS, D], F32, c)
        whi = k.sb("wo_hi", [P, QUADS, D], F32R, c)
        wlo = k.sb("wo_lo", [P, QUADS, D], F32R, c)
        bo = k.sb("bo", [P, DM], F32, c)
        gabo = k.sb("gabo", [P, DM, B], F32, c)
        yf = k.sb("yf", [P, DM, T], F32, c)
        S = lambda n: k.sem("a3_" + n)
        w_in, w_split, b_done = S("w_in"), S("w_split"), S("b_done")
        y_ready, yf_done, yT_ready, x_done = S("y_ready"), S("yf_done"), S("yT_ready"), S("x_done")
        block = c.enter_context(nc.Block())

        @block.sync
        def _(sp):
            for dup in range(2):
                for h in range(4):
                    sp.dma_start(wst[32 * h + 16 * dup:32 * h + 16 * dup + 16],
                                 wo.rearrange("(q h r) n -> h r q n", q=QUADS, h=4)[h]).then_inc(w_in, 16)
            sp.dma_start(bo[:], bo_col).then_inc(w_in, 16)

        @block.scalar
        def _(act):
            act.wait_ge(w_in, 9 * 16)
            act.activation(whi[:], wst[:], ACT.Copy).then_inc(w_split, 1)
            act.wait_ge(b_done, 1)
            def batch(b):
                for m in range(DM):
                    wait(act, y_ready, b * DM + m + 1)
                    wait(act, yT_ready, b * 2)
                    act.activation(yf[:, m, :], k.PS[:, m, :], ACT.Identity, scale=k.modc[:, 0, GA, m, bass.ds(b, 1)],
                                   bias=gabo[:, m, bass.ds(b, 1)]).then_inc(yf_done, 1)
            over_batches(act, batch)

        @block.vector
        def _(dve):
            dve.wait_ge(w_split, 1)
            dve.tensor_tensor(wlo[:], wst[:], f32(whi[:]), ALU.subtract).then_inc(w_split, 1)
            dve.tensor_tensor(gabo[:], k.modc[:, 0, GA], bo[:].unsqueeze(2).to_broadcast([P, DM, B]), ALU.mult).then_inc(b_done, 1)
            def batch(b):
                for g in range(2):
                    wait(dve, yT_ready, b * 2 + g + 1)
                    x = k.X[:, bass.ds(b * TT + 2 * g, 2), :]
                    dve.tensor_tensor(x, k.PS[:, 2 + g, :].rearrange("p (t d) -> p t d", t=2), x, ALU.add).then_inc(x_done, 1)
            over_batches(dve, batch)

        @block.tensor
        def _(pe):
            pe.wait_ge(w_split, 2)
            def batch(b):
                wait(pe, yf_done, b * DM)
                for m in range(DM):
                    for q in range(QUADS):
                        last = split3(pe, k.PS[:, m, :], whi[:, q, m * P:(m + 1) * P], wlo[:, q, m * P:(m + 1) * P],
                                      OT[0][:, b * QUADS + q, :], OT[1][:, b * QUADS + q, :], q == 0, q == QUADS - 1)
                    last.then_inc(y_ready, 1)
                wait(pe, yf_done, (b + 1) * DM)
                wait(pe, x_done, b * 2)
                for g in range(2):
                    for t in (2 * g, 2 * g + 1):
                        for m in range(DM):
                            last = pe.transpose(k.PS[:, 2 + g, (t % 2) * D + m * P:(t % 2) * D + m * P + P],
                                                yf[:, m, t * P:(t + 1) * P], k.ident[:])
                    last.then_inc(yT_ready, 1)
            over_batches(pe, batch)


def route(k, layer, hT, combT, gate_w, experts, topk):
    nc = k.nc
    E = experts
    with ExitStack() as c:
        n = lambda s: f"r{layer}_{s}"
        gst = k.sb(n("gst"), [P, DM, P], F32, c)
        ghi = k.sb(n("ghi"), [P, DM, P], F32R, c)
        glo = k.sb(n("glo"), [P, DM, P], F32R, c)
        stats = k.sb(n("stats"), [P, TT + 1, 6], F32, c)
        mv = k.sb(n("mv"), [P, TT, 2], F32, c)
        var, rs = k.sb(n("var"), [P, TT], F32, c), k.sb(n("rs"), [P, TT], F32, c)
        xh = k.sb(n("xh"), [P, TT, D], F32, c)
        hf = k.sb(n("hf"), [P, DM, T], F32, c)
        lg = k.sb(n("lg"), [P, T], F32, c)
        mx, sm = k.sb(n("mx"), [P, TT], F32, c), k.sb(n("sm"), [P, TT], F32, c)
        ex = k.sb(n("ex"), [P, TT, E], F32, c)
        CAND = max(E + 8 - topk, 8)
        cand = k.sb(n("cand"), [P, TT, CAND], F32, c)
        rep = k.sb(n("rep"), [P, TT, CAND], F32, c)
        top = k.sb(n("top"), [P, TT, 8], F32, c)
        comb = k.sb(n("comb"), [P, TT, GROW], F32, c)
        cf = k.sb(n("cf"), [GROW, T], F32, c)
        S = lambda s: k.sem(n(s))
        g_in, g_split, own_dve, zeroed = S("g_in"), S("g_split"), S("dve"), S("zeroed")
        var_ready, root_done, xh_ready, xT_ready = S("var_ready"), S("root_done"), S("xh_ready"), S("xT_ready")
        hf_done, hi_done, lo_done = S("hf_done"), S("hi_done"), S("lo_done")
        lT_ready, lg_done, l_ready = S("lT_ready"), S("lg_done"), S("l_ready")
        d_ready, ex_done, comb_done, cT_ready, cf_done, chi_done, clo_done = (
            S("d_ready"), S("ex_done"), S("comb_done"), S("cT_ready"), S("cf_done"), S("chi_done"), S("clo_done"))
        block = c.enter_context(nc.Block())

        @block.sync
        def _(sp):
            sp.dma_start(gst[:], gate_w).then_inc(g_in, 16)
            sp.wait_ge(g_in, 16)

        @block.gpsimd
        def _(pool):
            pool.memset(f32(combT[:]), 0.0).then_inc(zeroed, 1)
            pool.memset(cand[:], 2.0).then_inc(zeroed, 1)
            pool.memset(comb[:], 0.0).then_inc(zeroed, 1)
            pool.wait_ge(zeroed, 3)
            pool.memset(comb[:, :, ONE:ONE + 1], 1.0).then_inc(zeroed, 1)
            def batch(b):
                wait(pool, var_ready, b + 1)
                pool.tensor_tensor(rs[:], var[:], k.mhalf[:, 0:TT], ALU.pow).then_inc(root_done, 1)
            over_batches(pool, batch)

        @block.scalar
        def _(act):
            act.wait_ge(g_in, 16)
            act.activation(ghi[:], gst[:], ACT.Copy).then_inc(g_split, 1)
            act.wait_ge(zeroed, 4)
            def batch(b):
                wait(act, lo_done, b * DM)
                for m in range(DM):
                    wait(act, xT_ready, b * DM + m + 1)
                    act.activation(hf[:, m, :], k.PS[:, m, :], ACT.Identity, scale=k.modc[:, layer, CB, m, bass.ds(b, 1)],
                                   bias=k.modc[:, layer, SB, m, bass.ds(b, 1)]).then_inc(hf_done, 1)
                for m in range(DM):
                    wait(act, hf_done, b * DM + m + 1)
                    act.activation(hT[0][:, m, bass.ds(b * T, T)], hf[:, m, :], ACT.Copy).then_inc(hi_done, 1)
                wait(act, lT_ready, b + 1)
                act.activation(lg[:], k.PS[:, 2, :], ACT.Copy).then_inc(lg_done, 1)
                wait(act, d_ready, b + 1)
                act.activation(ex[:], ex[:], ACT.Exp).then_inc(ex_done, 1)
                wait(act, cT_ready, b + 1)
                wait(act, clo_done, b)
                act.activation(cf[:], k.PS[0:GROW, 4, :], ACT.Copy).then_inc(cf_done, 1)
                wait(act, cf_done, b + 1)
                act.activation(combT[0:GROW, bass.ds(b * T, T)], cf[:], ACT.Copy).then_inc(chi_done, 1)
            over_batches(act, batch)

        @block.vector
        def _(dve):
            dve.wait_ge(g_split, 1)
            dve.tensor_tensor(glo[:], gst[:], f32(ghi[:]), ALU.subtract).then_inc(g_split, 1)
            dve.wait_ge(zeroed, 4)
            per = STATS_OPS + 4 + ((TT + 1) + 1 + TT if topk > 1 else 2)
            def batch(b):
                own = Chain(dve, own_dve, b * per)
                row_stats(own, dve, lambda t: k.X[:, b * TT + t, :], stats, mv)
                dve.tensor_scalar(var[:], mv[:, :, 1], EPS, None, ALU.add).then_inc(var_ready, 1)
                wait(dve, root_done, b + 1)
                wait(dve, xT_ready, b * DM)
                for t in range(TT):
                    dve.tensor_scalar(xh[:, t, :], k.X[:, b * TT + t, :], mv[:, t, 0:1], rs[:, t:t + 1],
                                      ALU.subtract, ALU.mult).then_inc(xh_ready, 1)
                for m in range(DM):
                    wait(dve, hi_done, b * DM + m + 1)
                    hi = f32(hT[0][:, m, bass.ds(b * T, T)])
                    dve.tensor_tensor(hT[1][:, m, bass.ds(b * T, T)], hf[:, m, :], hi, ALU.subtract).then_inc(lo_done, 1)
                logits = k.PS[:, 3, :].rearrange("p (t e) -> p t e", e=P)[:, :, 0:E]
                wait(dve, l_ready, b + 1)
                own.link(dve.tensor_reduce(mx[:], logits, AX_X, ALU.max))
                own.wait()
                dve.tensor_tensor(ex[:], logits, mx[:].unsqueeze(2).to_broadcast([P, TT, E]), ALU.subtract).then_inc(d_ready, 1)
                wait(dve, ex_done, b + 1)
                own.link(dve.tensor_reduce(sm[:], ex[:], AX_X, ALU.add))
                own.wait()
                own.link(dve.reciprocal(sm[:], sm[:]))
                own.wait()
                wait(dve, cT_ready, b)
                pr = cand[:, :, 0:E]
                own.link(dve.tensor_tensor(pr, ex[:], sm[:].unsqueeze(2).to_broadcast([P, TT, E]), ALU.mult))
                own.wait()
                if topk > 1:
                    own.link(dve.tensor_copy(mx[:, 0:1], sm[:, 0:1]))
                    for t in range(TT):
                        own.link(dve.max(top[:, t, :], cand[:, t, 0:E]))
                    own.wait()
                    own.link(dve.memset(top[:, :, topk:8], 2.0))
                    own.wait()
                    dve.tensor_copy(mx[:, 1:2], sm[:, 1:2])
                    for t in range(TT):
                        own.link(dve.match_replace(out=rep[:, t, :], in_to_replace=top[:, t, :], in_values=cand[:, t, :],
                                                   imm_value=-1.0))
                    own.wait()
                    dve.scalar_tensor_tensor(out=comb[:, :, 0:E], in0=rep[:, :, 0:E], scalar=0.0, in1=pr,
                                             op0=ALU.is_lt, op1=ALU.mult).then_inc(comb_done, 1)
                else:
                    own.link(dve.tensor_tensor(rep[:, :, 0], cand[:, :, 0], cand[:, :, 1], ALU.is_ge))
                    own.link(dve.tensor_tensor(rep[:, :, 1], cand[:, :, 1], cand[:, :, 0], ALU.is_gt))
                    own.wait()
                    dve.tensor_tensor(comb[:, :, 0:E], rep[:, :, 0:E], pr, ALU.mult).then_inc(comb_done, 1)
                wait(dve, chi_done, b + 1)
                dve.tensor_tensor(combT[GROW:2 * GROW, bass.ds(b * T, T)], cf[:], f32(combT[0:GROW, bass.ds(b * T, T)]),
                                  ALU.subtract).then_inc(clo_done, 1)
            over_batches(dve, batch)

        @block.tensor
        def _(pe):
            pe.wait_ge(g_split, 2)
            def batch(b):
                for m in range(DM):
                    wait(pe, hf_done, b * DM)
                    for t in range(TT):
                        wait(pe, xh_ready, b * TT + t + 1)
                        last = pe.transpose(k.PS[:, m, t * P:(t + 1) * P], xh[:, t, m * P:(m + 1) * P], k.ident[:])
                    last.then_inc(xT_ready, 1)
                wait(pe, lo_done, (b + 1) * DM)
                wait(pe, lg_done, b)
                for d in range(DM):
                    last = split3(pe, k.PS[:, 2, :], ghi[:, d, :], glo[:, d, :], hT[0][:, d, bass.ds(b * T, T)],
                                  hT[1][:, d, bass.ds(b * T, T)], d == 0, d == DM - 1)
                last.then_inc(lT_ready, 1)
                wait(pe, lg_done, b + 1)
                wait(pe, d_ready, b)
                for t in range(TT):
                    last = pe.transpose(k.PS[:, 3, t * P:(t + 1) * P], lg[:, t * P:(t + 1) * P], k.ident[:])
                last.then_inc(l_ready, 1)
                wait(pe, comb_done, b + 1)
                wait(pe, cf_done, b)
                for t in range(TT):
                    last = pe.transpose(k.PS[0:GROW, 4, t * P:(t + 1) * P], comb[:, t, :], k.ident[:])
                last.then_inc(cT_ready, 1)
            over_batches(pe, batch)


W13 = 2 * DM * P
WC = W13 + P
WALL = WC + D


def experts(k, layer, hT, combT, w, tiles, out):
    nc = k.nc
    HALVES, C = 2, B // 2
    with ExitStack() as c:
        nm = lambda s: f"e{layer}_{s}"
        wst = k.sb(nm("wst"), [P, 2, WALL], F32, c)
        whi = k.sb(nm("whi"), [P, 2, WALL], F32R, c)
        wlo = k.sb(nm("wlo"), [P, 2, WALL], F32R, c)
        sg = k.sb(nm("sg"), [P, 2, T], F32, c)
        cb = k.sb(nm("cb"), [P, 2, T], F32, c)
        um = k.sb(nm("um"), [P, 2, T], F32, c)
        hf = k.sb(nm("hf"), [P, 2, T], F32, c)
        hhi = k.sb(nm("hhi"), [P, 4, T], F32R, c)
        hlo = k.sb(nm("hlo"), [P, 4, T], F32R, c)
        yf = k.sb(nm("yf"), [P, C, DM, T], F32, c)
        S = lambda s: k.sem(nm(s))
        w_in = [S(f"w_in{i}") for i in range(2)]
        w_split, w13_done, w2_done = S("w_split"), S("w13_done"), S("w2_done")
        g_ready, u_ready, c_ready, y_done = S("g_ready"), S("u_ready"), S("c_ready"), S("y_done")
        silu_done, cb_done, um_done, h_done, hi_done, lo_done = (
            S("silu_done"), S("cb_done"), S("um_done"), S("h_done"), S("hi_done"), S("lo_done"))
        yf_done, yT_ready, x_done, x_out = S("yf_done"), S("yT_ready"), S("x_done"), S("x_out")
        block = c.enter_context(nc.Block())
        PEEL = 2 + tiles % 2

        def each_tile(eng, half, body):
            base = half * tiles
            for t in range(PEEL):
                body(t, base + t, (base + t) % 2)
            with eng.Fori(0, (tiles - PEEL) // 2) as pair:
                for j in range(2):
                    t = pair * 2 + (PEEL + j)
                    body(t, base + t, (base + PEEL + j) % 2)

        @block.sync
        def _(sp):
            def load(t, g, par):
                wait(sp, w2_done, g - 1)
                sp.dma_start(wst[:, par, :], w[t]).then_inc(w_in[par], 16)
            for half in range(HALVES):
                each_tile(sp, half, load)
            if out is not None:
                for half in range(HALVES):
                    sp.wait_ge(x_done, 4 * (half + 1))
                    sp.dma_start(out.rearrange("(t p) d -> p t d", p=P)[:, half * 8:half * 8 + 8],
                                 k.X[:, half * 8:half * 8 + 8, :]).then_inc(x_out, 16)
                sp.wait_ge(x_out, 32)

        @block.gpsimd
        def _(pool):
            def split(t, g, par):
                count = (g - par) * 8 + 16 if isinstance(g, int) else (g - par) * 8 + 16
                for lo, hi, free, done in ((0, WC, c_ready, w13_done), (WC, WALL, y_done, w2_done)):
                    if lo == 0:
                        pool.wait_ge(w_in[par], count)
                    wait(pool, free, 2 * g - 2)
                    pool.tensor_tensor(wlo[:, par, W13:W13 + 1], wst[:, par, 0:1], wst[:, par, 1:2], ALU.mult).then_inc(w_split, 1)
                    pool.tensor_scalar(whi[:, par, lo:hi], wst[:, par, lo:hi], 1.0, 1.0, ALU.mult, ALU.mult).then_inc(w_split, 1)
                    pool.wait_ge(w_split, g * 4 + (2 if lo == 0 else 4))
                    end = min(hi, W13) if lo == 0 else hi
                    pool.tensor_tensor(wlo[:, par, lo:end], wst[:, par, lo:end], f32(whi[:, par, lo:end]), ALU.subtract).then_inc(done, 1)
            for half in range(HALVES):
                each_tile(pool, half, split)

        @block.scalar
        def _(act):
            def split_h(n, s):
                wait(act, h_done, n + 1)
                wait(act, y_done, n - 3)
                act.activation(hhi[:, s % 4, :], hf[:, s % 2, :], ACT.Copy).then_inc(hi_done, 1)

            def steps(t, g, par):
                for j in range(C):
                    n, s = 2 * g + j, 2 * par + j
                    if not (isinstance(t, int) and t == 0 and j == 0):
                        split_h(n - 1, s - 1)
                    wait(act, g_ready, n + 1)
                    wait(act, h_done, n - 1)
                    act.activation(sg[:, s % 2, :], k.PS[:, 3 * s % 4, :], ACT.Silu).then_inc(silu_done, 1)
                    wait(act, c_ready, n + 1)
                    wait(act, um_done, n - 1)
                    act.activation(cb[:, s % 2, :], k.PS[:, (3 * s + 2) % 4, :], ACT.Copy).then_inc(cb_done, 1)
            for half in range(HALVES):
                each_tile(act, half, steps)
                N = C * tiles * (half + 1)
                split_h(N - 1, N - 1)
                act.wait_ge(y_done, N)
                for j in range(C):
                    for m in range(DM):
                        if half:
                            act.wait_ge(yT_ready, 4 * half)
                        act.activation(yf[:, j, m, :], k.PS[:, 4 + 2 * j + m, :], ACT.Copy,
                                       scale=k.modc[:, layer, GB, m, C * half + j:C * half + j + 1]).then_inc(yf_done, 1)

        @block.vector
        def _(dve):
            def split_h(n, s):
                wait(dve, hi_done, n + 1)
                wait(dve, y_done, n - 3)
                dve.tensor_tensor(hlo[:, s % 4, :], hf[:, s % 2, :], f32(hhi[:, s % 4, :]), ALU.subtract).then_inc(lo_done, 1)

            def steps(t, g, par):
                for j in range(C):
                    n, s = 2 * g + j, 2 * par + j
                    if not (isinstance(t, int) and t == 0 and j == 0):
                        split_h(n - 1, s - 1)
                    wait(dve, u_ready, n + 1)
                    wait(dve, cb_done, n + 1)
                    dve.tensor_tensor(um[:, s % 2, :], k.PS[:, (3 * s + 1) % 4, :], cb[:, s % 2, :], ALU.mult).then_inc(um_done, 1)
                    wait(dve, um_done, n + 1)
                    wait(dve, silu_done, n + 1)
                    wait(dve, lo_done, n - 1)
                    dve.tensor_tensor(hf[:, s % 2, :], um[:, s % 2, :], sg[:, s % 2, :], ALU.mult).then_inc(h_done, 1)
            for half in range(HALVES):
                each_tile(dve, half, steps)
                N = C * tiles * (half + 1)
                split_h(N - 1, N - 1)
                for i in range(2 * C):
                    dve.wait_ge(yT_ready, 4 * half + i + 1)
                    x = k.X[:, 8 * half + 2 * i:8 * half + 2 * i + 2, :]
                    dve.tensor_tensor(x, k.PS[:, i, :].rearrange("p (t d) -> p t d", t=2), x, ALU.add).then_inc(x_done, 1)

        @block.tensor
        def _(pe):
            for half in range(HALVES):
                def steps(t, g, par):
                    start = isinstance(t, int) and t == 0
                    for j in range(C):
                        n, s = 2 * g + j, 2 * par + j
                        chunk = slice((C * half + j) * T, (C * half + j + 1) * T)
                        if start and j == 0 and half:
                            pe.wait_ge(x_done, 4 * half)
                        if j == 0:
                            wait(pe, w13_done, g + 1)
                        for i, (done, lag) in enumerate(((cb_done, 1), (silu_done, 0))):
                            wait(pe, done, n - lag)
                            for d in range(DM):
                                at = (i * DM + d) * P
                                ins = split3(pe, k.PS[:, (3 * s + i) % 4, :], whi[:, par, at:at + P], wlo[:, par, at:at + P],
                                             hT[0][:, d, chunk], hT[1][:, d, chunk], d == 0, d == DM - 1)
                            ins.then_inc((g_ready, u_ready)[i], 1)
                        wait(pe, um_done, n)
                        pe.matmul(k.PS[:, (3 * s + 2) % 4, :], whi[:, par, W13:WC], combT[:, chunk], start=True, stop=True).then_inc(c_ready, 1)
                        if not start:
                            into_y2(t - 1, g - 1, 1 - par, j)

                def into_y2(t, g, par, j, last=False):
                    n, s = 2 * g + j, 2 * par + j
                    wait(pe, lo_done, n + 1)
                    first = isinstance(t, int) and t == 0
                    if j == 0:
                        wait(pe, w2_done, g + 1)
                    if first and half:
                        pe.wait_ge(yf_done, 4 * half)
                    for m in range(DM):
                        ins = split3(pe, k.PS[:, 4 + 2 * j + m, :], whi[:, par, WC + m * P:WC + (m + 1) * P],
                                     wlo[:, par, WC + m * P:WC + (m + 1) * P], hhi[:, s % 4, :], hlo[:, s % 4, :], first, last)
                    ins.then_inc(y_done, 1)
                each_tile(pe, half, steps)
                g = (half + 1) * tiles - 1
                for j in range(C):
                    into_y2(tiles - 1, g, g % 2, j, True)
                N = C * tiles * (half + 1)
                pe.wait_ge(cb_done, N)
                pe.wait_ge(um_done, N)
                pe.wait_ge(silu_done, N)
                for j in range(C):
                    pe.wait_ge(yf_done, 4 * half + 2 * j + 2)
                    for i in range(2):
                        for t in (2 * i, 2 * i + 1):
                            for m in range(DM):
                                ins = pe.transpose(k.PS[:, 2 * j + i, (t % 2) * D + m * P:(t % 2) * D + m * P + P],
                                                   yf[:, j, m, t * P:(t + 1) * P], k.ident[:])
                        ins.then_inc(yT_ready, 1)


def gated_conv(k, H, hT, w_in_d, w_out_d, taps_d):
    nc = k.nc
    with ExitStack() as c:
        n = lambda s: f"c_{s}"
        wi_st = k.sb(n("wi_st"), [P, DM, 2 * INNER], F32, c)
        wi_hi = k.sb(n("wi_hi"), [P, DM, 2 * INNER], F32R, c)
        wi_lo = k.sb(n("wi_lo"), [P, DM, 2 * INNER], F32R, c)
        wo_st = k.sb(n("wo_st"), [P, IT, D], F32, c)
        wo_hi = k.sb(n("wo_hi"), [P, IT, D], F32R, c)
        wo_lo = k.sb(n("wo_lo"), [P, IT, D], F32R, c)
        tap = k.sb(n("tap"), [P, IT, TAPS + 1], F32, c)
        stats = k.sb(n("stats"), [P, TT + 1, 6], F32, c)
        mv = k.sb(n("mv"), [P, TT, 2], F32, c)
        var, rs = k.sb(n("var"), [P, TT], F32, c), k.sb(n("rs"), [P, TT], F32, c)
        ss, sq = k.sb(n("ss"), [P, TT], F32, c), k.sb(n("sq"), [P, TT, D], F32, c)
        hn = k.sb(n("hn"), [P, TT, D], F32, c)
        hb = k.sb(n("hb"), [P, TT, D], F32, c)
        rhi, rlo = k.sb(n("rhi"), [P, DM, T], F32R, c), k.sb(n("rlo"), [P, DM, T], F32R, c)
        acc = k.sb(n("acc"), [P, 2, T], F32, c)
        sx, sz = k.sb(n("sx"), [P, 2, T], F32, c), k.sb(n("sz"), [P, 2, T], F32, c)
        yv = k.sb(n("yv"), [P, 2, T], F32, c)
        yhi, ylo = k.sb(n("yhi"), [P, 2, T], F32R, c), k.sb(n("ylo"), [P, 2, T], F32R, c)
        yf = k.sb(n("yf"), [P, DM, T], F32, c)
        S = lambda s: k.sem(n(s))
        w_in, w_split, own_dve = S("w_in"), S("w_split"), S("dve")
        var_ready, root_done, h_ready, ss_done = S("var_ready"), S("root_done"), S("h_ready"), S("ss_done")
        hn_ready, rT_ready, rhi_done, rlo_done = S("hn_ready"), S("rT_ready"), S("rhi_done"), S("rlo_done")
        p_ready, z_ready, conv_done, sx_done, sz_done = S("p_ready"), S("z_ready"), S("conv_done"), S("sx_done"), S("sz_done")
        yv_done, yhi_done, ylo_done, o_done = S("yv_done"), S("yhi_done"), S("ylo_done"), S("o_done")
        yf_done, yT_ready, h_out = S("yf_done"), S("yT_ready"), S("h_out")
        block = c.enter_context(nc.Block())

        @block.sync
        def _(sp):
            sp.dma_start(wi_st[:], w_in_d.rearrange("(m p) n -> p m n", p=P)).then_inc(w_in, 16)
            sp.dma_start(wo_st[:], w_out_d.rearrange("(e p) n -> p e n", p=P)).then_inc(w_in, 16)
            sp.dma_start(tap[:], taps_d).then_inc(w_in, 16)
            def batch(b):
                wait(sp, h_ready, b * 8 + 8)
                sp.dma_start(H[:, bass.ds(b * TT, TT), :], hb[:]).then_inc(h_out, 16)
            over_batches(sp, batch)
            sp.wait_ge(h_out, B * 16)

        @block.gpsimd
        def _(pool):
            def batch(b):
                for i in range(2):
                    wait(pool, var_ready, b * 3 + i + 1)
                    pool.tensor_tensor(rs[:], var[:], k.mhalf[:, 0:TT], ALU.pow).then_inc(root_done, 1)
                for e in range(IT):
                    wait(pool, sx_done, b * IT + e + 1)
                    wait(pool, sz_done, b * IT + e + 1)
                    if e < 2:
                        wait(pool, ylo_done, b * IT)
                    else:
                        wait(pool, ylo_done, b * IT + e - 1)
                    pool.tensor_tensor(yv[:, e % 2, :], sx[:, e % 2, :], sz[:, e % 2, :], ALU.mult).then_inc(yv_done, 1)
                wait(pool, var_ready, b * 3 + 3)
                pool.tensor_tensor(rs[:], var[:], k.mhalf[:, 0:TT], ALU.pow).then_inc(root_done, 1)
            over_batches(pool, batch)

        @block.scalar
        def _(act):
            act.wait_ge(w_in, 48)
            act.activation(wi_hi[:], wi_st[:], ACT.Copy).then_inc(w_split, 1)
            act.activation(wo_hi[:], wo_st[:], ACT.Copy).then_inc(w_split, 1)
            def batch(b):
                def squares(i):
                    for t in range(TT):
                        wait(act, h_ready, b * 8 + i * TT + t + 1)
                        wait(act, ss_done, b * 8 + i * TT)
                        act.activation(sq[:, t, :], hb[:, t, :], ACT.Square, accum_out=ss[:, t:t + 1]).then_inc(ss_done, 1)
                squares(0)
                for m in range(DM):
                    wait(act, rT_ready, b * 4 + m + 1)
                    wait(act, z_ready, b * IT)
                    act.activation(rhi[:, m, :], k.PS[:, m, :], ACT.Copy).then_inc(rhi_done, 1)

                def split_y(e):
                    wait(act, yv_done, b * IT + e + 1)
                    if e < 2:
                        wait(act, o_done, b * IT)
                    else:
                        wait(act, o_done, b * IT + e - 1)
                    act.activation(yhi[:, e % 2, :], yv[:, e % 2, :], ACT.Copy).then_inc(yhi_done, 1)
                for e in range(IT):
                    wait(act, z_ready, b * IT + e + 1)
                    wait(act, yv_done, b * IT + max(e - 1, 0))
                    act.activation(sz[:, e % 2, :], k.PS[:, 3 + 2 * (e % 2), :], ACT.Silu).then_inc(sz_done, 1)
                    wait(act, conv_done, b * IT + e + 1)
                    act.activation(sx[:, e % 2, :], acc[:, e % 2, :], ACT.Silu).then_inc(sx_done, 1)
                    if e:
                        split_y(e - 1)
                split_y(IT - 1)
                wait(act, o_done, (b + 1) * IT)
                for m in range(DM):
                    wait(act, yT_ready, b * 2)
                    act.activation(yf[:, m, :], k.PS[:, 6 + m, :], ACT.Copy).then_inc(yf_done, 1)
                squares(1)
                for m in range(DM):
                    wait(act, rT_ready, b * 4 + 2 + m + 1)
                    act.activation(hT[0][:, m, bass.ds(b * T, T)], k.PS[:, m, :], ACT.Copy).then_inc(rhi_done, 1)
            over_batches(act, batch)

        @block.vector
        def _(dve):
            dve.wait_ge(w_split, 2)
            dve.tensor_tensor(wi_lo[:], wi_st[:], f32(wi_hi[:]), ALU.subtract).then_inc(w_split, 1)
            dve.tensor_tensor(wo_lo[:], wo_st[:], f32(wo_hi[:]), ALU.subtract).then_inc(w_split, 1)
            per = STATS_OPS + TT + 1 + 4 * IT - IT
            def batch(b):
                own = Chain(dve, own_dve, b * per)

                def rms(i):
                    wait(dve, ss_done, b * 8 + (i + 1) * TT)
                    dve.tensor_scalar(var[:], ss[:], 1e-24, 1.0 / D, ALU.max, ALU.mult).then_inc(var_ready, 1)
                    wait(dve, root_done, b * 3 + i + 2)
                    wait(dve, rT_ready, b * 4 + 2 * i)
                    for t in range(TT):
                        dve.tensor_scalar(hn[:, t, :], hb[:, t, :], rs[:, t:t + 1], None, ALU.mult).then_inc(hn_ready, 1)

                row_stats(own, dve, lambda t: k.X[:, b * TT + t, :], stats, mv)
                dve.tensor_scalar(var[:], mv[:, :, 1], EPS, None, ALU.add).then_inc(var_ready, 1)
                wait(dve, root_done, b * 3 + 1)
                wait(dve, h_out, b * 16)
                for t in range(TT):
                    own.link(dve.tensor_scalar(hb[:, t, :], k.X[:, b * TT + t, :], mv[:, t, 0:1], rs[:, t:t + 1],
                                               ALU.subtract, ALU.mult))
                own.wait()
                row = lambda part: k.rows[:, 1, part, b, :].unsqueeze(1).to_broadcast([P, TT, D])
                h = hb[:]
                own.link(dve.tensor_tensor(h, h, row(CA), ALU.mult))
                own.wait()
                dve.tensor_tensor(h, h, row(SA), ALU.add).then_inc(h_ready, 4)
                wait(dve, h_ready, b * 8 + 4)
                rms(0)
                for m in range(DM):
                    wait(dve, rhi_done, b * 4 + m + 1)
                    dve.tensor_tensor(rlo[:, m, :], k.PS[:, m, :], f32(rhi[:, m, :]), ALU.subtract).then_inc(rlo_done, 1)

                def split_y(e):
                    wait(dve, yhi_done, b * IT + e + 1)
                    dve.tensor_tensor(ylo[:, e % 2, :], yv[:, e % 2, :], f32(yhi[:, e % 2, :]), ALU.subtract).then_inc(ylo_done, 1)
                for e in range(IT):
                    p, a = k.PS[:, 2 + 2 * (e % 2), :], acc[:, e % 2, :]
                    wait(dve, p_ready, b * IT + e + 1)
                    wait(dve, sx_done, b * IT + max(e - 1, 0))
                    own.link(dve.tensor_scalar(a, p, tap[:, e, TAPS - 1:TAPS], tap[:, e, TAPS:TAPS + 1], ALU.mult, ALU.add))
                    for i in range(1, TAPS):
                        own.wait()
                        ins = dve.scalar_tensor_tensor(out=a[:, i:T], in0=p[:, 0:T - i], scalar=tap[:, e, TAPS - 1 - i:TAPS - i],
                                                       in1=a[:, i:T], op0=ALU.mult, op1=ALU.add)
                        if i < TAPS - 1:
                            own.link(ins)
                    ins.then_inc(conv_done, 1)
                    if e:
                        split_y(e - 1)
                split_y(IT - 1)
                for g in range(2):
                    wait(dve, yT_ready, b * 2 + g + 1)
                    x = hb[:, 2 * g:2 * g + 2, :]
                    dve.tensor_tensor(x, k.PS[:, g, :].rearrange("p (t d) -> p t d", t=2), x, ALU.add).then_inc(h_ready, 2)
                wait(dve, h_ready, b * 8 + 8)
                rms(1)
                for m in range(DM):
                    wait(dve, rhi_done, b * 4 + 2 + m + 1)
                    dve.tensor_tensor(hT[1][:, m, bass.ds(b * T, T)], k.PS[:, m, :], f32(hT[0][:, m, bass.ds(b * T, T)]),
                                      ALU.subtract).then_inc(rlo_done, 1)
            over_batches(dve, batch)

        @block.tensor
        def _(pe):
            pe.wait_ge(w_split, 4)
            def batch(b):
                def transposes(i):
                    for m in range(DM):
                        wait(pe, rlo_done, b * 4 + 2 * i)
                        if i:
                            wait(pe, h_ready, b * 8 + 8)
                        for t in range(TT):
                            wait(pe, hn_ready, b * 8 + i * TT + t + 1)
                            last = pe.transpose(k.PS[:, m, t * P:(t + 1) * P], hn[:, t, m * P:(m + 1) * P], k.ident[:])
                        last.then_inc(rT_ready, 1)
                transposes(0)
                wait(pe, rlo_done, b * 4 + 2)

                def up(e):
                    for i, (free, done) in enumerate(((conv_done, p_ready), (sz_done, z_ready))):
                        wait(pe, free, b * IT + max(e - 1, 0))
                        for d in range(DM):
                            at = i * INNER + e * P
                            last = split3(pe, k.PS[:, 2 + 2 * (e % 2) + i, :], wi_hi[:, d, at:at + P], wi_lo[:, d, at:at + P],
                                          rhi[:, d, :], rlo[:, d, :], d == 0, d == DM - 1)
                        last.then_inc(done, 1)

                def down(e):
                    if e == 0:
                        wait(pe, yf_done, b * DM)
                    wait(pe, ylo_done, b * IT + e + 1)
                    for m in range(DM):
                        last = split3(pe, k.PS[:, 6 + m, :], wo_hi[:, e, m * P:(m + 1) * P], wo_lo[:, e, m * P:(m + 1) * P],
                                      yhi[:, e % 2, :], ylo[:, e % 2, :], e == 0, e == IT - 1)
                    last.then_inc(o_done, 1)
                for e in range(IT):
                    up(e)
                    if e:
                        down(e - 1)
                down(IT - 1)
                wait(pe, yf_done, (b + 1) * DM)
                for g in range(2):
                    for t in (2 * g, 2 * g + 1):
                        for m in range(DM):
                            last = pe.transpose(k.PS[:, g, (t % 2) * D + m * P:(t % 2) * D + m * P + P],
                                                yf[:, m, t * P:(t + 1) * P], k.ident[:])
                    last.then_inc(yT_ready, 1)
                transposes(1)
            over_batches(pe, batch)


def mlp(k, H, hT, w_d):
    nc = k.nc
    WM = DM * P
    with ExitStack() as c:
        n = lambda s: f"m_{s}"
        wst = k.sb(n("wst"), [P, 2, WM + D], F32, c)
        whi = k.sb(n("whi"), [P, MLP_T, WM + D], F32R, c)
        wlo = k.sb(n("wlo"), [P, MLP_T, WM + D], F32R, c)
        hi, lo = k.sb(n("hi"), [P, 4, T], F32R, c), k.sb(n("lo"), [P, 4, T], F32R, c)
        yf = k.sb(n("yf"), [P, DM, T], F32, c)
        S = lambda s: k.sem(n(s))
        w_in = [S(f"w_in{i}") for i in range(2)]
        whi_done, wlo_done = S("whi_done"), S("wlo_done")
        u_ready, hi_done, lo_done, o_done = S("u_ready"), S("hi_done"), S("lo_done"), S("o_done")
        yf_done, yT_ready, h_done, x_done, own_dve = S("yf_done"), S("yT_ready"), S("h_done"), S("x_done"), S("dve")
        block = c.enter_context(nc.Block())

        @block.sync
        def _(sp):
            for i in range(MLP_T):
                if i >= 2:
                    sp.wait_ge(wlo_done, i - 1)
                sp.dma_start(wst[:, i % 2, :], w_d[i]).then_inc(w_in[i % 2], 16)

        @block.gpsimd
        def _(pool):
            for i in range(MLP_T):
                pool.wait_ge(w_in[i % 2], 16 * (i // 2 + 1))
                pool.tensor_scalar(whi[:, i, :], wst[:, i % 2, :], 1.0, 1.0, ALU.mult, ALU.mult).then_inc(whi_done, 1)
                pool.wait_ge(whi_done, i + 1)
                pool.tensor_tensor(wlo[:, i, :], wst[:, i % 2, :], f32(whi[:, i, :]), ALU.subtract).then_inc(wlo_done, 1)

        @block.scalar
        def _(act):
            def batch(b):
                for i in range(MLP_T):
                    wait(act, u_ready, b * MLP_T + i + 1)
                    wait(act, o_done, b * MLP_T + max(i - 3, 0))
                    act.activation(hi[:, i % 4, :], k.PS[:, i % 4, :], ACT.Relu).then_inc(hi_done, 1)
                wait(act, o_done, (b + 1) * MLP_T)
                for m in range(DM):
                    wait(act, yT_ready, b * 2)
                    act.activation(yf[:, m, :], k.PS[:, 4 + m, :], ACT.Copy).then_inc(yf_done, 1)
            over_batches(act, batch)

        @block.vector
        def _(dve):
            def batch(b):
                own = Chain(dve, own_dve, b * 2)
                for i in range(MLP_T):
                    wait(dve, hi_done, b * MLP_T + i + 1)
                    wait(dve, o_done, b * MLP_T + max(i - 3, 0))
                    dve.scalar_tensor_tensor(out=lo[:, i % 4, :], in0=k.PS[:, i % 4, :], scalar=0.0, in1=f32(hi[:, i % 4, :]),
                                             op0=ALU.max, op1=ALU.subtract).then_inc(lo_done, 1)
                h = H[:, bass.ds(b * TT, TT), :]
                for g in range(2):
                    wait(dve, yT_ready, b * 2 + g + 1)
                    hg = H[:, bass.ds(b * TT + 2 * g, 2), :]
                    dve.tensor_tensor(hg, k.PS[:, 6 + g, :].rearrange("p (t d) -> p t d", t=2), hg, ALU.add).then_inc(h_done, 1)
                wait(dve, h_done, b * 2 + 2)
                own.link(dve.tensor_tensor(h, h, k.rows[:, 1, GA, b, :].unsqueeze(1).to_broadcast([P, TT, D]), ALU.mult))
                own.wait()
                x = k.X[:, bass.ds(b * TT, TT), :]
                own.link(dve.tensor_tensor(x, x, h, ALU.add))
            over_batches(dve, batch)

        @block.tensor
        def _(pe):
            pe.wait_ge(wlo_done, MLP_T)
            def batch(b):
                def up(i):
                    wait(pe, lo_done, b * MLP_T + max(i - 3, 0))
                    for d in range(DM):
                        last = split3(pe, k.PS[:, i % 4, :], whi[:, i, d * P:(d + 1) * P], wlo[:, i, d * P:(d + 1) * P],
                                      hT[0][:, d, bass.ds(b * T, T)], hT[1][:, d, bass.ds(b * T, T)], d == 0, d == DM - 1)
                    last.then_inc(u_ready, 1)

                def down(i):
                    if i == 0:
                        wait(pe, yf_done, b * DM)
                    wait(pe, lo_done, b * MLP_T + i + 1)
                    for m in range(DM):
                        last = split3(pe, k.PS[:, 4 + m, :], whi[:, i, WM + m * P:WM + (m + 1) * P], wlo[:, i, WM + m * P:WM + (m + 1) * P],
                                      hi[:, i % 4, :], lo[:, i % 4, :], i == 0, i == MLP_T - 1)
                    last.then_inc(o_done, 1)
                for i in range(MLP_T):
                    up(i)
                    if i >= 2:
                        down(i - 2)
                down(MLP_T - 2)
                down(MLP_T - 1)
                wait(pe, yf_done, (b + 1) * DM)
                wait(pe, h_done, b * 2)
                for g in range(2):
                    for t in (2 * g, 2 * g + 1):
                        for m in range(DM):
                            last = pe.transpose(k.PS[:, 6 + g, (t % 2) * D + m * P:(t % 2) * D + m * P + P],
                                                yf[:, m, t * P:(t + 1) * P], k.ident[:])
                    last.then_inc(yT_ready, 1)
            over_batches(pe, batch)


def layout(a):
    import numpy as np

    def cols(*vs):
        return np.ascontiguousarray(np.stack([v.reshape(DM, P) for v in vs]).transpose(2, 0, 1))

    o = {"x": a["L0_attn_X"].reshape(B * T, D)}
    o["cT"] = np.ascontiguousarray(np.stack([a["L0_c"], a["L1_c"]]).reshape(2, B, DM, P).transpose(3, 0, 2, 1))
    o["wmod0"], o["wmod1"] = a["L0_wmod"], a["L1_wmod"]
    o["wqkv"] = np.stack([a["L0_attn_Wq"], a["L0_attn_Wk"], a["L0_attn_Wv"]])
    o["ln_gb"] = cols(a["L0_attn_ln_g"], a["L0_attn_ln_b"])
    o["bqk"] = cols(a["L0_attn_bq"], a["L0_attn_bk"])
    o["bv"] = a["L0_attn_bv"]
    o["wo"] = a["L0_attn_Wo"]
    o["bo"] = np.ascontiguousarray(a["L0_attn_bo"].reshape(DM, P).T)

    def gate(g):
        full = np.zeros((P, DM, P), np.float32)
        full[:, :, :g.shape[0]] = g.reshape(-1, DM, P).transpose(2, 1, 0)
        return full

    def blocks(w1, w3, w2, experts, ff, tiles):
        full = np.zeros((tiles, P, WALL), np.float32)
        up = np.zeros((2, tiles * P, D), np.float32)
        up[0, :w1.shape[0]], up[1, :w3.shape[0]] = w1, w3
        full[:, :, :W13] = up.reshape(2, tiles, P, DM, P).transpose(1, 4, 0, 3, 2).reshape(tiles, P, W13)
        row = np.minimum(np.arange(tiles * P) // ff, experts)
        row[row == experts] = ONE
        for part in (0, GROW):
            sel = np.zeros((tiles * P, P), np.float32)
            sel[np.arange(tiles * P), row + part] = 1.0
            full[:, :, W13:WC] += sel.reshape(tiles, P, P).transpose(0, 2, 1)
        down = np.zeros((tiles * P, D), np.float32)
        down[:w2.shape[1]] = w2.T
        full[:, :, WC:] = down.reshape(tiles, P, D)
        return full

    o["gate0"], o["gate1"] = gate(a["L0_ffn_Wg"]), gate(a["L1_ffn_gate_w"])
    flat = lambda v: v.reshape(-1, D)
    down = lambda v: v.transpose(1, 0, 2).reshape(D, -1)
    o["ffn0"] = blocks(np.concatenate([flat(a["L0_ffn_W1"]), a["L0_ffn_W1s"]]), np.concatenate([flat(a["L0_ffn_W3"]), a["L0_ffn_W3s"]]),
                       np.concatenate([down(a["L0_ffn_W2"]), a["L0_ffn_W2s"]], 1), L0_EXPERTS, L0_FF, L0_TILES)
    o["ffn1"] = blocks(flat(a["L1_ffn_w_gate"]), flat(a["L1_ffn_w_up"]), down(a["L1_ffn_w_down"]), L1_EXPERTS, L1_FF, L1_TILES)
    o["conv_in"] = np.ascontiguousarray(a["L1_attn_W_in"].T)
    o["conv_out"] = np.ascontiguousarray(a["L1_attn_W_out"].T)
    o["taps"] = np.ascontiguousarray(np.concatenate([a["L1_attn_conv_w"][:, 0], a["L1_attn_conv_b"][:, None]], 1)
                                     .reshape(IT, P, TAPS + 1).transpose(1, 0, 2))
    o["mlp"] = np.concatenate([a["L1_attn_W_mlp1"].reshape(MLP_T, P, DM, P).transpose(0, 3, 2, 1).reshape(MLP_T, P, D),
                               a["L1_attn_W_mlp2"].T.reshape(MLP_T, P, D)], 2)
    return o


def program(nc, a, out, upto=99):
    with ExitStack() as ctx, ExitStack() as att:
        k = Core(nc, ctx)
        setup(k, a["x"], a["cT"], a["wmod0"], a["wmod1"])
        if upto >= 1:
            attention_inputs(k, a["wqkv"], a["ln_gb"], a["bqk"], a["bv"])
        OT = [k.sb(f"OT{i}", [P, B * QUADS, T], F32R, att) for i in range(2)]
        if upto >= 2:
            attention(k, OT, None)
        if upto >= 3:
            attention_output(k, OT, a["wo"], a["bo"])
        k.recycle()
        att.close()
        hT = [k.sb(f"hT{i}", [P, DM, B * T], F32R) for i in range(2)]
        combT = k.sb("combT", [P, B * T], F32R)
        if upto >= 4:
            route(k, 0, hT, combT, a["gate0"], L0_EXPERTS, L0_TOPK)
        if upto >= 5:
            experts(k, 0, hT, combT, a["ffn0"], L0_TILES, out if upto == 5 else None)
        if upto >= 6:
            with ExitStack() as c:
                H = k.sb("H", [P, NT, D], F32, c)
                gated_conv(k, H, hT, a["conv_in"], a["conv_out"], a["taps"])
                if upto >= 7:
                    mlp(k, H, hT, a["mlp"])
        if upto >= 8:
            route(k, 1, hT, combT, a["gate1"], L1_EXPERTS, 1)
            experts(k, 1, hT, combT, a["ffn1"], L1_TILES, out)


def kernel(**inputs):
    import numpy as np
    import concourse.bacc as bacc
    from concourse.bass_utils import run_bass_kernel_spmd

    nc = bacc.Bacc("TRN2", target_bir_lowering=False, num_devices=1)
    arrays = {f"in_{n}": np.ascontiguousarray(v) for n, v in layout(inputs).items()}
    aps = {n[3:]: nc.dram_tensor(n, v.shape, mybir.dt.from_np(v.dtype), kind="ExternalInput").ap() for n, v in arrays.items()}
    out = nc.dram_tensor("out", (B * T, D), F32, kind="ExternalOutput").ap()
    program(nc, aps, out)
    got = run_bass_kernel_spmd(nc, [arrays], core_ids=[0])
    return got.results[0]["out"].reshape(B, T, D)
```

```python
from contextlib import ExitStack

import concourse.bass as bass
from concourse import mybir

F32 = mybir.dt.float32
F32R = mybir.dt.float32r
BF16 = mybir.dt.bfloat16
ALU = mybir.AluOpType
ACT = mybir.ActivationFunctionType
AX_X = mybir.AxisListType.X

P = 128
D = 256
DM = D // P
B, T = 4, 512
NT = B * T // P
TT = T // P
HEADS, DH = 16, 16
QUADS = HEADS // 4
EPS = 1e-5
L0_EXPERTS, L0_TOPK, L0_FF, L0_SHARED = 16, 4, 176, 352
L0_TILES = -(-(L0_EXPERTS * L0_FF + L0_SHARED) // P)
L1_EXPERTS, L1_FF = 2, 1024
L1_TILES = L1_EXPERTS * L1_FF // P
INNER, TAPS = 512, 4
IT = INNER // P
MLP_T = 4 * D // P
GROW = 32
ONE = 16
MASKED = -3.0e38
SA, CA, GA, SB, CB, GB = range(6)


def f32(ap):
    return ap.bitcast(F32)


def split3(pe, out, w_hi, w_lo, x_hi, x_lo, first, last):
    pe.matmul(out, w_hi, x_lo, start=first, stop=False)
    pe.matmul(out, w_lo, x_hi, start=False, stop=False)
    return pe.matmul(out, w_hi, x_hi, start=False, stop=last)


def wait(eng, sem, n):
    if not isinstance(n, int) or n > 0:
        eng.wait_ge(sem, n)


def over_batches(eng, batch):
    batch(0)
    with eng.Fori(1, B) as b:
        batch(b)


def wavefront(*stages):
    for step in range(B + max(lag for lag, _ in stages)):
        for lag, stage in stages:
            if 0 <= step - lag < B:
                stage(step - lag)


class Chain:

    def __init__(self, eng, sem, start=0):
        self.eng, self.sem, self.n = eng, sem, start

    def link(self, ins):
        ins.then_inc(self.sem, 1)
        self.n = self.n + 1
        return self.n

    def wait(self, n=None):
        self.eng.wait_ge(self.sem, self.n if n is None else n)


class Core:

    def __init__(self, nc, ctx):
        self.nc, self.ctx, self.sems = nc, ctx, []
        sb, dram = self.sb, self.dram
        self.PS = ctx.enter_context(nc.psum_tensor("PS", [P, 8, 512], F32))
        self.X = sb("X", [P, NT, D], F32)
        self.ident = sb("ident", [P, P], F32)
        self.identb = sb("identb", [P, P], BF16)
        self.mhalf = sb("mhalf", [P, TT], F32)
        self.maskb = sb("maskb", [P, P], BF16)
        self.modc = sb("modc", [P, 2, 6, DM, B], F32)
        self.rows = sb("rows", [P, 2, 3, B, D], F32)
        self.q_parts = dram("q_parts", [B, QUADS, 4, 2, DH, T])
        self.k_parts = dram("k_parts", [B, QUADS, 4, 2, DH, T])
        self.v_parts = dram("v_parts", [B, TT, P, HEADS, 2 * DH])

    def sb(self, name, shape, dt, ctx=None, side="left"):
        return (ctx or self.ctx).enter_context(self.nc.sbuf_tensor(name, shape, dt, side=side))

    def dram(self, name, shape):
        return self.nc.dram_tensor(name, shape, F32, kind="Internal").ap()

    def sem(self, name):
        sem = self.nc.alloc_semaphore(name=name)
        self.sems.append(sem)
        return sem

    def recycle(self):
        self.nc.clear_and_free_semaphores(self.sems)
        self.nc.all_engine_barrier()
        self.sems = []


def setup(k, x, cT, wmod0, wmod1):
    nc = k.nc
    with ExitStack() as c:
        cs = k.sb("cs", [P, 2, DM, B], F32, c)
        scT = k.sb("scT", [P, 2, DM, B], F32, c)
        scB = k.sb("scB", [P, 2, DM, B, P], F32, c)
        wm = k.sb("wm", [P, 2, DM, 6 * D], F32, c)
        sgn = k.sb("sgn", [P, B, D], F32, c)
        mag = k.sb("mag", [P, B, D], F32, c)
        zero = k.sb("zero", [P, P], F32, c)
        x_in, c_in, w_in = k.sem("x_in"), k.sem("c_in"), k.sem("wm_in")
        silu_done, cols_ready, rows_ready = k.sem("silu_done"), k.sem("cols_ready"), k.sem("rows_ready")
        rows_taken, pool_own, dve_own = k.sem("rows_taken"), k.sem("setup_pool"), k.sem("setup_dve")
        cols = k.PS[:, 0, 0:2 * 12 * B].rearrange("p (l j b) -> p l j b", l=2, j=12)
        block = c.enter_context(nc.Block())

        @block.sync
        def _(sp):
            sp.dma_start(cs[:], cT).then_inc(c_in, 16)
            for l, w in enumerate((wmod0, wmod1)):
                sp.dma_start(wm[:, l], w.rearrange("(m p) n -> p m n", p=P)).then_inc(w_in, 16)
            sp.dma_start(k.X[:], x.rearrange("(t p) d -> p t d", p=P)).then_inc(x_in, 16)
            sp.wait_ge(x_in, 16)

        @block.gpsimd
        def _(pool):
            own = Chain(pool, pool_own)
            own.link(pool.memset(k.ident[:], 0.0))
            own.link(pool.memset(k.maskb[:], 0.0))
            own.link(pool.memset(k.mhalf[:], -0.5))
            own.wait()
            own.link(pool.affine_select(out=k.ident[:], in_=k.ident[:], compare_op=ALU.not_equal, fill=1.0,
                                        base=0, pattern=[[-1, P]], channel_multiplier=1))
            own.link(pool.affine_select(out=k.maskb[:], in_=k.maskb[:], compare_op=ALU.is_ge, fill=MASKED,
                                        base=0, pattern=[[-1, P]], channel_multiplier=1))
            own.wait()
            own.link(pool.tensor_copy(k.identb[:], k.ident[:]))
            own.wait()

        @block.scalar
        def _(act):
            act.wait_ge(c_in, 16)
            act.activation(scT[:], cs[:], ACT.Silu).then_inc(silu_done, 1)

        @block.tensor
        def _(pe):
            pe.wait_ge(silu_done, 1)
            pe.wait_ge(w_in, 32)
            for l in range(2):
                for j in range(12):
                    for m in range(DM):
                        last = pe.matmul(cols[:, l, j, :], wm[:, l, m, j * P:(j + 1) * P], scT[:, l, m, :],
                                         start=(m == 0), stop=(m == DM - 1))
            last.then_inc(cols_ready, 1)
            pe.wait_ge(dve_own, 1)
            n = 0
            for l in range(2):
                for b in range(B):
                    for lo, hi in ((0, 2 * D), (2 * D, 3 * D))[:1 + l]:
                        if n >= 4:
                            pe.wait_ge(rows_taken, n - 3)
                        for m in range(DM):
                            last = pe.matmul(k.PS[:, 1 + n % 4, 0:hi - lo], scB[:, l, m, b, :], wm[:, l, m, lo:hi],
                                             start=(m == 0), stop=(m == DM - 1))
                        last.then_inc(rows_ready, 1)
                        n += 1

        @block.vector
        def _(dve):
            own = Chain(dve, dve_own)
            dve.wait_ge(silu_done, 1)
            own.link(dve.tensor_copy(scB[:], scT[:].unsqueeze(4).to_broadcast([P, 2, DM, B, P])))
            dve.wait_ge(cols_ready, 1)
            own.link(dve.tensor_copy(k.modc[:].rearrange("p l c m b -> p (l c m b)"),
                                     cols.rearrange("p l j b -> p (l j b)")))
            own.wait()
            for l in range(2):
                for part in (CA, CB):
                    own.link(dve.tensor_scalar(k.modc[:, l, part], k.modc[:, l, part], 1.0, None, ALU.add))

            def gate(v, s, a):
                own.link(dve.tensor_scalar(s, v, 0.0, 2.0, ALU.is_ge, ALU.mult))
                own.link(dve.scalar_tensor_tensor(out=a, in0=v, scalar=-1.0, in1=v, op0=ALU.mult, op1=ALU.max))
                own.wait()
                own.link(dve.tensor_scalar(s, s, -1.0, None, ALU.add))
                own.wait()
                own.link(dve.scalar_tensor_tensor(out=v, in0=a, scalar=0.25, in1=s, op0=ALU.max, op1=ALU.mult))
                own.wait()

            for l in range(2):
                for part in (GA, GB):
                    gate(k.modc[:, l, part], sgn[:, 0, 0:DM * B].rearrange("p (m b) -> p m b", m=DM),
                         mag[:, 0, 0:DM * B].rearrange("p (m b) -> p m b", m=DM))
            n = 0
            for l in range(2):
                for b in range(B):
                    for parts in ((SA, CA), (GA,))[:1 + l]:
                        dve.wait_ge(rows_ready, n + 1)
                        for i, part in enumerate(parts):
                            src = k.PS[:, 1 + n % 4, i * D:(i + 1) * D]
                            last = dve.tensor_scalar(k.rows[:, l, part, b, :], src,
                                                     1.0 if part == CA else 0.0, None, ALU.add)
                        last.then_inc(rows_taken, 1)
                        n += 1
            dve.wait_ge(rows_taken, n)
            gate(k.rows[:, 1, GA], sgn[:], mag[:])


def row_stats(own, dve, src, stats, mv):
    for t in range(TT):
        own.link(dve.bn_stats(stats[:, t, :], src(t)))
    own.wait()
    own.link(dve.tensor_copy(stats[:, TT, 0:1], stats[:, 0, 0:1]))
    for t in range(TT):
        own.link(dve.bn_aggr(mv[:, t, :], stats[:, t, :]))
    own.wait()


STATS_OPS = 2 * TT + 1


def attention_inputs(k, w, ln_gb, bqk, bv_row):
    nc = k.nc
    with ExitStack() as c:
        wst = k.sb("wst", [P, 3, DM, D], F32, c)
        whi = k.sb("whi", [P, 3, DM, D], F32R, c)
        wlo = k.sb("wlo", [P, 3, DM, D], F32R, c)
        gb = k.sb("gb", [P, 2, DM], F32, c)
        bq = k.sb("bq", [P, 2, DM], F32, c)
        bv = k.sb("bv", [P, D], F32, c)
        stats = k.sb("stats", [P, TT + 1, 6], F32, c)
        mv = k.sb("mv", [P, TT, 2], F32, c)
        var = k.sb("var", [P, TT], F32, c)
        rs = k.sb("rs", [P, TT], F32, c)
        xh = k.sb("xh", [P, TT, D], F32, c)
        h = k.sb("h", [P, TT, D], F32, c)
        hn = k.sb("hn", [P, TT, D], F32, c)
        hf = k.sb("hf", [P, DM, T], F32, c)
        hhi = k.sb("hhi", [P, DM, T], F32R, c)
        hlo = k.sb("hlo", [P, DM, T], F32R, c)
        qf = k.sb("qf", [P, 4, T], F32, c)
        qhi = k.sb("qhi", [P, 4, T], F32R, c)
        qlo = k.sb("qlo", [P, 4, T], F32R, c)
        vf = k.sb("vf", [P, TT, D], F32, c)
        vp = k.sb("vp", [P, TT, HEADS, 2, DH], F32R, c)
        S = lambda n: k.sem("a1_" + n)
        par_in, w_split, own_dve, own_act = S("par_in"), S("w_split"), S("dve"), S("act")
        var_ready, root_done, hn_ready, hT_ready = S("var_ready"), S("root_done"), S("hn_ready"), S("hT_ready")
        hf_done, hhi_done, hlo_done = S("hf_done"), S("hhi_done"), S("hlo_done")
        q_ready, q_done, qhi_done, qlo_done = S("q_ready"), S("q_done"), S("qhi_done"), S("qlo_done")
        v_ready, vf_done, vhi_done, vlo_done = S("v_ready"), S("vf_done"), S("vhi_done"), S("vlo_done")
        q_out, v_out = S("q_out"), S("v_out")
        block = c.enter_context(nc.Block())

        @block.sync
        def _(sp):
            sp.dma_start(gb[:], ln_gb).then_inc(par_in, 16)
            sp.dma_start(bq[:], bqk).then_inc(par_in, 16)
            sp.dma_start(bv[:], bv_row.partition_broadcast(P)).then_inc(par_in, 16)
            for i in range(3):
                sp.dma_start(wst[:, i], w[i].rearrange("(m p) n -> p m n", p=P)).then_inc(par_in, 16)
            def batch(b):
                for j in range(4):
                    wait(sp, qhi_done, b * 4 + j + 1)
                    wait(sp, qlo_done, b * 4 + j + 1)
                    dst = (k.q_parts, k.k_parts)[j // 2]
                    for part, tile in enumerate((qhi, qlo)):
                        sp.dma_start(dst[b, 2 * (j % 2):2 * (j % 2) + 2, :, part].rearrange("q s r t -> (q s) r t"),
                                     f32(tile[:, j, :])).then_inc(q_out, 16)
                wait(sp, vhi_done, (b + 1) * 2)
                wait(sp, vlo_done, (b + 1) * 2)
                sp.dma_start(k.v_parts[b].rearrange("t p h d -> p t (h d)"),
                             f32(vp[:].rearrange("p t h a d -> p t (h a d)"))).then_inc(v_out, 16)
            over_batches(sp, batch)
            sp.wait_ge(q_out, B * 8 * 16)
            sp.wait_ge(v_out, B * 16)

        @block.gpsimd
        def _(pool):
            def batch(b):
                for i in range(2):
                    wait(pool, var_ready, b * 2 + i + 1)
                    pool.tensor_tensor(rs[:], var[:], k.mhalf[:, 0:TT], ALU.pow).then_inc(root_done, 1)
            over_batches(pool, batch)

        @block.scalar
        def _(act):
            act.wait_ge(par_in, 96)
            act.activation(whi[:], wst[:], ACT.Copy).then_inc(w_split, 1)
            act.mul(bq[:, 0], bq[:, 0], 0.25).then_inc(own_act, 1)
            act.wait_ge(own_act, 1)
            def batch(b):
                for m in range(DM):
                    wait(act, hT_ready, b * DM + m + 1)
                    wait(act, hlo_done, b * DM)
                    act.activation(hf[:, m, :], k.PS[:, m, :], ACT.Identity, scale=gb[:, 0, m:m + 1],
                                   bias=gb[:, 1, m:m + 1]).then_inc(hf_done, 1)
                for m in range(DM):
                    wait(act, hf_done, b * DM + m + 1)
                    wait(act, v_ready, b * 2)
                    act.activation(hhi[:, m, :], hf[:, m, :], ACT.Copy).then_inc(hhi_done, 1)
                for j in range(4):
                    wait(act, q_ready, b * 4 + j + 1)
                    wait(act, q_out, b * 128)
                    act.activation(qf[:, j, :], k.PS[:, 2 + j, :], ACT.Identity, scale=(0.25 if j < 2 else 1.0),
                                   bias=bq[:, j // 2, j % 2:j % 2 + 1]).then_inc(q_done, 1)
                    wait(act, q_done, b * 4 + j + 1)
                    act.activation(qhi[:, j, :], qf[:, j, :], ACT.Copy).then_inc(qhi_done, 1)
                for g in range(2):
                    wait(act, vf_done, b * 2 + g + 1)
                    wait(act, v_out, b * 16)
                    for t in (2 * g, 2 * g + 1):
                        last = act.activation(vp[:, t, :, 0, :], vf[:, t, :].rearrange("p (h d) -> p h d", d=DH), ACT.Copy)
                    last.then_inc(vhi_done, 1)
            over_batches(act, batch)

        @block.vector
        def _(dve):
            dve.wait_ge(par_in, 96)
            dve.wait_ge(w_split, 1)
            dve.tensor_tensor(wlo[:], wst[:], f32(whi[:]), ALU.subtract).then_inc(w_split, 1)
            per = 2 * STATS_OPS + TT + 2
            def batch(b):
                own = Chain(dve, own_dve, b * per)
                row_stats(own, dve, lambda t: k.X[:, b * TT + t, :], stats, mv)
                dve.tensor_scalar(var[:], mv[:, :, 1], EPS, None, ALU.add).then_inc(var_ready, 1)
                wait(dve, root_done, b * 2 + 1)
                for t in range(TT):
                    own.link(dve.tensor_scalar(xh[:, t, :], k.X[:, b * TT + t, :], mv[:, t, 0:1], rs[:, t:t + 1],
                                               ALU.subtract, ALU.mult))
                own.wait()
                row = lambda part: k.rows[:, 0, part, b, :].unsqueeze(1).to_broadcast([P, TT, D])
                own.link(dve.tensor_tensor(h[:], xh[:], row(CA), ALU.mult))
                own.wait()
                own.link(dve.tensor_tensor(h[:], h[:], row(SA), ALU.add))
                own.wait()
                row_stats(own, dve, lambda t: h[:, t, :], stats, mv)
                dve.tensor_scalar(var[:], mv[:, :, 1], EPS, None, ALU.add).then_inc(var_ready, 1)
                wait(dve, root_done, b * 2 + 2)
                wait(dve, hT_ready, b * DM)
                for t in range(TT):
                    dve.tensor_scalar(hn[:, t, :], h[:, t, :], mv[:, t, 0:1], rs[:, t:t + 1],
                                      ALU.subtract, ALU.mult).then_inc(hn_ready, 1)
                for m in range(DM):
                    wait(dve, hhi_done, b * DM + m + 1)
                    dve.tensor_tensor(hlo[:, m, :], hf[:, m, :], f32(hhi[:, m, :]), ALU.subtract).then_inc(hlo_done, 1)
                for j in range(4):
                    wait(dve, qhi_done, b * 4 + j + 1)
                    dve.tensor_tensor(qlo[:, j, :], qf[:, j, :], f32(qhi[:, j, :]), ALU.subtract).then_inc(qlo_done, 1)
                for g in range(2):
                    wait(dve, v_ready, b * 2 + g + 1)
                    wait(dve, vlo_done, b * 2)
                    dve.tensor_tensor(vf[:, 2 * g:2 * g + 2, :], k.PS[:, 6 + g, :].rearrange("p (t d) -> p t d", t=2),
                                      bv[:].unsqueeze(1).to_broadcast([P, 2, D]), ALU.add).then_inc(vf_done, 1)
                for g in range(2):
                    wait(dve, vhi_done, b * 2 + g + 1)
                    for t in (2 * g, 2 * g + 1):
                        last = dve.tensor_tensor(vp[:, t, :, 1, :], vf[:, t, :].rearrange("p (h d) -> p h d", d=DH),
                                                 f32(vp[:, t, :, 0, :]), ALU.subtract)
                    last.then_inc(vlo_done, 1)
            over_batches(dve, batch)

        @block.tensor
        def _(pe):
            pe.wait_ge(w_split, 2)
            def batch(b):
                for m in range(DM):
                    wait(pe, hf_done, b * DM)
                    for t in range(TT):
                        wait(pe, hn_ready, b * TT + t + 1)
                        last = pe.transpose(k.PS[:, m, t * P:(t + 1) * P], hn[:, t, m * P:(m + 1) * P], k.ident[:])
                    last.then_inc(hT_ready, 1)
                wait(pe, hlo_done, (b + 1) * DM)
                wait(pe, q_done, b * 4)
                for j in range(4):
                    i, m = j // 2, j % 2
                    for d in range(DM):
                        last = split3(pe, k.PS[:, 2 + j, :], whi[:, i, d, m * P:(m + 1) * P], wlo[:, i, d, m * P:(m + 1) * P],
                                      hhi[:, d, :], hlo[:, d, :], d == 0, d == DM - 1)
                    last.then_inc(q_ready, 1)
                wait(pe, vf_done, b * 2)
                for g in range(2):
                    for t in (2 * g, 2 * g + 1):
                        out = k.PS[:, 6 + g, (t % 2) * D:(t % 2 + 1) * D]
                        for d in range(DM):
                            last = split3(pe, out, hhi[:, d, t * P:(t + 1) * P], hlo[:, d, t * P:(t + 1) * P],
                                          whi[:, 2, d, :], wlo[:, 2, d, :], d == 0, d == DM - 1)
                    last.then_inc(v_ready, 1)
            over_batches(pe, batch)


PT_AT = (0, 4 * P, 8 * P, 7 * P)
PT_BANKS = ((0, 4 * P), (4 * P, 4 * P), (8 * P, 2 * P))


def attention(k, OT):
    nc = k.nc
    NQ = B * QUADS
    with ExitStack() as c:
        Q4 = [k.sb(f"Q4_{u}", [P, 2, T], F32R, c) for u in range(2)]
        K4 = [k.sb(f"K4_{u}", [P, 4, T], F32R, c) for u in range(2)]
        V4 = [k.sb(f"V4_{u}", [P, TT, 4, P], F32R, c) for u in range(2)]
        PR = k.sb("PR", [P, 4, TT, T], F32, c)
        PThi = k.sb("PThi", [P, 2, 10 * P], F32R, c)
        PTlo = k.sb("PTlo", [P, 2, 10 * P], F32R, c)
        nmax = k.sb("nmax", [P, 4, TT], F32, c)
        rsum = k.sb("rsum", [P, 4, TT], F32, c)
        rinv = k.sb("rinv", [P, 4, TT], F32, c)
        carry = k.sb("carry", [P, 8], F32, c)
        S = lambda n: k.sem("a2_" + n)
        zeroed = S("zeroed")
        k_in, q_in, v_in = ([S(f"{n}_in{u}") for u in range(2)] for n in "kqv")
        s_ready, max_done, exp_done, inv_done, norm_done = S("s_ready"), S("max_done"), S("exp_done"), S("inv_done"), S("norm_done")
        t_ready, hi_done, lo_done, av_done, o_hi, o_lo = S("t_ready"), S("hi_done"), S("lo_done"), S("av_done"), S("o_hi"), S("o_lo")
        O = k.PS[:, 7, :]
        block = c.enter_context(nc.Block())
        LT, LA = 2, 3
        ITERS = NQ // 2

        @block.sync
        def _(sp):
            sp.wait_ge(zeroed, 4)
            def batch(b):
                for qp in range(QUADS // 2):
                    it = b * (QUADS // 2) + qp
                    for u in range(2):
                        wait(sp, s_ready, it * 32)
                        for s in range(4):
                            r = 64 * (s % 2)
                            src = k.k_parts[b, qp * 2 + u, s].rearrange("a r t -> (a r) t")
                            for dup in range(2):
                                sp.dma_start(f32(K4[u][r + 32 * dup:r + 32 * dup + 32, s, :]), src).then_inc(k_in[u], 16)
                            src = k.q_parts[b, qp * 2 + u, s]
                            sp.dma_start(f32(Q4[u][r:r + 32, s // 2, :]), src.rearrange("a r t -> (a r) t")).then_inc(q_in[u], 16)
                            for dup in range(2):
                                sp.dma_start(f32(Q4[u][r + 32 + 16 * dup:r + 48 + 16 * dup, s // 2, :]), src[1 - dup]).then_inc(q_in[u], 16)
                    for u in range(2):
                        wait(sp, av_done, it * 8)
                        for s in range(4):
                            sp.dma_start(f32(V4[u][:, :, s, 32 * s:32 * s + 32]),
                                         k.v_parts[b].rearrange("t p h d -> p t h d")[:, :, (qp * 2 + u) * 4 + s, :]).then_inc(v_in[u], 16)
            over_batches(sp, batch)

        @block.gpsimd
        def _(pool):
            for u in range(2):
                pool.memset(f32(K4[u][:]), 0.0).then_inc(zeroed, 1)
                pool.memset(f32(V4[u][:]), 0.0).then_inc(zeroed, 1)
            with pool.Fori(0, ITERS) as it:
                for e in range(8):
                    pool.wait_ge(inv_done, it * 8 + e + 1)
                    pool.tensor_tensor(carry[:, e:e + 1], rinv[:, e % 4, 0:1], rinv[:, e % 4, 0:1], ALU.mult)
                    for i in range(TT):
                        w = P * (i + 1)
                        pool.tensor_scalar(PR[:, e % 4, i, 0:w], PR[:, e % 4, i, 0:w], rinv[:, e % 4, i:i + 1], 1.0,
                                           ALU.mult, ALU.mult).then_inc(norm_done, 1)

        def loop(eng, body):
            body(0, True, False)
            with eng.Fori(1, ITERS) as it:
                body(it, False, False)
            body(ITERS, False, True)

        @block.tensor
        def _(pe):
            def body(it, first, last):
                for e in range(8):
                    h = it * 8 + e
                    u, s = e // 4, e % 4
                    if not last:
                        if s == 0:
                            pe.wait_ge(k_in[u], it * 128 + 128)
                            pe.wait_ge(q_in[u], it * 192 + 192)
                        for i in range(TT):
                            w = P * (i + 1)
                            if not (first and e == 0):
                                pe.wait_ge(exp_done, (h - 1) * TT + i + 1)
                            pe.matmul(k.PS[:, i, 0:w], Q4[u][:, s // 2, P * i:P * i + P], K4[u][:, s, 0:w], start=True, stop=False)
                            pe.matmul(k.PS[:, i, w - P:w], k.identb[:], k.maskb[:], start=False, stop=True).then_inc(s_ready, 1)
                    if (not last or e < LT) and not (first and e < LT):
                        g = h - LT
                        for i in range(TT):
                            pe.wait_ge(norm_done, g * TT + i + 1)
                            for j in (0, 1, 3, 2):
                                if j > i:
                                    continue
                                if not (first and e == LT) and i == j:
                                    bank = (0, 1, 2, 1)[j]
                                    pe.wait_ge(lo_done, (g - 1) * 3 + bank + 1)
                                at = PT_AT[j] + P * (i - j)
                                ins = pe.transpose(k.PS[:, 4 + at // 512, at % 512:at % 512 + P],
                                                   PR[:, (e - LT) % 4, i, P * j:P * j + P], k.ident[:])
                                if i == 3 and j != 1:
                                    ins.then_inc(t_ready, 1)
                    if (not last or e < LA) and not (first and e < LA):
                        g, ge = h - LA, (e - LA) % 8
                        u, s = ge // 4, ge % 4
                        if s == 0:
                            pe.wait_ge(v_in[u], (it if e >= LA else it - 1) * 64 + 64)
                            if not (first and e == LA):
                                pe.wait_ge(o_lo, (it * 2 + u) if e >= LA else (it - 1) * 2 + u)
                        for j in (0, 1, 3, 2):
                            bank = (0, 1, 2, 1)[j]
                            pe.wait_ge(lo_done, g * 3 + bank + 1)
                            w = T - P * j
                            for part, pt in enumerate((PThi, PTlo)):
                                ins = pe.matmul(O[:, P * j:T], V4[u][:, j, s, :], pt[:, ge % 2, PT_AT[j]:PT_AT[j] + w],
                                                start=(s == 0 and j == 0 and part == 0), stop=(s == 3 and j == 2 and part == 1))
                        ins.then_inc(av_done, 1)
            loop(pe, body)

        @block.scalar
        def _(act):
            def body(it, first, last):
                for e in range(8):
                    h = it * 8 + e
                    if not last:
                        if not (first and e < 4):
                            act.wait_ge(t_ready, (h - 4) * 3 + 3)
                        for i in range(TT):
                            w = P * (i + 1)
                            act.wait_ge(max_done, h * TT + i + 1)
                            act.activation(PR[:, e % 4, i, 0:w], k.PS[:, i, 0:w], ACT.Exp, bias=nmax[:, e % 4, i:i + 1],
                                           accum_out=rsum[:, e % 4, i:i + 1]).then_inc(exp_done, 1)
                    if (not last or e < LT) and not (first and e < LT):
                        g = h - LT
                        if not (first and e < LT + 2):
                            act.wait_ge(av_done, g - 1)
                        for n, (at, w) in enumerate(PT_BANKS):
                            act.wait_ge(t_ready, g * 3 + n + 1)
                            act.activation(PThi[:, e % 2, at:at + w], k.PS[:, 4 + n, 0:w], ACT.Copy).then_inc(hi_done, 1)
                    if (not last or e < LA) and not (first and e < LA) and (e - LA) % 4 == 3:
                        q = it * 2 + (0 if e == 6 else -1)
                        act.wait_ge(av_done, (q + 1) * 4)
                        act.activation(OT[0][:, q, :], O, ACT.Copy).then_inc(o_hi, 1)
            loop(act, body)

        @block.vector
        def _(dve):
            def body(it, first, last):
                for e in range(8):
                    h = it * 8 + e
                    if not last:
                        for i in range(TT):
                            w = P * (i + 1)
                            dve.wait_ge(s_ready, h * TT + i + 1)
                            dve.tensor_reduce(nmax[:, e % 4, i:i + 1], k.PS[:, i, 0:w], AX_X, ALU.max, negate=True).then_inc(max_done, 1)
                    if (not last or e < LT) and not (first and e < LT):
                        g = h - LT
                        if not (first and e < LT + 2):
                            dve.wait_ge(av_done, g - 1)
                        for n, (at, w) in enumerate(PT_BANKS):
                            dve.wait_ge(hi_done, g * 3 + n + 1)
                            dve.tensor_tensor(PTlo[:, e % 2, at:at + w], k.PS[:, 4 + n, 0:w], f32(PThi[:, e % 2, at:at + w]),
                                              ALU.subtract).then_inc(lo_done, 1)
                    if not last:
                        dve.wait_ge(exp_done, h * TT + TT)
                        if not (first and e < 4):
                            dve.wait_ge(norm_done, (h - 4) * TT + TT)
                        dve.reciprocal(rinv[:, e % 4, :], rsum[:, e % 4, :]).then_inc(inv_done, 1)
                    if (not last or e < LA) and not (first and e < LA) and (e - LA) % 4 == 3:
                        q = it * 2 + (0 if e == 6 else -1)
                        dve.wait_ge(o_hi, q + 1)
                        dve.tensor_tensor(OT[1][:, q, :], O, f32(OT[0][:, q, :]), ALU.subtract).then_inc(o_lo, 1)
            loop(dve, body)


class Route:

    def __init__(self, k, layer, hT, combT, experts, topk, c):
        n = lambda s: f"r{layer}_{s}"
        sb = lambda name, shape, dt=F32: k.sb(n(name), [P] + shape, dt, c)
        self.k, self.layer, self.hT, self.combT, self.E, self.topk = k, layer, hT, combT, experts, topk
        self.gst, self.ghi, self.glo = sb("gst", [DM, P]), sb("ghi", [DM, P], F32R), sb("glo", [DM, P], F32R)
        self.stats, self.mv = sb("stats", [B, TT + 1, 6]), sb("mv", [B, TT, 2])
        self.var, self.rs = sb("var", [B, TT]), sb("rs", [B, TT])
        self.xh, self.hf, self.lg = sb("xh", [2, TT, D]), sb("hf", [2, DM, T]), sb("lg", [2, T])
        self.mx, self.sm, self.ex = sb("mx", [B, TT]), sb("sm", [B, TT]), sb("ex", [B, TT, experts])
        cand = max(experts + 8 - topk, 8)
        self.cand, self.rep, self.top = sb("cand", [B, TT, cand]), sb("rep", [B, TT, cand]), sb("top", [B, TT, 8])
        self.comb = sb("comb", [B, TT, GROW])
        self.cf = k.sb(n("cf"), [GROW, 2, T], F32, c)
        S = lambda s: k.sem(n(s))
        self.g_in, self.g_split, self.own_dve, self.zeroed = S("g_in"), S("g_split"), S("dve"), S("zeroed")
        self.var_ready, self.root_done, self.xh_ready, self.xT_ready = S("var_ready"), S("root_done"), S("xh_ready"), S("xT_ready")
        self.hf_done, self.lo_done = S("hf_done"), S("lo_done")
        self.lT_ready, self.lg_done, self.l_ready = S("lT_ready"), S("lg_done"), S("l_ready")
        self.d_ready, self.ex_done, self.comb_done = S("d_ready"), S("ex_done"), S("comb_done")
        self.cT_ready, self.cf_done, self.clo_done = S("cT_ready"), S("cf_done"), S("clo_done")

    def load(self, sp, gate_w):
        sp.dma_start(self.gst[:], gate_w).then_inc(self.g_in, 16)

    def fill(self, pool):
        pool.memset(f32(self.combT[:]), 0.0).then_inc(self.zeroed, 1)
        pool.memset(self.cand[:], 2.0).then_inc(self.zeroed, 1)
        pool.memset(self.comb[:], 0.0).then_inc(self.zeroed, 1)
        pool.wait_ge(self.zeroed, 3)
        pool.memset(self.comb[:, :, :, ONE:ONE + 1], 1.0).then_inc(self.zeroed, 1)

    def root(self, pool, b):
        pool.wait_ge(self.var_ready, b + 1)
        pool.tensor_tensor(self.rs[:, b], self.var[:, b], self.k.mhalf[:, 0:TT], ALU.pow).then_inc(self.root_done, 1)

    def act_gate(self, act):
        act.wait_ge(self.g_in, 16)
        act.activation(self.ghi[:], self.gst[:], ACT.Copy).then_inc(self.g_split, 1)
        act.wait_ge(self.zeroed, 4)

    def act_columns(self, act, b):
        modc = self.k.modc
        for m in range(DM):
            act.wait_ge(self.xT_ready, b * DM + m + 1)
            if b >= 2:
                act.wait_ge(self.lo_done, (b - 1) * DM)
            for out in (self.hf[:, b % 2, m, :], self.hT[0][:, m, b * T:(b + 1) * T]):
                act.activation(out, self.k.PS[:, 2 * b + m, :], ACT.Identity, scale=modc[:, self.layer, CB, m, b:b + 1],
                               bias=modc[:, self.layer, SB, m, b:b + 1]).then_inc(self.hf_done, 1)

    def act_logits(self, act, b):
        act.wait_ge(self.lT_ready, b + 1)
        if b >= 2:
            act.wait_ge(self.l_ready, b - 1)
        act.activation(self.lg[:, b % 2], self.k.PS[:, 2 * b, :], ACT.Copy).then_inc(self.lg_done, 1)

    def act_exp(self, act, b):
        act.wait_ge(self.d_ready, b + 1)
        act.activation(self.ex[:, b], self.ex[:, b], ACT.Exp).then_inc(self.ex_done, 1)

    def act_weights(self, act, b):
        act.wait_ge(self.cT_ready, b + 1)
        if b >= 2:
            act.wait_ge(self.clo_done, b - 1)
        for out in (self.cf[:, b % 2], self.combT[0:GROW, b * T:(b + 1) * T]):
            act.activation(out, self.k.PS[0:GROW, 2 * b, :], ACT.Copy).then_inc(self.cf_done, 1)

    def dve_gate(self, dve):
        dve.wait_ge(self.g_split, 1)
        dve.tensor_tensor(self.glo[:], self.gst[:], f32(self.ghi[:]), ALU.subtract).then_inc(self.g_split, 1)
        dve.wait_ge(self.zeroed, 4)
        self.own = Chain(dve, self.own_dve)

    def dve_stats(self, dve, b):
        row_stats(self.own, dve, lambda t: self.k.X[:, b * TT + t, :], self.stats[:, b], self.mv[:, b])
        dve.tensor_scalar(self.var[:, b], self.mv[:, b, :, 1], EPS, None, ALU.add).then_inc(self.var_ready, 1)

    def dve_norm(self, dve, b):
        dve.wait_ge(self.root_done, b + 1)
        if b >= 2:
            dve.wait_ge(self.xT_ready, (b - 1) * DM)
        for t in range(TT):
            dve.tensor_scalar(self.xh[:, b % 2, t, :], self.k.X[:, b * TT + t, :], self.mv[:, b, t, 0:1], self.rs[:, b, t:t + 1],
                              ALU.subtract, ALU.mult).then_inc(self.xh_ready, 1)

    def dve_lo(self, dve, b):
        for m in range(DM):
            dve.wait_ge(self.hf_done, (b * DM + m + 1) * 2)
            cols = slice(b * T, (b + 1) * T)
            dve.tensor_tensor(self.hT[1][:, m, cols], self.hf[:, b % 2, m, :], f32(self.hT[0][:, m, cols]),
                              ALU.subtract).then_inc(self.lo_done, 1)

    def dve_center(self, dve, b):
        own = self.own
        logits = self.k.PS[:, 2 * b + 1, :].rearrange("p (t e) -> p t e", e=P)[:, :, 0:self.E]
        dve.wait_ge(self.l_ready, b + 1)
        own.link(dve.tensor_reduce(self.mx[:, b], logits, AX_X, ALU.max))
        own.wait()
        dve.tensor_tensor(self.ex[:, b], logits, self.mx[:, b].unsqueeze(2).to_broadcast([P, TT, self.E]),
                          ALU.subtract).then_inc(self.d_ready, 1)

    def dve_choose(self, dve, b):
        own, E, topk = self.own, self.E, self.topk
        cand, rep, comb = self.cand[:, b], self.rep[:, b], self.comb[:, b]
        dve.wait_ge(self.ex_done, b + 1)
        own.link(dve.tensor_reduce(self.sm[:, b], self.ex[:, b], AX_X, ALU.add))
        own.wait()
        own.link(dve.reciprocal(self.sm[:, b], self.sm[:, b]))
        own.wait()
        pr = cand[:, :, 0:E]
        own.link(dve.tensor_tensor(pr, self.ex[:, b], self.sm[:, b].unsqueeze(2).to_broadcast([P, TT, E]), ALU.mult))
        own.wait()
        if topk > 1:
            for t in range(TT):
                own.link(dve.max(self.top[:, b, t, :], cand[:, t, 0:E]))
            own.wait()
            own.link(dve.memset(self.top[:, b, :, topk:8], 2.0))
            own.wait()
            for t in range(TT):
                own.link(dve.match_replace(out=rep[:, t, :], in_to_replace=self.top[:, b, t, :], in_values=cand[:, t, :],
                                           imm_value=-1.0))
            own.wait()
            dve.scalar_tensor_tensor(out=comb[:, :, 0:E], in0=rep[:, :, 0:E], scalar=0.0, in1=pr,
                                     op0=ALU.is_lt, op1=ALU.mult).then_inc(self.comb_done, 1)
        else:
            own.link(dve.tensor_tensor(rep[:, :, 0], cand[:, :, 0], cand[:, :, 1], ALU.is_ge))
            own.link(dve.tensor_tensor(rep[:, :, 1], cand[:, :, 1], cand[:, :, 0], ALU.is_gt))
            own.wait()
            dve.tensor_tensor(comb[:, :, 0:E], rep[:, :, 0:E], pr, ALU.mult).then_inc(self.comb_done, 1)

    def dve_weights_lo(self, dve, b):
        dve.wait_ge(self.cf_done, 2 * b + 2)
        cols = slice(b * T, (b + 1) * T)
        dve.tensor_tensor(self.combT[GROW:2 * GROW, cols], self.cf[:, b % 2], f32(self.combT[0:GROW, cols]),
                          ALU.subtract).then_inc(self.clo_done, 1)

    def pe_columns(self, pe, b):
        for m in range(DM):
            for t in range(TT):
                pe.wait_ge(self.xh_ready, b * TT + t + 1)
                last = pe.transpose(self.k.PS[:, 2 * b + m, t * P:(t + 1) * P], self.xh[:, b % 2, t, m * P:(m + 1) * P], self.k.ident[:])
            last.then_inc(self.xT_ready, 1)

    def pe_logits(self, pe, b):
        pe.wait_ge(self.g_split, 2)
        pe.wait_ge(self.lo_done, (b + 1) * DM)
        cols = slice(b * T, (b + 1) * T)
        for d in range(DM):
            last = split3(pe, self.k.PS[:, 2 * b, :], self.ghi[:, d, :], self.glo[:, d, :], self.hT[0][:, d, cols],
                          self.hT[1][:, d, cols], d == 0, d == DM - 1)
        last.then_inc(self.lT_ready, 1)

    def pe_rows(self, pe, b):
        pe.wait_ge(self.lg_done, b + 1)
        for t in range(TT):
            last = pe.transpose(self.k.PS[:, 2 * b + 1, t * P:(t + 1) * P], self.lg[:, b % 2, t * P:(t + 1) * P], self.k.ident[:])
        last.then_inc(self.l_ready, 1)

    def pe_weights(self, pe, b):
        pe.wait_ge(self.comb_done, b + 1)
        for t in range(TT):
            last = pe.transpose(self.k.PS[0:GROW, 2 * b, t * P:(t + 1) * P], self.comb[:, b, t, :], self.k.ident[:])
        last.then_inc(self.cT_ready, 1)


def attention_output_and_route(k, OT, wo, bo_col, hT, combT, gate_w):
    nc = k.nc
    with ExitStack() as c:
        wst = k.sb("wo_st", [P, QUADS, D], F32, c)
        whi = k.sb("wo_hi", [P, QUADS, D], F32R, c)
        wlo = k.sb("wo_lo", [P, QUADS, D], F32R, c)
        bo = k.sb("bo", [P, DM], F32, c)
        gabo = k.sb("gabo", [P, DM, B], F32, c)
        yf = k.sb("yf", [P, 2, DM, T], F32, c)
        S = lambda n: k.sem("a3_" + n)
        w_in, w_split, b_done = S("w_in"), S("w_split"), S("b_done")
        y_ready, yf_done, yT_ready, x_done = S("y_ready"), S("yf_done"), S("yT_ready"), S("x_done")
        r = Route(k, 0, hT, combT, L0_EXPERTS, L0_TOPK, c)
        block = c.enter_context(nc.Block())

        @block.sync
        def _(sp):
            for dup in range(2):
                for h in range(4):
                    sp.dma_start(wst[32 * h + 16 * dup:32 * h + 16 * dup + 16],
                                 wo.rearrange("(q h r) n -> h r q n", q=QUADS, h=4)[h]).then_inc(w_in, 16)
            sp.dma_start(bo[:], bo_col).then_inc(w_in, 16)
            r.load(sp, gate_w)

        @block.gpsimd
        def _(pool):
            r.fill(pool)
            wavefront((0, lambda b: r.root(pool, b)))

        @block.scalar
        def _(act):
            act.wait_ge(w_in, 9 * 16)
            act.activation(whi[:], wst[:], ACT.Copy).then_inc(w_split, 1)
            act.wait_ge(b_done, 1)
            r.act_gate(act)

            def add_bias(b):
                for m in range(DM):
                    act.wait_ge(y_ready, b * DM + m + 1)
                    if b >= 2:
                        act.wait_ge(yT_ready, (b - 1) * 2)
                    act.activation(yf[:, b % 2, m, :], k.PS[:, 2 * b + m, :], ACT.Identity, scale=k.modc[:, 0, GA, m, b:b + 1],
                                   bias=gabo[:, m, b:b + 1]).then_inc(yf_done, 1)
            wavefront((0, add_bias), (2, lambda b: r.act_columns(act, b)), (3, lambda b: r.act_logits(act, b)),
                      (4, lambda b: r.act_exp(act, b)), (5, lambda b: r.act_weights(act, b)))

        @block.vector
        def _(dve):
            dve.wait_ge(w_split, 1)
            dve.tensor_tensor(wlo[:], wst[:], f32(whi[:]), ALU.subtract).then_inc(w_split, 1)
            dve.tensor_tensor(gabo[:], k.modc[:, 0, GA], bo[:].unsqueeze(2).to_broadcast([P, DM, B]), ALU.mult).then_inc(b_done, 1)
            r.dve_gate(dve)

            def add(b):
                for g in range(2):
                    dve.wait_ge(yT_ready, b * 2 + g + 1)
                    x = k.X[:, b * TT + 2 * g:b * TT + 2 * g + 2, :]
                    dve.tensor_tensor(x, k.PS[:, 2 * b + g, :].rearrange("p (t d) -> p t d", t=2), x, ALU.add).then_inc(x_done, 1)
                dve.wait_ge(x_done, b * 2 + 2)
                r.dve_stats(dve, b)
                r.dve_norm(dve, b)
            wavefront((1, add), (2, lambda b: r.dve_lo(dve, b)), (3, lambda b: r.dve_center(dve, b)),
                      (4, lambda b: r.dve_choose(dve, b)), (5, lambda b: r.dve_weights_lo(dve, b)))

        @block.tensor
        def _(pe):
            pe.wait_ge(w_split, 2)

            def products(b):
                for m in range(DM):
                    for q in range(QUADS):
                        last = split3(pe, k.PS[:, 2 * b + m, :], whi[:, q, m * P:(m + 1) * P], wlo[:, q, m * P:(m + 1) * P],
                                      OT[0][:, b * QUADS + q, :], OT[1][:, b * QUADS + q, :], q == 0, q == QUADS - 1)
                    last.then_inc(y_ready, 1)

            def to_rows(b):
                pe.wait_ge(yf_done, (b + 1) * DM)
                for g in range(2):
                    for t in (2 * g, 2 * g + 1):
                        for m in range(DM):
                            last = pe.transpose(k.PS[:, 2 * b + g, (t % 2) * D + m * P:(t % 2) * D + m * P + P],
                                                yf[:, b % 2, m, t * P:(t + 1) * P], k.ident[:])
                    last.then_inc(yT_ready, 1)

            def columns(b):
                pe.wait_ge(x_done, b * 2 + 2)
                r.pe_columns(pe, b)
            wavefront((0, products), (1, to_rows), (2, columns), (3, lambda b: r.pe_logits(pe, b)),
                      (4, lambda b: r.pe_rows(pe, b)), (5, lambda b: r.pe_weights(pe, b)))


def route_alone(k, layer, hT, combT, gate_w, experts, topk):
    with ExitStack() as c:
        r = Route(k, layer, hT, combT, experts, topk, c)
        block = c.enter_context(k.nc.Block())

        @block.sync
        def _(sp):
            r.load(sp, gate_w)
            sp.wait_ge(r.g_in, 16)

        @block.gpsimd
        def _(pool):
            r.fill(pool)
            wavefront((0, lambda b: r.root(pool, b)))

        @block.scalar
        def _(act):
            r.act_gate(act)
            wavefront((0, lambda b: r.act_columns(act, b)), (1, lambda b: r.act_logits(act, b)),
                      (2, lambda b: r.act_exp(act, b)), (3, lambda b: r.act_weights(act, b)))

        @block.vector
        def _(dve):
            r.dve_gate(dve)

            def norm(b):
                r.dve_stats(dve, b)
                r.dve_norm(dve, b)
            wavefront((0, norm), (1, lambda b: r.dve_lo(dve, b)), (2, lambda b: r.dve_center(dve, b)),
                      (3, lambda b: r.dve_choose(dve, b)), (4, lambda b: r.dve_weights_lo(dve, b)))

        @block.tensor
        def _(pe):
            wavefront((0, lambda b: r.pe_columns(pe, b)), (1, lambda b: r.pe_logits(pe, b)),
                      (2, lambda b: r.pe_rows(pe, b)), (3, lambda b: r.pe_weights(pe, b)))


W13 = 2 * DM * P
WC = W13 + P
WALL = WC + D


def experts(k, layer, hT, combT, w, tiles, out):
    nc = k.nc
    HALVES, C = 2, B // 2
    with ExitStack() as c:
        nm = lambda s: f"e{layer}_{s}"
        wst = k.sb(nm("wst"), [P, 2, WALL], F32, c)
        whi = k.sb(nm("whi"), [P, 2, WALL], F32R, c)
        wlo = k.sb(nm("wlo"), [P, 2, WALL], F32R, c)
        sg = k.sb(nm("sg"), [P, 2, T], F32, c)
        cb = k.sb(nm("cb"), [P, 2, T], F32, c)
        um = k.sb(nm("um"), [P, 2, T], F32, c)
        hf = k.sb(nm("hf"), [P, 2, T], F32, c)
        hhi = k.sb(nm("hhi"), [P, 4, T], F32R, c)
        hlo = k.sb(nm("hlo"), [P, 4, T], F32R, c)
        yf = k.sb(nm("yf"), [P, C, DM, T], F32, c)
        S = lambda s: k.sem(nm(s))
        w_in = [S(f"w_in{i}") for i in range(2)]
        w_split, w13_done, w2_done = S("w_split"), S("w13_done"), S("w2_done")
        g_ready, u_ready, c_ready, y_done = S("g_ready"), S("u_ready"), S("c_ready"), S("y_done")
        silu_done, cb_done, um_done, h_done, hi_done, lo_done = (
            S("silu_done"), S("cb_done"), S("um_done"), S("h_done"), S("hi_done"), S("lo_done"))
        yf_done, yT_ready, x_done, x_out = S("yf_done"), S("yT_ready"), S("x_done"), S("x_out")
        block = c.enter_context(nc.Block())
        PEEL = 2 + tiles % 2

        def each_tile(eng, half, body):
            base = half * tiles
            for t in range(PEEL):
                body(t, base + t, (base + t) % 2)
            with eng.Fori(0, (tiles - PEEL) // 2) as pair:
                for j in range(2):
                    t = pair * 2 + (PEEL + j)
                    body(t, base + t, (base + PEEL + j) % 2)

        @block.sync
        def _(sp):
            def load(t, g, par):
                wait(sp, w2_done, g - 1)
                sp.dma_start(wst[:, par, :], w[t]).then_inc(w_in[par], 16)
            for half in range(HALVES):
                each_tile(sp, half, load)
            if out is not None:
                for half in range(HALVES):
                    sp.wait_ge(x_done, 4 * (half + 1))
                    sp.dma_start(out.rearrange("(t p) d -> p t d", p=P)[:, half * 8:half * 8 + 8],
                                 k.X[:, half * 8:half * 8 + 8, :]).then_inc(x_out, 16)
                sp.wait_ge(x_out, 32)

        @block.gpsimd
        def _(pool):
            def split(t, g, par):
                count = (g - par) * 8 + 16 if isinstance(g, int) else (g - par) * 8 + 16
                for lo, hi, free, done in ((0, WC, c_ready, w13_done), (WC, WALL, y_done, w2_done)):
                    if lo == 0:
                        pool.wait_ge(w_in[par], count)
                    wait(pool, free, 2 * g - 2)
                    pool.tensor_tensor(wlo[:, par, W13:W13 + 1], wst[:, par, 0:1], wst[:, par, 1:2], ALU.mult).then_inc(w_split, 1)
                    pool.tensor_scalar(whi[:, par, lo:hi], wst[:, par, lo:hi], 1.0, 1.0, ALU.mult, ALU.mult).then_inc(w_split, 1)
                    pool.wait_ge(w_split, g * 4 + (2 if lo == 0 else 4))
                    end = min(hi, W13) if lo == 0 else hi
                    pool.tensor_tensor(wlo[:, par, lo:end], wst[:, par, lo:end], f32(whi[:, par, lo:end]), ALU.subtract).then_inc(done, 1)
            for half in range(HALVES):
                each_tile(pool, half, split)

        @block.scalar
        def _(act):
            def split_h(n, s):
                wait(act, h_done, n + 1)
                wait(act, y_done, n - 3)
                act.activation(hhi[:, s % 4, :], hf[:, s % 2, :], ACT.Copy).then_inc(hi_done, 1)

            def steps(t, g, par):
                for j in range(C):
                    n, s = 2 * g + j, 2 * par + j
                    if not (isinstance(t, int) and t == 0 and j == 0):
                        split_h(n - 1, s - 1)
                    wait(act, g_ready, n + 1)
                    wait(act, h_done, n - 1)
                    act.activation(sg[:, s % 2, :], k.PS[:, 3 * s % 4, :], ACT.Silu).then_inc(silu_done, 1)
                    wait(act, c_ready, n + 1)
                    wait(act, um_done, n - 1)
                    act.activation(cb[:, s % 2, :], k.PS[:, (3 * s + 2) % 4, :], ACT.Copy).then_inc(cb_done, 1)
            for half in range(HALVES):
                each_tile(act, half, steps)
                N = C * tiles * (half + 1)
                split_h(N - 1, N - 1)
                act.wait_ge(y_done, N)
                for j in range(C):
                    for m in range(DM):
                        if half:
                            act.wait_ge(yT_ready, 4 * half)
                        act.activation(yf[:, j, m, :], k.PS[:, 4 + 2 * j + m, :], ACT.Copy,
                                       scale=k.modc[:, layer, GB, m, C * half + j:C * half + j + 1]).then_inc(yf_done, 1)

        @block.vector
        def _(dve):
            def split_h(n, s):
                wait(dve, hi_done, n + 1)
                wait(dve, y_done, n - 3)
                dve.tensor_tensor(hlo[:, s % 4, :], hf[:, s % 2, :], f32(hhi[:, s % 4, :]), ALU.subtract).then_inc(lo_done, 1)

            def steps(t, g, par):
                for j in range(C):
                    n, s = 2 * g + j, 2 * par + j
                    if not (isinstance(t, int) and t == 0 and j == 0):
                        split_h(n - 1, s - 1)
                    wait(dve, u_ready, n + 1)
                    wait(dve, cb_done, n + 1)
                    dve.tensor_tensor(um[:, s % 2, :], k.PS[:, (3 * s + 1) % 4, :], cb[:, s % 2, :], ALU.mult).then_inc(um_done, 1)
                    wait(dve, um_done, n + 1)
                    wait(dve, silu_done, n + 1)
                    wait(dve, lo_done, n - 1)
                    dve.tensor_tensor(hf[:, s % 2, :], um[:, s % 2, :], sg[:, s % 2, :], ALU.mult).then_inc(h_done, 1)
            for half in range(HALVES):
                each_tile(dve, half, steps)
                N = C * tiles * (half + 1)
                split_h(N - 1, N - 1)
                for i in range(2 * C):
                    dve.wait_ge(yT_ready, 4 * half + i + 1)
                    x = k.X[:, 8 * half + 2 * i:8 * half + 2 * i + 2, :]
                    dve.tensor_tensor(x, k.PS[:, i, :].rearrange("p (t d) -> p t d", t=2), x, ALU.add).then_inc(x_done, 1)

        @block.tensor
        def _(pe):
            for half in range(HALVES):
                def steps(t, g, par):
                    start = isinstance(t, int) and t == 0
                    for j in range(C):
                        n, s = 2 * g + j, 2 * par + j
                        chunk = slice((C * half + j) * T, (C * half + j + 1) * T)
                        if start and j == 0 and half:
                            pe.wait_ge(x_done, 4 * half)
                        if j == 0:
                            wait(pe, w13_done, g + 1)
                        for i, (done, lag) in enumerate(((cb_done, 1), (silu_done, 0))):
                            wait(pe, done, n - lag)
                            for d in range(DM):
                                at = (i * DM + d) * P
                                ins = split3(pe, k.PS[:, (3 * s + i) % 4, :], whi[:, par, at:at + P], wlo[:, par, at:at + P],
                                             hT[0][:, d, chunk], hT[1][:, d, chunk], d == 0, d == DM - 1)
                            ins.then_inc((g_ready, u_ready)[i], 1)
                        wait(pe, um_done, n)
                        pe.matmul(k.PS[:, (3 * s + 2) % 4, :], whi[:, par, W13:WC], combT[:, chunk], start=True, stop=True).then_inc(c_ready, 1)
                        if not start:
                            into_y2(t - 1, g - 1, 1 - par, j)

                def into_y2(t, g, par, j, last=False):
                    n, s = 2 * g + j, 2 * par + j
                    wait(pe, lo_done, n + 1)
                    first = isinstance(t, int) and t == 0
                    if j == 0:
                        wait(pe, w2_done, g + 1)
                    if first and half:
                        pe.wait_ge(yf_done, 4 * half)
                    for m in range(DM):
                        ins = split3(pe, k.PS[:, 4 + 2 * j + m, :], whi[:, par, WC + m * P:WC + (m + 1) * P],
                                     wlo[:, par, WC + m * P:WC + (m + 1) * P], hhi[:, s % 4, :], hlo[:, s % 4, :], first, last)
                    ins.then_inc(y_done, 1)
                each_tile(pe, half, steps)
                g = (half + 1) * tiles - 1
                for j in range(C):
                    into_y2(tiles - 1, g, g % 2, j, True)
                N = C * tiles * (half + 1)
                pe.wait_ge(cb_done, N)
                pe.wait_ge(um_done, N)
                pe.wait_ge(silu_done, N)
                for j in range(C):
                    pe.wait_ge(yf_done, 4 * half + 2 * j + 2)
                    for i in range(2):
                        for t in (2 * i, 2 * i + 1):
                            for m in range(DM):
                                ins = pe.transpose(k.PS[:, 2 * j + i, (t % 2) * D + m * P:(t % 2) * D + m * P + P],
                                                   yf[:, j, m, t * P:(t + 1) * P], k.ident[:])
                        ins.then_inc(yT_ready, 1)


def gated_conv(k, H, hT, w_in_d, w_out_d, taps_d):
    nc = k.nc
    with ExitStack() as c:
        n = lambda s: f"c_{s}"
        wi_st = k.sb(n("wi_st"), [P, DM, 2 * INNER], F32, c)
        wi_hi = k.sb(n("wi_hi"), [P, DM, 2 * INNER], F32R, c)
        wi_lo = k.sb(n("wi_lo"), [P, DM, 2 * INNER], F32R, c)
        wo_st = k.sb(n("wo_st"), [P, IT, D], F32, c)
        wo_hi = k.sb(n("wo_hi"), [P, IT, D], F32R, c)
        wo_lo = k.sb(n("wo_lo"), [P, IT, D], F32R, c)
        tap = k.sb(n("tap"), [P, IT, TAPS + 1], F32, c)
        stats = k.sb(n("stats"), [P, TT + 1, 6], F32, c)
        mv = k.sb(n("mv"), [P, TT, 2], F32, c)
        var, rs = k.sb(n("var"), [P, 3, TT], F32, c), k.sb(n("rs"), [P, 3, TT], F32, c)
        ss, sq = k.sb(n("ss"), [P, 2, TT], F32, c), k.sb(n("sq"), [P, 2, TT, D], F32, c)
        hn = k.sb(n("hn"), [P, 2, TT, D], F32, c)
        rhi, rlo = k.sb(n("rhi"), [P, 2, DM, T], F32R, c), k.sb(n("rlo"), [P, 2, DM, T], F32R, c)
        acc = k.sb(n("acc"), [P, 2, T], F32, c)
        sx, sz = k.sb(n("sx"), [P, 2, T], F32, c), k.sb(n("sz"), [P, 2, T], F32, c)
        yv = k.sb(n("yv"), [P, IT, T], F32, c)
        yhi, ylo = k.sb(n("yhi"), [P, IT, T], F32R, c), k.sb(n("ylo"), [P, IT, T], F32R, c)
        yf = k.sb(n("yf"), [P, DM, T], F32, c)
        S = lambda s: k.sem(n(s))
        w_in, w_hi, w_lo, own_dve = S("w_in"), S("w_hi"), S("w_lo"), S("dve")
        LN, IN, OUT = 0, 1, 2
        var_ready, root_done = [S(f"var_ready{i}") for i in range(3)], [S(f"root_done{i}") for i in range(3)]
        h_ready, h_added = S("h_ready"), S("h_added")
        ss_done, hn_ready, rT_ready = ([S(f"{s}{i}") for i in range(2)] for s in ("ss_done", "hn_ready", "rT_ready"))
        rhi_done, rlo_done = ([S(f"{s}{i}") for i in range(2)] for s in ("rhi_done", "rlo_done"))
        p_ready, z_ready, conv_done, sx_done, sz_done = S("p_ready"), S("z_ready"), S("conv_done"), S("sx_done"), S("sz_done")
        yv_done, yhi_done, ylo_done, o_done = S("yv_done"), S("yhi_done"), S("ylo_done"), S("o_done")
        yf_done, yT_ready = S("yf_done"), S("yT_ready")
        block = c.enter_context(nc.Block())

        turns = []
        wavefront((2, lambda b: turns.append(("rows", b))), (0, lambda b: turns.append((IN, b))),
                  (2, lambda b: turns.append((OUT, b))))

        def wait_turn(pe, kind, b):
            at = turns.index((kind, b))
            if at:
                before, bb = turns[at - 1]
                pe.wait_ge(h_added if before == "rows" else rlo_done[before - 1], DM * (bb + 1))

        @block.sync
        def _(sp):
            sp.dma_start(wi_st[:], w_in_d.rearrange("(m p) n -> p m n", p=P)).then_inc(w_in, 16)
            sp.dma_start(wo_st[:], w_out_d.rearrange("(e p) n -> p e n", p=P)).then_inc(w_in, 16)
            sp.dma_start(tap[:], taps_d).then_inc(w_in, 16)
            sp.wait_ge(w_in, 48)

        @block.gpsimd
        def _(pool):
            def root(kind):
                def stage(b):
                    pool.wait_ge(var_ready[kind], b + 1)
                    pool.tensor_tensor(rs[:, kind], var[:, kind], k.mhalf[:, 0:TT], ALU.pow).then_inc(root_done[kind], 1)
                return stage

            def gate(e):
                def stage(b):
                    i = b * IT + e
                    pool.wait_ge(sx_done, i + 1)
                    pool.wait_ge(sz_done, i + 1)
                    if b:
                        pool.wait_ge(ylo_done, i - IT + 1)
                    pool.tensor_tensor(yv[:, e, :], sx[:, i % 2, :], sz[:, i % 2, :], ALU.mult).then_inc(yv_done, 1)
                return stage
            wavefront((1, gate(0)), (0, root(LN)), (1, gate(1)), (0, root(IN)), (1, gate(2)), (2, root(OUT)), (1, gate(3)))

        @block.scalar
        def _(act):
            def y_out(b):
                act.wait_ge(o_done, (b + 1) * IT)
                if b:
                    act.wait_ge(yT_ready, 2 * b)
                for m in range(DM):
                    act.activation(yf[:, m, :], k.PS[:, 6 + m, :], ACT.Copy).then_inc(yf_done, 1)

            def silu_z(e):
                def stage(b):
                    i = b * IT + e
                    act.wait_ge(z_ready, i + 1)
                    if i >= 2:
                        act.wait_ge(yv_done, i - 1)
                    act.activation(sz[:, i % 2, :], k.PS[:, 3 + 2 * (i % 2), :], ACT.Silu).then_inc(sz_done, 1)
                return stage

            def silu_x(e):
                def stage(b):
                    i = b * IT + e
                    act.wait_ge(conv_done, i + 1)
                    act.activation(sx[:, i % 2, :], acc[:, i % 2, :], ACT.Silu).then_inc(sx_done, 1)
                return stage

            def split_y(e):
                def stage(b):
                    i = b * IT + e
                    act.wait_ge(yv_done, i + 1)
                    if b:
                        act.wait_ge(o_done, i - IT + 1)
                    act.activation(yhi[:, e, :], yv[:, e, :], ACT.Copy).then_inc(yhi_done, 1)
                return stage

            def squares(i):
                def stage(b):
                    act.wait_ge((h_ready, h_added)[i], (1, 2)[i] * (b + 1))
                    if b:
                        act.wait_ge(var_ready[1 + i], b)
                    for t in range(TT):
                        act.activation(sq[:, i, t, :], H[:, b * TT + t, :], ACT.Square,
                                       accum_out=ss[:, i, t:t + 1]).then_inc(ss_done[i], 1)
                return stage

            def hi(i):
                def stage(b):
                    for m in range(DM):
                        act.wait_ge(rT_ready[i], b * DM + m + 1)
                        if i == 0 and b >= 2:
                            act.wait_ge(z_ready, (b - 1) * IT)
                        out = rhi[:, b % 2, m, :] if i == 0 else hT[0][:, m, b * T:(b + 1) * T]
                        act.activation(out, k.PS[:, m, :], ACT.Copy).then_inc(rhi_done[i], 1)
                return stage

            act.wait_ge(w_in, 48)
            act.activation(wi_hi[:], wi_st[:], ACT.Copy).then_inc(w_hi, 1)
            act.activation(wo_hi[:], wo_st[:], ACT.Copy).then_inc(w_hi, 1)
            wavefront((1, silu_z(0)), (3, hi(1)), (1, silu_x(0)), (2, split_y(3)), (1, silu_z(1)), (1, silu_x(1)),
                      (0, squares(0)), (2, y_out), (1, split_y(0)), (1, silu_z(2)), (1, silu_x(2)), (1, split_y(1)),
                      (2, squares(1)), (1, silu_z(3)), (0, hi(0)), (1, silu_x(3)), (1, split_y(2)))

        @block.vector
        def _(dve):
            own = Chain(dve, own_dve)

            def stats_of(b):
                row_stats(own, dve, lambda t: k.X[:, b * TT + t, :], stats, mv)
                dve.tensor_scalar(var[:, LN], mv[:, :, 1], EPS, None, ALU.add).then_inc(var_ready[LN], 1)

            def layer_norm(b):
                dve.wait_ge(root_done[LN], b + 1)
                h = H[:, b * TT:(b + 1) * TT, :]
                for t in range(TT):
                    own.link(dve.tensor_scalar(H[:, b * TT + t, :], k.X[:, b * TT + t, :], mv[:, t, 0:1], rs[:, LN, t:t + 1],
                                               ALU.subtract, ALU.mult))
                own.wait()
                row = lambda part: k.rows[:, 1, part, b, :].unsqueeze(1).to_broadcast([P, TT, D])
                own.link(dve.tensor_tensor(h, h, row(CA), ALU.mult))
                own.wait()
                dve.tensor_tensor(h, h, row(SA), ALU.add).then_inc(h_ready, 1)

            def rms_var(i):
                def stage(b):
                    dve.wait_ge(ss_done[i], (b + 1) * TT)
                    dve.tensor_scalar(var[:, 1 + i], ss[:, i], 1e-24, 1.0 / D, ALU.max, ALU.mult).then_inc(var_ready[1 + i], 1)
                    if i == 0 and b == 0:
                        dve.wait_ge(w_hi, 2)
                        dve.tensor_tensor(wi_lo[:], wi_st[:], f32(wi_hi[:]), ALU.subtract).then_inc(w_lo, 1)
                        dve.tensor_tensor(wo_lo[:], wo_st[:], f32(wo_hi[:]), ALU.subtract).then_inc(w_lo, 1)
                return stage

            def rms(i):
                def stage(b):
                    dve.wait_ge(root_done[1 + i], b + 1)
                    if b:
                        dve.wait_ge(rT_ready[i], b * DM)
                    for t in range(TT):
                        dve.tensor_scalar(hn[:, i, t, :], H[:, b * TT + t, :], rs[:, 1 + i, t:t + 1], None,
                                          ALU.mult).then_inc(hn_ready[i], 1)
                return stage

            def lo(i):
                def stage(b):
                    cols = slice(b * T, (b + 1) * T)
                    for m in range(DM):
                        dve.wait_ge(rhi_done[i], b * DM + m + 1)
                        hi, out = (rhi[:, b % 2, m, :], rlo[:, b % 2, m, :]) if i == 0 else (hT[0][:, m, cols], hT[1][:, m, cols])
                        dve.tensor_tensor(out, k.PS[:, m, :], f32(hi), ALU.subtract).then_inc(rlo_done[i], 1)
                return stage

            def conv(e):
                def stage(b):
                    i = b * IT + e
                    p, a = k.PS[:, 2 + 2 * (i % 2), :], acc[:, i % 2, :]
                    dve.wait_ge(p_ready, i + 1)
                    if i >= 2:
                        dve.wait_ge(sx_done, i - 1)
                    own.link(dve.tensor_scalar(a, p, tap[:, e, TAPS - 1:TAPS], tap[:, e, TAPS:TAPS + 1], ALU.mult, ALU.add))
                    for j in range(1, TAPS):
                        own.wait()
                        ins = dve.scalar_tensor_tensor(out=a[:, j:T], in0=p[:, 0:T - j], scalar=tap[:, e, TAPS - 1 - j:TAPS - j],
                                                       in1=a[:, j:T], op0=ALU.mult, op1=ALU.add)
                        if j < TAPS - 1:
                            own.link(ins)
                    ins.then_inc(conv_done, 1)
                return stage

            def split_y(e):
                def stage(b):
                    i = b * IT + e
                    dve.wait_ge(yhi_done, i + 1)
                    dve.tensor_tensor(ylo[:, e, :], yv[:, e, :], f32(yhi[:, e, :]), ALU.subtract).then_inc(ylo_done, 1)
                return stage

            def add(b):
                for g in range(2):
                    dve.wait_ge(yT_ready, b * 2 + g + 1)
                    x = H[:, b * TT + 2 * g:b * TT + 2 * g + 2, :]
                    dve.tensor_tensor(x, k.PS[:, g, :].rearrange("p (t d) -> p t d", t=2), x, ALU.add).then_inc(h_added, 1)
            wavefront((1, conv(0)), (3, lo(1)), (2, split_y(2)), (0, stats_of), (1, conv(1)), (2, split_y(3)),
                      (0, layer_norm), (1, conv(2)), (1, split_y(0)), (0, rms_var(0)), (2, add), (0, rms(0)), (1, conv(3)),
                      (1, split_y(1)), (2, rms_var(1)), (0, lo(0)), (2, rms(1)))

        @block.tensor
        def _(pe):
            def columns(i):
                def stage(b):
                    wait_turn(pe, 1 + i, b)
                    for m in range(DM):
                        for t in range(TT):
                            pe.wait_ge(hn_ready[i], b * TT + t + 1)
                            last = pe.transpose(k.PS[:, m, t * P:(t + 1) * P], hn[:, i, t, m * P:(m + 1) * P], k.ident[:])
                        last.then_inc(rT_ready[i], 1)
                return stage

            def up(e):
                def stage(b):
                    i = b * IT + e
                    if e == 0:
                        pe.wait_ge(rlo_done[0], (b + 1) * DM)
                    for part, (free, done) in enumerate(((conv_done, p_ready), (sz_done, z_ready))):
                        if i >= 2:
                            pe.wait_ge(free, i - 1)
                        for d in range(DM):
                            at = part * INNER + e * P
                            last = split3(pe, k.PS[:, 2 + 2 * (i % 2) + part, :], wi_hi[:, d, at:at + P], wi_lo[:, d, at:at + P],
                                          rhi[:, b % 2, d, :], rlo[:, b % 2, d, :], d == 0, d == DM - 1)
                        last.then_inc(done, 1)
                return stage

            def down(e):
                def stage(b):
                    i = b * IT + e
                    if e == 0 and b:
                        pe.wait_ge(yf_done, b * DM)
                    pe.wait_ge(ylo_done, i + 1)
                    for m in range(DM):
                        last = split3(pe, k.PS[:, 6 + m, :], wo_hi[:, e, m * P:(m + 1) * P], wo_lo[:, e, m * P:(m + 1) * P],
                                      yhi[:, e, :], ylo[:, e, :], e == 0, e == IT - 1)
                    last.then_inc(o_done, 1)
                return stage

            def rows(b):
                wait_turn(pe, "rows", b)
                pe.wait_ge(yf_done, (b + 1) * DM)
                for g in range(2):
                    for t in (2 * g, 2 * g + 1):
                        for m in range(DM):
                            last = pe.transpose(k.PS[:, g, (t % 2) * D + m * P:(t % 2) * D + m * P + P],
                                                yf[:, m, t * P:(t + 1) * P], k.ident[:])
                    last.then_inc(yT_ready, 1)
            pe.wait_ge(w_lo, 2)
            wavefront((1, up(0)), (2, down(2)), (1, up(1)), (2, down(3)), (1, up(2)), (2, rows), (1, down(0)), (1, up(3)),
                      (0, columns(0)), (1, down(1)), (2, columns(1)))


def mlp(k, H, hT, w_d):
    nc = k.nc
    WM = DM * P
    with ExitStack() as c:
        n = lambda s: f"m_{s}"
        wst = k.sb(n("wst"), [P, MLP_T, WM + D], F32, c)
        whi = k.sb(n("whi"), [P, MLP_T, WM + D], F32R, c)
        wlo = k.sb(n("wlo"), [P, MLP_T, WM + D], F32R, c)
        hi, lo = k.sb(n("hi"), [P, 4, T], F32R, c), k.sb(n("lo"), [P, 4, T], F32R, c)
        yf = k.sb(n("yf"), [P, DM, T], F32, c)
        S = lambda s: k.sem(n(s))
        w_in = [S(f"w_in{i}") for i in range(MLP_T)]
        whi_done, wlo_done = S("whi_done"), S("wlo_done")
        u_ready, hi_done, lo_done, o_done = S("u_ready"), S("hi_done"), S("lo_done"), S("o_done")
        yf_done, yT_ready, h_done, x_done, own_dve = S("yf_done"), S("yT_ready"), S("h_done"), S("x_done"), S("dve")
        block = c.enter_context(nc.Block())

        def split_weights(b, i, split):
            if isinstance(b, int) and b == 0:
                for j in range(0 if i == 0 else i + 2, min(i + 3, MLP_T)):
                    split(j)

        @block.sync
        def _(sp):
            for i in range(MLP_T):
                sp.dma_start(wst[:, i, :], w_d[i]).then_inc(w_in[i], 16)

        @block.scalar
        def _(act):
            def split(i):
                act.wait_ge(w_in[i], 16)
                act.activation(whi[:, i, :], wst[:, i, :], ACT.Copy).then_inc(whi_done, 1)

            def batch(b):
                for i in range(MLP_T):
                    split_weights(b, i, split)
                    wait(act, u_ready, b * MLP_T + i + 1)
                    wait(act, o_done, b * MLP_T + max(i - 3, 0))
                    act.activation(hi[:, i % 4, :], k.PS[:, i % 4, :], ACT.Relu).then_inc(hi_done, 1)
                wait(act, o_done, (b + 1) * MLP_T)
                for m in range(DM):
                    wait(act, yT_ready, b * 2)
                    act.activation(yf[:, m, :], k.PS[:, 4 + m, :], ACT.Copy).then_inc(yf_done, 1)
            over_batches(act, batch)

        @block.vector
        def _(dve):
            def split(i):
                dve.wait_ge(whi_done, i + 1)
                dve.tensor_tensor(wlo[:, i, :], wst[:, i, :], f32(whi[:, i, :]), ALU.subtract).then_inc(wlo_done, 1)

            def residual(b):
                own = Chain(dve, own_dve, b * 2)
                h = H[:, bass.ds(b * TT, TT), :]
                for g in range(2):
                    wait(dve, yT_ready, b * 2 + g + 1)
                    hg = H[:, bass.ds(b * TT + 2 * g, 2), :]
                    dve.tensor_tensor(hg, k.PS[:, 6 + g, :].rearrange("p (t d) -> p t d", t=2), hg, ALU.add).then_inc(h_done, 1)
                wait(dve, h_done, b * 2 + 2)
                own.link(dve.tensor_tensor(h, h, k.rows[:, 1, GA, b, :].unsqueeze(1).to_broadcast([P, TT, D]), ALU.mult))
                own.wait()
                x = k.X[:, bass.ds(b * TT, TT), :]
                own.link(dve.tensor_tensor(x, x, h, ALU.add))

            def batch(b):
                for i in range(MLP_T):
                    split_weights(b, i, split)
                    if i == 2 and not (isinstance(b, int) and b == 0):
                        residual(b - 1)
                    wait(dve, hi_done, b * MLP_T + i + 1)
                    wait(dve, o_done, b * MLP_T + max(i - 3, 0))
                    dve.scalar_tensor_tensor(out=lo[:, i % 4, :], in0=k.PS[:, i % 4, :], scalar=0.0, in1=f32(hi[:, i % 4, :]),
                                             op0=ALU.max, op1=ALU.subtract).then_inc(lo_done, 1)
            over_batches(dve, batch)
            residual(B - 1)

        @block.tensor
        def _(pe):
            def rows(b):
                wait(pe, yf_done, (b + 1) * DM)
                for g in range(2):
                    for t in (2 * g, 2 * g + 1):
                        for m in range(DM):
                            last = pe.transpose(k.PS[:, 6 + g, (t % 2) * D + m * P:(t % 2) * D + m * P + P],
                                                yf[:, m, t * P:(t + 1) * P], k.ident[:])
                    last.then_inc(yT_ready, 1)

            def batch(b):
                def up(i):
                    if isinstance(b, int):
                        pe.wait_ge(wlo_done, i + 1)
                    wait(pe, lo_done, b * MLP_T + max(i - 3, 0))
                    for d in range(DM):
                        last = split3(pe, k.PS[:, i % 4, :], whi[:, i, d * P:(d + 1) * P], wlo[:, i, d * P:(d + 1) * P],
                                      hT[0][:, d, bass.ds(b * T, T)], hT[1][:, d, bass.ds(b * T, T)], d == 0, d == DM - 1)
                    last.then_inc(u_ready, 1)

                def down(i):
                    if i == 0:
                        wait(pe, yf_done, b * DM)
                    wait(pe, lo_done, b * MLP_T + i + 1)
                    for m in range(DM):
                        last = split3(pe, k.PS[:, 4 + m, :], whi[:, i, WM + m * P:WM + (m + 1) * P], wlo[:, i, WM + m * P:WM + (m + 1) * P],
                                      hi[:, i % 4, :], lo[:, i % 4, :], i == 0, i == MLP_T - 1)
                    last.then_inc(o_done, 1)
                for i in range(MLP_T):
                    up(i)
                    if i == 1 and not (isinstance(b, int) and b == 0):
                        rows(b - 1)
                    if i >= 2:
                        down(i - 2)
                down(MLP_T - 2)
                down(MLP_T - 1)
            over_batches(pe, batch)
            rows(B - 1)


def layout(a):
    import numpy as np

    def cols(*vs):
        return np.ascontiguousarray(np.stack([v.reshape(DM, P) for v in vs]).transpose(2, 0, 1))

    o = {"x": a["L0_attn_X"].reshape(B * T, D)}
    o["cT"] = np.ascontiguousarray(np.stack([a["L0_c"], a["L1_c"]]).reshape(2, B, DM, P).transpose(3, 0, 2, 1))
    o["wmod0"], o["wmod1"] = a["L0_wmod"], a["L1_wmod"]
    o["wqkv"] = np.stack([a["L0_attn_Wq"], a["L0_attn_Wk"], a["L0_attn_Wv"]])
    o["ln_gb"] = cols(a["L0_attn_ln_g"], a["L0_attn_ln_b"])
    o["bqk"] = cols(a["L0_attn_bq"], a["L0_attn_bk"])
    o["bv"] = a["L0_attn_bv"]
    o["wo"] = a["L0_attn_Wo"]
    o["bo"] = np.ascontiguousarray(a["L0_attn_bo"].reshape(DM, P).T)

    def gate(g):
        full = np.zeros((P, DM, P), np.float32)
        full[:, :, :g.shape[0]] = g.reshape(-1, DM, P).transpose(2, 1, 0)
        return full

    def blocks(w1, w3, w2, experts, ff, tiles):
        full = np.zeros((tiles, P, WALL), np.float32)
        up = np.zeros((2, tiles * P, D), np.float32)
        up[0, :w1.shape[0]], up[1, :w3.shape[0]] = w1, w3
        full[:, :, :W13] = up.reshape(2, tiles, P, DM, P).transpose(1, 4, 0, 3, 2).reshape(tiles, P, W13)
        row = np.minimum(np.arange(tiles * P) // ff, experts)
        row[row == experts] = ONE
        for part in (0, GROW):
            sel = np.zeros((tiles * P, P), np.float32)
            sel[np.arange(tiles * P), row + part] = 1.0
            full[:, :, W13:WC] += sel.reshape(tiles, P, P).transpose(0, 2, 1)
        down = np.zeros((tiles * P, D), np.float32)
        down[:w2.shape[1]] = w2.T
        full[:, :, WC:] = down.reshape(tiles, P, D)
        return full

    o["gate0"], o["gate1"] = gate(a["L0_ffn_Wg"]), gate(a["L1_ffn_gate_w"])
    flat = lambda v: v.reshape(-1, D)
    down = lambda v: v.transpose(1, 0, 2).reshape(D, -1)
    o["ffn0"] = blocks(np.concatenate([flat(a["L0_ffn_W1"]), a["L0_ffn_W1s"]]), np.concatenate([flat(a["L0_ffn_W3"]), a["L0_ffn_W3s"]]),
                       np.concatenate([down(a["L0_ffn_W2"]), a["L0_ffn_W2s"]], 1), L0_EXPERTS, L0_FF, L0_TILES)
    o["ffn1"] = blocks(flat(a["L1_ffn_w_gate"]), flat(a["L1_ffn_w_up"]), down(a["L1_ffn_w_down"]), L1_EXPERTS, L1_FF, L1_TILES)
    o["conv_in"] = np.ascontiguousarray(a["L1_attn_W_in"].T)
    o["conv_out"] = np.ascontiguousarray(a["L1_attn_W_out"].T)
    o["taps"] = np.ascontiguousarray(np.concatenate([a["L1_attn_conv_w"][:, 0], a["L1_attn_conv_b"][:, None]], 1)
                                     .reshape(IT, P, TAPS + 1).transpose(1, 0, 2))
    o["mlp"] = np.concatenate([a["L1_attn_W_mlp1"].reshape(MLP_T, P, DM, P).transpose(0, 3, 2, 1).reshape(MLP_T, P, D),
                               a["L1_attn_W_mlp2"].T.reshape(MLP_T, P, D)], 2)
    return o


def program(nc, a, out):
    with ExitStack() as ctx:
        k = Core(nc, ctx)
        setup(k, a["x"], a["cT"], a["wmod0"], a["wmod1"])
        attention_inputs(k, a["wqkv"], a["ln_gb"], a["bqk"], a["bv"])
        with ExitStack() as c:
            OT = [k.sb(f"OT{i}", [P, B * QUADS, T], F32R, c) for i in range(2)]
            attention(k, OT)
            hT = [k.sb(f"hT{i}", [P, DM, B * T], F32R, side="right") for i in range(2)]
            combT = k.sb("combT", [P, B * T], F32R, side="right")
            attention_output_and_route(k, OT, a["wo"], a["bo"], hT, combT, a["gate0"])
        k.recycle()
        experts(k, 0, hT, combT, a["ffn0"], L0_TILES, None)
        with ExitStack() as c:
            H = k.sb("H", [P, NT, D], F32, c)
            gated_conv(k, H, hT, a["conv_in"], a["conv_out"], a["taps"])
            mlp(k, H, hT, a["mlp"])
        route_alone(k, 1, hT, combT, a["gate1"], L1_EXPERTS, 1)
        experts(k, 1, hT, combT, a["ffn1"], L1_TILES, out)


def kernel(**inputs):
    import numpy as np
    import concourse.bacc as bacc
    from concourse.bass_utils import run_bass_kernel_spmd

    nc = bacc.Bacc("TRN2", target_bir_lowering=False, num_devices=1)
    arrays = {f"in_{n}": np.ascontiguousarray(v) for n, v in layout(inputs).items()}
    aps = {n[3:]: nc.dram_tensor(n, v.shape, mybir.dt.from_np(v.dtype), kind="ExternalInput").ap() for n, v in arrays.items()}
    out = nc.dram_tensor("out", (B * T, D), F32, kind="ExternalOutput").ap()
    program(nc, aps, out)
    got = run_bass_kernel_spmd(nc, [arrays], core_ids=[0])
    return got.results[0]["out"].reshape(B, T, D)
```

```python
from contextlib import ExitStack

import concourse.bass as bass
from concourse import mybir

F32 = mybir.dt.float32
F32R = mybir.dt.float32r
BF16 = mybir.dt.bfloat16
ALU = mybir.AluOpType
ACT = mybir.ActivationFunctionType
AX_X = mybir.AxisListType.X

P = 128
D = 256
DM = D // P
B, T = 4, 512
NT = B * T // P
TT = T // P
HEADS, DH = 16, 16
QUADS = HEADS // 4
EPS = 1e-5
L0_EXPERTS, L0_TOPK, L0_FF, L0_SHARED = 16, 4, 176, 352
L0_TILES = -(-(L0_EXPERTS * L0_FF + L0_SHARED) // P)
L1_EXPERTS, L1_FF = 2, 1024
L1_TILES = L1_EXPERTS * L1_FF // P
INNER, TAPS = 512, 4
IT = INNER // P
MLP_T = 4 * D // P
GROW = 32
ONE = 16
MASKED = -3.0e38
SA, CA, GA, SB, CB, GB = range(6)


def f32(ap):
    return ap.bitcast(F32)


def split3(pe, out, w_hi, w_lo, x_hi, x_lo, first, last):
    pe.matmul(out, w_hi, x_lo, start=first, stop=False)
    pe.matmul(out, w_lo, x_hi, start=False, stop=False)
    return pe.matmul(out, w_hi, x_hi, start=False, stop=last)


def wait(eng, sem, n):
    if not isinstance(n, int) or n > 0:
        eng.wait_ge(sem, n)


def wavefront(*stages):
    for step in range(B + max(lag for lag, _ in stages)):
        for lag, stage in stages:
            if 0 <= step - lag < B:
                stage(step - lag)


class Chain:

    def __init__(self, eng, sem, start=0):
        self.eng, self.sem, self.n = eng, sem, start

    def link(self, ins):
        ins.then_inc(self.sem, 1)
        self.n = self.n + 1
        return self.n

    def wait(self, n=None):
        self.eng.wait_ge(self.sem, self.n if n is None else n)


class Core:

    def __init__(self, nc, ctx):
        self.nc, self.ctx, self.sems = nc, ctx, []
        sb, dram = self.sb, self.dram
        self.PS = ctx.enter_context(nc.psum_tensor("PS", [P, 8, 512], F32))
        self.X = sb("X", [P, NT, D], F32)
        self.ident = sb("ident", [P, P], F32)
        self.identb = sb("identb", [P, P], BF16)
        self.mhalf = sb("mhalf", [P, TT], F32)
        self.maskb = sb("maskb", [P, P], BF16)
        self.modc = sb("modc", [P, 2, 6, DM, B], F32)
        self.rows = sb("rows", [P, 2, 3, B, D], F32)
        self.q_parts = dram("q_parts", [B, QUADS, 4, 2, DH, T])
        self.k_parts = dram("k_parts", [B, QUADS, 4, 2, DH, T])
        self.v_parts = dram("v_parts", [B, TT, P, HEADS, 2 * DH])

    def sb(self, name, shape, dt, ctx=None, side="left"):
        return (ctx or self.ctx).enter_context(self.nc.sbuf_tensor(name, shape, dt, side=side))

    def dram(self, name, shape):
        return self.nc.dram_tensor(name, shape, F32, kind="Internal").ap()

    def sem(self, name):
        sem = self.nc.alloc_semaphore(name=name)
        self.sems.append(sem)
        return sem

    def lasting_sem(self, name):
        return self.nc.alloc_semaphore(name=name)

    def recycle(self):
        self.nc.clear_and_free_semaphores(self.sems)
        self.nc.all_engine_barrier()
        self.sems = []


def setup(k, heads, x, cT, wmod0, wmod1):
    nc = k.nc
    COL_PARTS = ((GA, SB, CB, GB),) * 2
    ROW_PARTS = ((0, SA, CA), (1, SA, CA), (1, GA))
    with ExitStack() as c:
        cs = k.sb("cs", [P, 2, DM, B], F32, c)
        scT = k.sb("scT", [P, 2, DM, B], F32, c)
        wm = k.sb("wm", [P, 2, DM, 6 * D], F32, c)
        row = k.sb("row", [B, 3, 2 * D], F32, c)
        split = k.sb("row_split", [2 * GROW, 3, 2 * D], F32R, c)
        ones = k.sb("pick_ones", [2 * GROW, B, P], F32, c)
        pick = k.sb("pick", [2 * GROW, B, P], F32R, c)
        sgn = k.sb("sgn", [P, D], F32, c)
        mag = k.sb("mag", [P, D], F32, c)
        x_in, c_in, w_in = k.sem("x_in"), k.sem("c_in"), [k.sem(f"wm_in{i}") for i in range(2)]
        silu_done, cols_ready, row_ready = k.sem("silu_done"), k.sem("cols_ready"), k.sem("row_ready")
        split_zeroed, ones_done, pick_done, row_split, spread = k.sem("split_zeroed"), k.sem("ones_done"), k.sem("pick_done"), k.sem("row_split_done"), k.sem("spread")
        taken, pool_own, dve_own = [k.sem(f"rows_taken{i}") for i in range(2)], k.sem("setup_pool"), k.sem("setup_dve")
        cols = k.PS[:, 0:2, 0:12 * B].rearrange("p l (j b) -> p l j b", j=12)
        turns = [(i, b) for i in range(3) for b in range(B)]
        block = c.enter_context(nc.Block())

        def take(turn):
            i, b = turns[turn]
            layer, parts = ROW_PARTS[i][0], ROW_PARTS[i][1:]
            return (k.rows[:, layer, parts[0]:parts[0] + len(parts), b, :],
                    k.PS[:, 4 + turn % 4, 0:len(parts) * D].rearrange("p (i d) -> p i d", d=D))

        @block.sync
        def _(sp):
            sp.dma_start(cs[:], cT).then_inc(c_in, 16)
            sp.dma_start(wm[:, 0], wmod0.rearrange("(m p) n -> p m n", p=P)).then_inc(w_in[0], 16)
            sp.dma_start(wm[:, 1], wmod1.rearrange("(m p) n -> p m n", p=P)).then_inc(w_in[1], 16)
            sp.dma_start(k.X[:], x.rearrange("(t p) d -> p t d", p=P)).then_inc(x_in, 16)
            sp.wait_ge(x_in, 16)

        @block.gpsimd
        def _(pool):
            own = Chain(pool, pool_own)
            pool.memset(f32(split[:]), 0.0).then_inc(split_zeroed, 1)
            own.link(pool.memset(ones[:], 0.0))
            own.link(pool.memset(k.ident[:], 0.0))
            own.link(pool.memset(k.maskb[:], 0.0))
            own.link(pool.memset(k.mhalf[:], -0.5))
            own.wait()
            for first in (0, GROW):
                ins = pool.affine_select(out=ones[:], in_=ones[:], compare_op=ALU.not_equal, fill=1.0,
                                         base=-first, pattern=[[-1, B], [0, P]], channel_multiplier=1)
                if first == 0:
                    own.link(ins)
                    own.wait()
            ins.then_inc(ones_done, 1)
            own.link(pool.affine_select(out=k.ident[:], in_=k.ident[:], compare_op=ALU.not_equal, fill=1.0,
                                        base=0, pattern=[[-1, P]], channel_multiplier=1))
            own.link(pool.affine_select(out=k.maskb[:], in_=k.maskb[:], compare_op=ALU.is_ge, fill=MASKED,
                                        base=0, pattern=[[-1, P]], channel_multiplier=1))
            own.wait()
            own.link(pool.tensor_copy(k.identb[:], k.ident[:]))
            own.wait()
            heads.zero(pool)

        @block.scalar
        def _(act):
            act.wait_ge(c_in, 16)
            act.activation(scT[:], cs[:], ACT.Silu).then_inc(silu_done, 1)
            act.wait_ge(ones_done, 1)
            act.activation(pick[:], ones[:], ACT.Copy).then_inc(pick_done, 1)
            for turn in range(0, len(turns), 2):
                act.wait_ge(spread, turn + 1)
                out, src = take(turn)
                act.activation(out, src, ACT.Copy).then_inc(taken[0], 1)

        @block.tensor
        def _(pe):
            def spread_rows(bank):
                pe.wait_ge(row_split, bank + 1)
                for turn, (i, b) in enumerate(turns):
                    if i == bank:
                        if turn >= 4:
                            pe.wait_ge(taken[turn % 2], turn // 2 - 1)
                        w = (len(ROW_PARTS[i]) - 1) * D
                        pe.matmul(k.PS[:, 4 + turn % 4, 0:w], pick[:, b, :], split[:, i, 0:w], start=True, stop=True).then_inc(spread, 1)

            pe.wait_ge(silu_done, 1)
            for l in range(2):
                pe.wait_ge(w_in[l], 16)
                for i, (layer, *parts) in enumerate(ROW_PARTS):
                    if layer == l:
                        for m in range(DM):
                            last = pe.matmul(k.PS[0:B, 1 + i, 0:len(parts) * D], scT[:, l, m, :],
                                             wm[:, l, m, parts[0] * D:(parts[0] + len(parts)) * D], start=(m == 0), stop=(m == DM - 1))
                        last.then_inc(row_ready, 1)
                for part in COL_PARTS[l]:
                    for j in (DM * part, DM * part + 1):
                        for m in range(DM):
                            last = pe.matmul(cols[:, l, j, :], wm[:, l, m, j * P:(j + 1) * P], scT[:, l, m, :],
                                             start=(m == 0), stop=(m == DM - 1))
                last.then_inc(cols_ready, 1)
                if l == 0:
                    pe.wait_ge(pick_done, 1)
                    spread_rows(0)
            spread_rows(1)
            spread_rows(2)

        @block.vector
        def _(dve):
            own = Chain(dve, dve_own)

            def gate(v, s, a):
                own.link(dve.tensor_scalar(s, v, 0.0, 2.0, ALU.is_ge, ALU.mult))
                own.link(dve.scalar_tensor_tensor(out=a, in0=v, scalar=-1.0, in1=v, op0=ALU.mult, op1=ALU.max))
                own.wait()
                own.link(dve.tensor_scalar(s, s, -1.0, None, ALU.add))
                own.wait()
                own.link(dve.scalar_tensor_tensor(out=v, in0=a, scalar=0.25, in1=s, op0=ALU.max, op1=ALU.mult))
                own.wait()

            def columns(l):
                dve.wait_ge(cols_ready, l + 1)
                first, last = COL_PARTS[l][0], COL_PARTS[l][-1]
                v = k.modc[:, l, first:last + 1]
                own.link(dve.tensor_copy(v.rearrange("p c m b -> p (c m b)"),
                                         cols[:, l, DM * first:DM * (last + 1)].rearrange("p j b -> p (j b)")))
                own.wait()
                own.link(dve.tensor_scalar(k.modc[:, l, CB], k.modc[:, l, CB], 1.0, None, ALU.add))
                for part in {GA, GB} & set(COL_PARTS[l]):
                    gate(k.modc[:, l, part], sgn[:, 0:DM * B].rearrange("p (m b) -> p m b", m=DM),
                         mag[:, 0:DM * B].rearrange("p (m b) -> p m b", m=DM))

            def rows(i):
                dve.wait_ge(row_ready, i + 1)
                parts = ROW_PARTS[i][1:]
                for n, part in enumerate(parts):
                    own.link(dve.tensor_scalar(row[:, i, n * D:(n + 1) * D], k.PS[0:B, 1 + i, n * D:(n + 1) * D],
                                               1.0 if part == CA else 0.0, None, ALU.add))
                own.wait()
                w = len(parts) * D
                if GA in parts:
                    gate(row[:, i, 0:w], sgn[0:B, 0:w], mag[0:B, 0:w])
                own.link(dve.tensor_copy(split[0:B, i, 0:w], row[:, i, 0:w]))
                own.wait()
                dve.tensor_tensor(split[GROW:GROW + B, i, 0:w], row[:, i, 0:w], f32(split[0:B, i, 0:w]),
                                  ALU.subtract).then_inc(row_split, 1)

            def take_rows(i):
                for turn in range(1 + B * i, B * (i + 1), 2):
                    dve.wait_ge(spread, turn + 1)
                    out, src = take(turn)
                    dve.tensor_copy(out, src).then_inc(taken[1], 1)
            dve.wait_ge(split_zeroed, 1)
            rows(0)
            take_rows(0)
            columns(0)
            rows(1)
            rows(2)
            take_rows(1)
            take_rows(2)
            columns(1)


def row_stats(own, dve, src, stats, mv):
    for t in range(TT):
        own.link(dve.bn_stats(stats[:, t, :], src(t)))
    own.wait()
    for t in range(TT):
        own.link(dve.bn_aggr(mv[:, t, :], stats[:, t, :]))
    own.wait()


def attention_inputs(k, heads, w, ln_gb, bqk, bv_row):
    nc = k.nc
    with ExitStack() as c:
        qhi = k.sb("qhi", [P, 4, T], F32R, c)
        qlo = k.sb("qlo", [P, 4, T], F32R, c)
        vp = k.sb("vp", [P, TT, HEADS, 2, DH], F32R, c)
        wst = k.sb("wst", [P, 3, DM, D], F32, c)
        whi = k.sb("whi", [P, 3, DM, D], F32R, c)
        wlo = k.sb("wlo", [P, 3, DM, D], F32R, c)
        gb = k.sb("gb", [P, 2, DM], F32, c)
        bq = k.sb("bq", [P, 2, DM], F32, c)
        bv = k.sb("bv", [P, D], F32, c)
        stats = k.sb("stats", [P, 2, TT, 6], F32, c)
        mv = k.sb("mv", [P, 2, TT, 2], F32, c)
        var = k.sb("var", [P, 2, TT], F32, c)
        rs = k.sb("rs", [P, 2, TT], F32, c)
        xh = k.sb("xh", [P, TT, D], F32, c)
        h = k.sb("h", [P, TT, D], F32, c)
        hn = k.sb("hn", [P, TT, D], F32, c)
        hf = k.sb("hf", [P, DM, T], F32, c)
        hhi = k.sb("hhi", [P, 2, DM, T], F32R, c)
        hlo = k.sb("hlo", [P, 2, DM, T], F32R, c)
        qf = k.sb("qf", [P, 4, T], F32, c)
        vf = k.sb("vf", [P, TT, D], F32, c)
        S = lambda n: k.sem("a1_" + n)
        par_in, w_in, w_hi, w_lo, own_dve, bq_done = S("par_in"), S("w_in"), S("w_hi"), S("w_lo"), S("dve"), S("bq_done")
        var_ready, root_done = ([S(f"{n}{i}") for i in range(2)] for n in ("var_ready", "root_done"))
        hn_ready, hT_ready, h_done, hlo_done = S("hn_ready"), S("hT_ready"), S("h_done"), S("hlo_done")
        q_ready, q_done, qlo_done = S("q_ready"), S("q_done"), S("qlo_done")
        v_ready, vf_done, vhi_done, vlo_done = S("v_ready"), S("vf_done"), S("vhi_done"), S("vlo_done")
        q_out, v_out = heads.q_out, heads.v_out
        block = c.enter_context(nc.Block())

        @block.sync
        def _(sp):
            for i in range(3):
                sp.dma_start(wst[:, i], w[i].rearrange("(m p) n -> p m n", p=P)).then_inc(w_in, 16)
            sp.dma_start(gb[:], ln_gb).then_inc(par_in, 16)
            sp.dma_start(bq[:], bqk).then_inc(par_in, 16)
            sp.dma_start(bv[:], bv_row.partition_broadcast(P)).then_inc(par_in, 16)

            def store(b):
                for j in range(4):
                    sp.wait_ge(q_done, (b * 4 + j + 1) * 2)
                    sp.wait_ge(qlo_done, b * 4 + j + 1)
                    dst = (k.q_parts, k.k_parts)[j // 2]
                    for part, tile in enumerate((qhi, qlo)):
                        sp.dma_start(dst[b, 2 * (j % 2):2 * (j % 2) + 2, :, part].rearrange("q s r t -> (q s) r t"),
                                     f32(tile[:, j, :])).then_inc(q_out[j], 16)
                sp.wait_ge(vhi_done, (b + 1) * 2)
                sp.wait_ge(vlo_done, (b + 1) * 2)
                sp.dma_start(k.v_parts[b].rearrange("t p h d -> p t (h d)"),
                             f32(vp[:].rearrange("p t h a d -> p t (h a d)"))).then_inc(v_out, 16)

            sp.wait_ge(heads.zeroed, 4)
            for b in range(B):
                store(b)
                if b == 1:
                    heads.wait_stored(sp, 0)
                    heads.load_keys(sp, 0, 0, 0)

        @block.gpsimd
        def _(pool):
            def root(i):
                def stage(b):
                    pool.wait_ge(var_ready[i], b + 1)
                    pool.tensor_tensor(rs[:, i], var[:, i], k.mhalf[:, 0:TT], ALU.pow).then_inc(root_done[i], 1)
                return stage
            def queries(j):
                def stage(b):
                    if b:
                        pool.wait_ge(q_out[j], b * 32)
                    pool.wait_ge(q_done, (b * 4 + j + 1) * 2)
                    pool.tensor_tensor(qlo[:, j, :], qf[:, j, :], f32(qhi[:, j, :]), ALU.subtract).then_inc(qlo_done, 1)
                return stage

            def values_lo(b):
                for g in range(2):
                    pool.wait_ge(vhi_done, b * 2 + g + 1)
                    for t in (2 * g, 2 * g + 1):
                        last = pool.tensor_tensor(vp[:, t, :, 1, :], vf[:, t, :].rearrange("p (h d) -> p h d", d=DH),
                                                 f32(vp[:, t, :, 0, :]), ALU.subtract)
                    last.then_inc(vlo_done, 1)
            wavefront((0, root(0)), (1, queries(0)), (1, queries(1)), (0, root(1)), (1, queries(2)), (1, queries(3)), (1, values_lo))

        @block.scalar
        def _(act):
            act.wait_ge(w_in, 48)
            act.activation(whi[:], wst[:], ACT.Copy).then_inc(w_hi, 1)
            act.wait_ge(par_in, 48)
            act.mul(bq[:, 0], bq[:, 0], 0.25).then_inc(bq_done, 1)
            act.wait_ge(bq_done, 1)

            def columns(b):
                if b:
                    act.wait_ge(hlo_done, b * DM)
                if b >= 2:
                    act.wait_ge(v_ready, (b - 1) * 2)
                for m in range(DM):
                    act.wait_ge(hT_ready, b * DM + m + 1)
                    for out in (hf[:, m, :], hhi[:, b % 2, m, :]):
                        act.activation(out, k.PS[:, m, :], ACT.Identity, scale=gb[:, 0, m:m + 1],
                                       bias=gb[:, 1, m:m + 1]).then_inc(h_done, 1)

            def queries(j):
                def stage(b):
                    act.wait_ge(q_ready, b * 4 + j + 1)
                    if b:
                        act.wait_ge(q_out[j], b * 32)
                    for out in (qf[:, j, :], qhi[:, j, :]):
                        act.activation(out, k.PS[:, 2 + j, :], ACT.Identity, scale=(0.25 if j < 2 else 1.0),
                                       bias=bq[:, j // 2, j % 2:j % 2 + 1]).then_inc(q_done, 1)
                return stage

            def values(b):
                if b:
                    act.wait_ge(v_out, b * 16)
                for g in range(2):
                    act.wait_ge(vf_done, b * 2 + g + 1)
                    for t in (2 * g, 2 * g + 1):
                        last = act.activation(vp[:, t, :, 0, :], vf[:, t, :].rearrange("p (h d) -> p h d", d=DH), ACT.Copy)
                    last.then_inc(vhi_done, 1)
            wavefront((1, queries(0)), (1, queries(1)), (1, queries(2)), (1, queries(3)), (0, columns), (1, values))

        @block.vector
        def _(dve):
            own = Chain(dve, own_dve)

            def first_stats(b):
                row_stats(own, dve, lambda t: k.X[:, b * TT + t, :], stats[:, 0], mv[:, 0])
                dve.tensor_scalar(var[:, 0], mv[:, 0, :, 1], EPS, None, ALU.add).then_inc(var_ready[0], 1)

            def second_stats(b):
                dve.wait_ge(root_done[0], b + 1)
                for t in range(TT):
                    own.link(dve.tensor_scalar(xh[:, t, :], k.X[:, b * TT + t, :], mv[:, 0, t, 0:1], rs[:, 0, t:t + 1],
                                               ALU.subtract, ALU.mult))
                own.wait()
                row = lambda part: k.rows[:, 0, part, b, :].unsqueeze(1).to_broadcast([P, TT, D])
                own.link(dve.tensor_tensor(h[:], xh[:], row(CA), ALU.mult))
                own.wait()
                own.link(dve.tensor_tensor(h[:], h[:], row(SA), ALU.add))
                own.wait()
                row_stats(own, dve, lambda t: h[:, t, :], stats[:, 1], mv[:, 1])
                dve.tensor_scalar(var[:, 1], mv[:, 1, :, 1], EPS, None, ALU.add).then_inc(var_ready[1], 1)
                if b == 0:
                    dve.wait_ge(w_hi, 1)
                    dve.tensor_tensor(wlo[:], wst[:], f32(whi[:]), ALU.subtract).then_inc(w_lo, 1)
                    dve.wait_ge(par_in, 48)

            def norm(b):
                dve.wait_ge(root_done[1], b + 1)
                if b:
                    dve.wait_ge(hT_ready, b * DM)
                for t in range(TT):
                    dve.tensor_scalar(hn[:, t, :], h[:, t, :], mv[:, 1, t, 0:1], rs[:, 1, t:t + 1],
                                      ALU.subtract, ALU.mult).then_inc(hn_ready, 1)

            def lo(b):
                if b >= 2:
                    dve.wait_ge(v_ready, (b - 1) * 2)
                for m in range(DM):
                    dve.wait_ge(h_done, (b * DM + m + 1) * 2)
                    dve.tensor_tensor(hlo[:, b % 2, m, :], hf[:, m, :], f32(hhi[:, b % 2, m, :]), ALU.subtract).then_inc(hlo_done, 1)

            def values(b):
                if b:
                    dve.wait_ge(vhi_done, b * 2)
                    dve.wait_ge(vlo_done, b * 2)
                for g in range(2):
                    dve.wait_ge(v_ready, b * 2 + g + 1)
                    dve.tensor_tensor(vf[:, 2 * g:2 * g + 2, :], k.PS[:, 6 + g, :].rearrange("p (t d) -> p t d", t=2),
                                      bv[:].unsqueeze(1).to_broadcast([P, 2, D]), ALU.add).then_inc(vf_done, 1)

            wavefront((0, first_stats), (0, second_stats), (0, norm), (1, values), (0, lo))

        @block.tensor
        def _(pe):
            def columns(b):
                if b:
                    pe.wait_ge(h_done, b * DM * 2)
                for m in range(DM):
                    for t in range(TT):
                        pe.wait_ge(hn_ready, b * TT + t + 1)
                        last = pe.transpose(k.PS[:, m, t * P:(t + 1) * P], hn[:, t, m * P:(m + 1) * P], k.ident[:])
                    last.then_inc(hT_ready, 1)

            def queries(b):
                pe.wait_ge(hlo_done, (b + 1) * DM)
                for j in range(4):
                    if b:
                        pe.wait_ge(q_done, ((b - 1) * 4 + j + 1) * 2)
                    i, m = j // 2, j % 2
                    for d in range(DM):
                        last = split3(pe, k.PS[:, 2 + j, :], whi[:, i, d, m * P:(m + 1) * P], wlo[:, i, d, m * P:(m + 1) * P],
                                      hhi[:, b % 2, d, :], hlo[:, b % 2, d, :], d == 0, d == DM - 1)
                    last.then_inc(q_ready, 1)

            def values(b):
                if b:
                    pe.wait_ge(vf_done, b * 2)
                for g in range(2):
                    for t in (2 * g, 2 * g + 1):
                        out = k.PS[:, 6 + g, (t % 2) * D:(t % 2 + 1) * D]
                        for d in range(DM):
                            last = split3(pe, out, hhi[:, b % 2, d, t * P:(t + 1) * P], hlo[:, b % 2, d, t * P:(t + 1) * P],
                                          whi[:, 2, d, :], wlo[:, 2, d, :], d == 0, d == DM - 1)
                    last.then_inc(v_ready, 1)
            pe.wait_ge(w_lo, 1)
            wavefront((1, queries), (0, columns), (1, values))


PT_AT = (0, 4 * P, 8 * P, 7 * P)
PT_BANKS = ((0, 4 * P), (4 * P, 4 * P), (8 * P, 2 * P))


class Heads:

    def __init__(self, k, c):
        self.k = k
        self.Q4 = [k.sb(f"Q4_{u}", [P, 2, T], F32R, c, "right") for u in range(2)]
        self.K4 = [k.sb(f"K4_{u}", [P, 4, T], F32R, c, "right") for u in range(2)]
        self.V4 = [k.sb(f"V4_{u}", [P, TT, 4, P], F32R, c, "right") for u in range(2)]
        self.zeroed = k.sem("zeroed")
        self.k_in, self.q_in, self.v_in = ([k.sem(f"{n}_in{u}") for u in range(2)] for n in "kqv")

        self.q_out, self.v_out = [k.sem(f"q_out{j}") for j in range(4)], k.sem("v_out")

    def wait_stored(self, eng, b):
        for j in range(4):
            eng.wait_ge(self.q_out[j], (b + 1) * 32)
        eng.wait_ge(self.v_out, (b + 1) * 16)

    def zero(self, pool):
        for u in range(2):
            pool.memset(f32(self.K4[u][:]), 0.0).then_inc(self.zeroed, 1)
            pool.memset(f32(self.V4[u][:]), 0.0).then_inc(self.zeroed, 1)

    def load_keys(self, sp, b, q, u):
        for s in range(4):
            r = 64 * (s % 2)
            src = self.k.k_parts[b, q, s].rearrange("a r t -> (a r) t")
            for dup in range(2):
                sp.dma_start(f32(self.K4[u][r + 32 * dup:r + 32 * dup + 32, s, :]), src).then_inc(self.k_in[u], 16)
            src = self.k.q_parts[b, q, s]
            sp.dma_start(f32(self.Q4[u][r:r + 32, s // 2, :]), src.rearrange("a r t -> (a r) t")).then_inc(self.q_in[u], 16)
            for dup in range(2):
                sp.dma_start(f32(self.Q4[u][r + 32 + 16 * dup:r + 48 + 16 * dup, s // 2, :]), src[1 - dup]).then_inc(self.q_in[u], 16)

    def load_values(self, sp, b, q, u):
        for s in range(4):
            sp.dma_start(f32(self.V4[u][:, :, s, 32 * s:32 * s + 32]),
                         self.k.v_parts[b].rearrange("t p h d -> p t h d")[:, :, q * 4 + s, :]).then_inc(self.v_in[u], 16)


class OutputWeights:

    def __init__(self, k, c):
        self.st, self.w_in = k.sb("wo_st", [P, QUADS, D], F32, c), k.sem("wo_in")

    def load(self, sp, wo):
        for dup in range(2):
            for h in range(4):
                sp.dma_start(self.st[32 * h + 16 * dup:32 * h + 16 * dup + 16],
                             wo.rearrange("(q h r) n -> h r q n", q=QUADS, h=4)[h]).then_inc(self.w_in, 16)


def attention(k, heads, OT, out_weights, wo):
    nc = k.nc
    NQ = B * QUADS
    with ExitStack() as c:
        Q4, K4, V4, k_in, q_in, v_in = heads.Q4, heads.K4, heads.V4, heads.k_in, heads.q_in, heads.v_in
        PR = k.sb("PR", [P, 4, TT, T], F32, c)
        PThi = k.sb("PThi", [P, 2, 10 * P], F32R, c)
        PTlo = k.sb("PTlo", [P, 2, 10 * P], F32R, c)
        nmax = k.sb("nmax", [P, 4, TT], F32, c)
        rsum = k.sb("rsum", [P, 4, TT], F32, c)
        rinv = k.sb("rinv", [P, 4, TT], F32, c)
        carry = k.sb("carry", [P, 8], F32, c)
        S = lambda n: k.sem("a2_" + n)
        s_ready, max_done, exp_done, inv_done, norm_done = S("s_ready"), S("max_done"), S("exp_done"), S("inv_done"), S("norm_done")
        t_ready, hi_done, lo_done, av_done, o_hi, o_lo = S("t_ready"), S("hi_done"), S("lo_done"), S("av_done"), S("o_hi"), S("o_lo")
        O = k.PS[:, 7, :]
        block = c.enter_context(nc.Block())
        INV, TRANS, LO, VALUES = 1, 2, 3, 4
        ITERS = NQ // 2

        @block.sync
        def _(sp):
            heads.load_keys(sp, 0, 1, 1)
            for u in range(2):
                heads.load_values(sp, 0, u, u)

            def pair(it, b, qp):
                for u in range(2):
                    sp.wait_ge(s_ready, it * 32 - 16 + 16 * u)
                    heads.load_keys(sp, b, qp * 2 + u, u)
                for u in range(2):
                    sp.wait_ge(av_done, it * 8 - 4 + 4 * u)
                    heads.load_values(sp, b, qp * 2 + u, u)
            pair(1, 0, 1)
            heads.wait_stored(sp, B - 1)
            out_weights.load(sp, wo)
            with sp.Fori(1, B) as b:
                pair(b * 2, b, 0)
                pair(b * 2 + 1, b, 1)

        @block.gpsimd
        def _(pool):
            with pool.Fori(0, ITERS) as it:
                for e in range(8):
                    pool.wait_ge(inv_done, it * 8 + e + 1)
                    pool.tensor_tensor(carry[:, e:e + 1], rinv[:, e % 4, 0:1], rinv[:, e % 4, 0:1], ALU.mult)
                    for i in range(TT):
                        w = P * (i + 1)
                        pool.tensor_scalar(PR[:, e % 4, i, 0:w], PR[:, e % 4, i, 0:w], rinv[:, e % 4, i:i + 1], 1.0,
                                           ALU.mult, ALU.mult).then_inc(norm_done, 1)

        def loop(eng, body):
            body(0, lambda e, lag: e >= lag)
            with eng.Fori(1, ITERS) as it:
                body(it, lambda e, lag: True)
            body(ITERS, lambda e, lag: e < lag)

        @block.tensor
        def _(pe):
            def body(it, on):
                for e in range(8):
                    h = it * 8 + e

                    def scores(i):
                        u, s = e // 4, e % 4
                        if s == 0 and i == 0:
                            pe.wait_ge(k_in[u], it * 128 + 128)
                            pe.wait_ge(q_in[u], it * 192 + 192)
                        w = P * (i + 1)
                        wait(pe, exp_done, (h - 1) * TT + i + 1)
                        pe.matmul(k.PS[:, i, 0:w], Q4[u][:, s // 2, P * i:P * i + P], K4[u][:, s, 0:w], start=True, stop=False)
                        pe.matmul(k.PS[:, i, w - P:w], k.identb[:], k.maskb[:], start=False, stop=True).then_inc(s_ready, 1)

                    def transposes(bank):
                        g = h - TRANS
                        if bank == 0:
                            pe.wait_ge(norm_done, (g + 1) * TT)
                        if not (isinstance(g, int) and g == 0):
                            pe.wait_ge(lo_done, (g - 1) * 3 + bank + 1)
                        for j in ((0,), (1, 3), (2,))[bank]:
                            for i in range(j, TT):
                                at = PT_AT[j] + P * (i - j)
                                ins = pe.transpose(k.PS[:, 4 + bank, at % 512:at % 512 + P],
                                                   PR[:, (e - TRANS) % 4, i, P * j:P * j + P], k.ident[:])
                        ins.then_inc(t_ready, 1)

                    def values():
                        g, ge = h - VALUES, (e - VALUES) % 8
                        u, s = ge // 4, ge % 4
                        if s == 0:
                            past = 0 if e >= VALUES else 1
                            pe.wait_ge(v_in[u], (it - past) * 64 + 64)
                            wait(pe, o_lo, (it - past) * 2 + u)
                        pe.wait_ge(lo_done, (g + 1) * 3)
                        for j in (0, 1, 3, 2):
                            w = T - P * j
                            for part, pt in enumerate((PThi, PTlo)):
                                ins = pe.matmul(O[:, P * j:T], V4[u][:, j, s, :], pt[:, ge % 2, PT_AT[j]:PT_AT[j] + w],
                                                start=(s == 0 and j == 0 and part == 0), stop=(s == 3 and j == 2 and part == 1))
                        ins.then_inc(av_done, 1)

                    if on(e, 0):
                        for i in range(TT - 1):
                            scores(i)
                    if on(e, VALUES):
                        values()
                    if on(e, 0):
                        scores(TT - 1)
                    if on(e, TRANS):
                        for bank in range(3):
                            transposes(bank)
            loop(pe, body)

        @block.scalar
        def _(act):
            def body(it, on):
                for e in range(8):
                    h = it * 8 + e

                    def exponential(i):
                        if i == 0:
                            wait(act, t_ready, (h - 4) * 3 + 3)
                        w = P * (i + 1)
                        act.wait_ge(max_done, h * TT + i + 1)
                        act.activation(PR[:, e % 4, i, 0:w], k.PS[:, i, 0:w], ACT.Exp, bias=nmax[:, e % 4, i:i + 1],
                                       accum_out=rsum[:, e % 4, i:i + 1]).then_inc(exp_done, 1)

                    def hi(n):
                        g = h - TRANS
                        at, w = PT_BANKS[n]
                        if n == 0:
                            wait(act, av_done, g - 1)
                        act.wait_ge(t_ready, g * 3 + n + 1)
                        act.activation(PThi[:, e % 2, at:at + w], k.PS[:, 4 + n, 0:w], ACT.Copy).then_inc(hi_done, 1)

                    if on(e, 0):
                        for i in range(TT - 2):
                            exponential(i)
                    if on(e, VALUES) and (e - VALUES) % 4 == 3:
                        q = it * 2 + (0 if e == 7 else -1)
                        act.wait_ge(av_done, (q + 1) * 4)
                        if isinstance(q, int) and q == 0:
                            heads.wait_stored(act, B - 1)
                        act.activation(OT[0][:, q, :], O, ACT.Copy).then_inc(o_hi, 1)
                    if on(e, 0):
                        exponential(TT - 2)
                    if on(e, TRANS):
                        hi(0)
                    if on(e, 0):
                        exponential(TT - 1)
                    if on(e, TRANS):
                        hi(1)
                        hi(2)
            loop(act, body)

        @block.vector
        def _(dve):
            def body(it, on):
                for e in range(8):
                    h = it * 8 + e

                    def maximum(i):
                        dve.wait_ge(s_ready, h * TT + i + 1)
                        dve.tensor_reduce(nmax[:, e % 4, i:i + 1], k.PS[:, i, 0:P * (i + 1)], AX_X, ALU.max, negate=True).then_inc(max_done, 1)

                    def lo(n):
                        g = h - LO
                        at, w = PT_BANKS[n]
                        if n == 0:
                            wait(dve, av_done, g - 1)
                        dve.wait_ge(hi_done, g * 3 + n + 1)
                        dve.tensor_tensor(PTlo[:, (e - LO) % 2, at:at + w], k.PS[:, 4 + n, 0:w], f32(PThi[:, (e - LO) % 2, at:at + w]),
                                          ALU.subtract).then_inc(lo_done, 1)

                    if on(e, 0):
                        for i in range(TT - 1):
                            maximum(i)
                    if on(e, LO):
                        lo(0)
                        lo(1)
                        lo(2)
                    if on(e, INV):
                        g = h - INV
                        dve.wait_ge(exp_done, (g + 1) * TT)
                        wait(dve, norm_done, (g - 3) * TT)
                        dve.reciprocal(rinv[:, (e - INV) % 4, :], rsum[:, (e - INV) % 4, :]).then_inc(inv_done, 1)
                    if on(e, VALUES) and (e - VALUES) % 4 == 3:
                        q = it * 2 + (0 if e == 7 else -1)
                        dve.wait_ge(o_hi, q + 1)
                        dve.tensor_tensor(OT[1][:, q, :], O, f32(OT[0][:, q, :]), ALU.subtract).then_inc(o_lo, 1)
                    if on(e, 0):
                        maximum(TT - 1)
            loop(dve, body)


class Route:

    def __init__(self, k, layer, hT, combT, experts, topk, lanes, banks, c):
        n = lambda s: f"r{layer}_{s}"
        sb = lambda name, shape, dt=F32: k.sb(n(name), [P] + shape, dt, c)
        self.lanes, self.banks = lanes, banks
        self.k, self.layer, self.hT, self.combT, self.E, self.topk = k, layer, hT, combT, experts, topk
        self.gst, self.ghi, self.glo = sb("gst", [DM, P]), sb("ghi", [DM, P], F32R), sb("glo", [DM, P], F32R)
        self.stats, self.mv = sb("stats", [B, TT, 6]), sb("mv", [B, TT, 2])
        self.var, self.rs = sb("var", [B, TT]), sb("rs", [B, TT])
        self.xh, self.hf, self.lg = sb("xh", [lanes, TT, D]), sb("hf", [lanes, DM, T]), sb("lg", [lanes, T])
        self.mx, self.sm, self.ex = sb("mx", [B, TT]), sb("sm", [B, TT]), sb("ex", [B, TT, experts])
        cand = max(experts + 8 - topk, 8)
        self.cand, self.rep, self.top = sb("cand", [B, TT, cand]), sb("rep", [B, TT, cand]), sb("top", [B, TT, 8])
        self.comb = sb("comb", [B, TT, GROW])
        self.cf = k.sb(n("cf"), [GROW, lanes, T], F32, c)
        S = lambda s: k.sem(n(s))
        self.g_in, self.g_split, self.own_dve, self.zeroed = S("g_in"), S("g_split"), S("dve"), S("zeroed")
        self.var_ready, self.root_done, self.xh_ready, self.xT_ready = S("var_ready"), S("root_done"), S("xh_ready"), S("xT_ready")
        self.hf_done, self.lo_done = S("hf_done"), S("lo_done")
        self.lT_ready, self.lg_done, self.l_ready = S("lT_ready"), S("lg_done"), S("l_ready")
        self.d_ready, self.ex_done, self.comb_done = S("d_ready"), S("ex_done"), S("comb_done")
        self.cT_ready, self.cf_done, self.clo_done = S("cT_ready"), S("cf_done"), S("clo_done")

    def load(self, sp, gate_w):
        sp.dma_start(self.gst[:], gate_w).then_inc(self.g_in, 16)

    def fill(self, pool):
        pool.memset(f32(self.combT[:]), 0.0).then_inc(self.zeroed, 1)
        pool.memset(self.cand[:], 2.0).then_inc(self.zeroed, 1)
        pool.memset(self.comb[:], 0.0).then_inc(self.zeroed, 1)
        pool.wait_ge(self.zeroed, 3)
        pool.memset(self.comb[:, :, :, ONE:ONE + 1], 1.0).then_inc(self.zeroed, 1)

    def root(self, pool, b):
        pool.wait_ge(self.var_ready, b + 1)
        pool.tensor_tensor(self.rs[:, b], self.var[:, b], self.k.mhalf[:, 0:TT], ALU.pow).then_inc(self.root_done, 1)

    def act_gate(self, act):
        act.wait_ge(self.g_in, 16)
        act.activation(self.ghi[:], self.gst[:], ACT.Copy).then_inc(self.g_split, 1)
        act.wait_ge(self.zeroed, 4)

    def act_columns(self, act, b):
        modc = self.k.modc
        for m in range(DM):
            act.wait_ge(self.xT_ready, b * DM + m + 1)
            if b >= self.lanes:
                act.wait_ge(self.lo_done, (b - self.lanes + 1) * DM)
            for out in (self.hf[:, b % self.lanes, m, :], self.hT[0][:, m, b * T:(b + 1) * T]):
                act.activation(out, self.k.PS[:, self.banks(b) + m, :], ACT.Identity, scale=modc[:, self.layer, CB, m, b:b + 1],
                               bias=modc[:, self.layer, SB, m, b:b + 1]).then_inc(self.hf_done, 1)

    def act_logits(self, act, b):
        act.wait_ge(self.lT_ready, b + 1)
        if b >= self.lanes:
            act.wait_ge(self.l_ready, b - self.lanes + 1)
        act.activation(self.lg[:, b % self.lanes], self.k.PS[:, self.banks(b), :], ACT.Copy).then_inc(self.lg_done, 1)

    def act_exp(self, act, b):
        act.wait_ge(self.d_ready, b + 1)
        act.activation(self.ex[:, b], self.ex[:, b], ACT.Exp).then_inc(self.ex_done, 1)

    def act_weights(self, act, b):
        act.wait_ge(self.cT_ready, b + 1)
        if b >= self.lanes:
            act.wait_ge(self.clo_done, b - self.lanes + 1)
        for out in (self.cf[:, b % self.lanes], self.combT[0:GROW, b * T:(b + 1) * T]):
            act.activation(out, self.k.PS[0:GROW, self.banks(b), :], ACT.Copy).then_inc(self.cf_done, 1)

    def dve_gate(self, dve):
        dve.wait_ge(self.g_split, 1)
        dve.tensor_tensor(self.glo[:], self.gst[:], f32(self.ghi[:]), ALU.subtract).then_inc(self.g_split, 1)
        dve.wait_ge(self.zeroed, 4)
        self.own = Chain(dve, self.own_dve)

    def dve_stats(self, dve, b):
        row_stats(self.own, dve, lambda t: self.k.X[:, b * TT + t, :], self.stats[:, b], self.mv[:, b])
        dve.tensor_scalar(self.var[:, b], self.mv[:, b, :, 1], EPS, None, ALU.add).then_inc(self.var_ready, 1)

    def dve_norm(self, dve, b):
        dve.wait_ge(self.root_done, b + 1)
        if b >= self.lanes:
            dve.wait_ge(self.xT_ready, (b - self.lanes + 1) * DM)
        for t in range(TT):
            dve.tensor_scalar(self.xh[:, b % self.lanes, t, :], self.k.X[:, b * TT + t, :], self.mv[:, b, t, 0:1], self.rs[:, b, t:t + 1],
                              ALU.subtract, ALU.mult).then_inc(self.xh_ready, 1)

    def dve_lo(self, dve, b):
        for m in range(DM):
            dve.wait_ge(self.hf_done, (b * DM + m + 1) * 2)
            cols = slice(b * T, (b + 1) * T)
            dve.tensor_tensor(self.hT[1][:, m, cols], self.hf[:, b % self.lanes, m, :], f32(self.hT[0][:, m, cols]),
                              ALU.subtract).then_inc(self.lo_done, 1)

    def dve_center(self, dve, b):
        own = self.own
        logits = self.k.PS[:, self.banks(b) + 1, :].rearrange("p (t e) -> p t e", e=P)[:, :, 0:self.E]
        dve.wait_ge(self.l_ready, b + 1)
        own.link(dve.tensor_reduce(self.mx[:, b], logits, AX_X, ALU.max))
        own.wait()
        dve.tensor_tensor(self.ex[:, b], logits, self.mx[:, b].unsqueeze(2).to_broadcast([P, TT, self.E]),
                          ALU.subtract).then_inc(self.d_ready, 1)

    def dve_choose(self, dve, b):
        own, E, topk = self.own, self.E, self.topk
        cand, rep, comb = self.cand[:, b], self.rep[:, b], self.comb[:, b]
        dve.wait_ge(self.ex_done, b + 1)
        own.link(dve.tensor_reduce(self.sm[:, b], self.ex[:, b], AX_X, ALU.add))
        own.wait()
        own.link(dve.reciprocal(self.sm[:, b], self.sm[:, b]))
        own.wait()
        pr = cand[:, :, 0:E]
        own.link(dve.tensor_tensor(pr, self.ex[:, b], self.sm[:, b].unsqueeze(2).to_broadcast([P, TT, E]), ALU.mult))
        own.wait()
        if topk > 1:
            for t in range(TT):
                own.link(dve.max(self.top[:, b, t, :], cand[:, t, 0:E]))
            own.wait()
            own.link(dve.memset(self.top[:, b, :, topk:8], 2.0))
            own.wait()
            for t in range(TT):
                own.link(dve.match_replace(out=rep[:, t, :], in_to_replace=self.top[:, b, t, :], in_values=cand[:, t, :],
                                           imm_value=-1.0))
            own.wait()
            dve.scalar_tensor_tensor(out=comb[:, :, 0:E], in0=rep[:, :, 0:E], scalar=0.0, in1=pr,
                                     op0=ALU.is_lt, op1=ALU.mult).then_inc(self.comb_done, 1)
        else:
            own.link(dve.tensor_tensor(rep[:, :, 0], cand[:, :, 0], cand[:, :, 1], ALU.is_ge))
            own.link(dve.tensor_tensor(rep[:, :, 1], cand[:, :, 1], cand[:, :, 0], ALU.is_gt))
            own.wait()
            dve.tensor_tensor(comb[:, :, 0:E], rep[:, :, 0:E], pr, ALU.mult).then_inc(self.comb_done, 1)

    def dve_weights_lo(self, dve, b):
        dve.wait_ge(self.cf_done, 2 * b + 2)
        cols = slice(b * T, (b + 1) * T)
        dve.tensor_tensor(self.combT[GROW:2 * GROW, cols], self.cf[:, b % self.lanes], f32(self.combT[0:GROW, cols]),
                          ALU.subtract).then_inc(self.clo_done, 1)

    def pe_columns(self, pe, b):
        for m in range(DM):
            for t in range(TT):
                pe.wait_ge(self.xh_ready, b * TT + t + 1)
                last = pe.transpose(self.k.PS[:, self.banks(b) + m, t * P:(t + 1) * P], self.xh[:, b % self.lanes, t, m * P:(m + 1) * P], self.k.ident[:])
            last.then_inc(self.xT_ready, 1)

    def pe_logits(self, pe, b):
        pe.wait_ge(self.g_split, 2)
        pe.wait_ge(self.lo_done, (b + 1) * DM)
        cols = slice(b * T, (b + 1) * T)
        for d in range(DM):
            last = split3(pe, self.k.PS[:, self.banks(b), :], self.ghi[:, d, :], self.glo[:, d, :], self.hT[0][:, d, cols],
                          self.hT[1][:, d, cols], d == 0, d == DM - 1)
        last.then_inc(self.lT_ready, 1)

    def pe_rows(self, pe, b):
        pe.wait_ge(self.lg_done, b + 1)
        for t in range(TT):
            last = pe.transpose(self.k.PS[:, self.banks(b) + 1, t * P:(t + 1) * P], self.lg[:, b % self.lanes, t * P:(t + 1) * P], self.k.ident[:])
        last.then_inc(self.l_ready, 1)

    def pe_weights(self, pe, b):
        pe.wait_ge(self.comb_done, b + 1)
        for t in range(TT):
            last = pe.transpose(self.k.PS[0:GROW, self.banks(b), t * P:(t + 1) * P], self.comb[:, b, t, :], self.k.ident[:])
        last.then_inc(self.cT_ready, 1)


def attention_output_and_route(k, OT, out_weights, bo_col, hT, combT, gate_w, expert_weights, w):
    nc = k.nc
    with ExitStack() as c:
        wst = out_weights.st
        whi = k.sb("wo_hi", [P, QUADS, D], F32R, c)
        wlo = k.sb("wo_lo", [P, QUADS, D], F32R, c)
        bo = k.sb("bo", [P, DM], F32, c)
        gabo = k.sb("gabo", [P, DM, B], F32, c)
        yf = k.sb("yf", [P, 2, DM, T], F32, c)
        S = lambda n: k.sem("a3_" + n)
        b_in, w_split, b_done = S("b_in"), S("w_split"), S("b_done")
        y_ready, yf_done, yT_ready, x_done = S("y_ready"), S("yf_done"), S("yT_ready"), S("x_done")
        r = Route(k, 0, hT, combT, L0_EXPERTS, L0_TOPK, 2, lambda b: 2 * b, c)
        block = c.enter_context(nc.Block())

        @block.sync
        def _(sp):
            sp.dma_start(bo[:], bo_col).then_inc(b_in, 16)
            r.load(sp, gate_w)
            for tile in range(2):
                expert_weights.load(sp, w, tile, tile)

        @block.gpsimd
        def _(pool):
            r.fill(pool)
            wavefront((0, lambda b: r.root(pool, b)))

        @block.scalar
        def _(act):
            act.wait_ge(out_weights.w_in, 8 * 16)
            act.activation(whi[:], wst[:], ACT.Copy).then_inc(w_split, 1)
            act.wait_ge(b_done, 1)
            r.act_gate(act)

            def add_bias(b):
                for m in range(DM):
                    act.wait_ge(y_ready, b * DM + m + 1)
                    if b >= 2:
                        act.wait_ge(yT_ready, (b - 1) * 2)
                    act.activation(yf[:, b % 2, m, :], k.PS[:, 2 * b + m, :], ACT.Identity, scale=k.modc[:, 0, GA, m, b:b + 1],
                                   bias=gabo[:, m, b:b + 1]).then_inc(yf_done, 1)
            wavefront((0, add_bias), (2, lambda b: r.act_columns(act, b)), (3, lambda b: r.act_logits(act, b)),
                      (4, lambda b: r.act_exp(act, b)), (5, lambda b: r.act_weights(act, b)))

        @block.vector
        def _(dve):
            dve.wait_ge(w_split, 1)
            dve.tensor_tensor(wlo[:], wst[:], f32(whi[:]), ALU.subtract).then_inc(w_split, 1)
            dve.wait_ge(b_in, 16)
            dve.tensor_tensor(gabo[:], k.modc[:, 0, GA], bo[:].unsqueeze(2).to_broadcast([P, DM, B]), ALU.mult).then_inc(b_done, 1)
            r.dve_gate(dve)

            def add(b):
                for g in range(2):
                    dve.wait_ge(yT_ready, b * 2 + g + 1)
                    x = k.X[:, b * TT + 2 * g:b * TT + 2 * g + 2, :]
                    dve.tensor_tensor(x, k.PS[:, 2 * b + g, :].rearrange("p (t d) -> p t d", t=2), x, ALU.add).then_inc(x_done, 1)
                dve.wait_ge(x_done, b * 2 + 2)
                r.dve_stats(dve, b)
                r.dve_norm(dve, b)
            wavefront((1, add), (2, lambda b: r.dve_lo(dve, b)), (3, lambda b: r.dve_center(dve, b)),
                      (4, lambda b: r.dve_choose(dve, b)), (5, lambda b: r.dve_weights_lo(dve, b)))

        @block.tensor
        def _(pe):
            pe.wait_ge(w_split, 2)

            def products(b):
                for m in range(DM):
                    for q in range(QUADS):
                        last = split3(pe, k.PS[:, 2 * b + m, :], whi[:, q, m * P:(m + 1) * P], wlo[:, q, m * P:(m + 1) * P],
                                      OT[0][:, b * QUADS + q, :], OT[1][:, b * QUADS + q, :], q == 0, q == QUADS - 1)
                    last.then_inc(y_ready, 1)

            def to_rows(b):
                pe.wait_ge(yf_done, (b + 1) * DM)
                for g in range(2):
                    for t in (2 * g, 2 * g + 1):
                        for m in range(DM):
                            last = pe.transpose(k.PS[:, 2 * b + g, (t % 2) * D + m * P:(t % 2) * D + m * P + P],
                                                yf[:, b % 2, m, t * P:(t + 1) * P], k.ident[:])
                    last.then_inc(yT_ready, 1)

            def columns(b):
                pe.wait_ge(x_done, b * 2 + 2)
                r.pe_columns(pe, b)
            wavefront((0, products), (1, to_rows), (2, columns), (3, lambda b: r.pe_logits(pe, b)),
                      (4, lambda b: r.pe_rows(pe, b)), (5, lambda b: r.pe_weights(pe, b)))


W13 = 2 * DM * P
WC = W13 + P
WALL = WC + D


class ExpertWeights:

    def __init__(self, k, layer, c):
        self.st = k.sb(f"e{layer}_st", [P, 2, WALL], F32, c, "right")
        self.w_in = [k.lasting_sem(f"e{layer}_in{i}") for i in range(2)]

    def load(self, sp, w, tile, par):
        sp.dma_start(self.st[:, par, :], w[tile]).then_inc(self.w_in[par], 16)


def experts(k, layer, hT, combT, weights, w, tiles, groups, out, prefetch=None):
    nc = k.nc
    HALVES, C = 2, B // 2
    with ExitStack() as c:
        nm = lambda s: f"e{layer}_{s}"
        wst, w_in = weights.st, weights.w_in
        whi = k.sb(nm("whi"), [P, 2, WALL], F32R, c)
        wlo = k.sb(nm("wlo"), [P, 2, WALL], F32R, c)
        sg = k.sb(nm("sg"), [P, 2, T], F32, c)
        cb = k.sb(nm("cb"), [P, 2, T], F32, c)
        um = k.sb(nm("um"), [P, 2, T], F32, c)
        hf = k.sb(nm("hf"), [P, 2, T], F32, c)
        hhi = k.sb(nm("hhi"), [P, 4, T], F32R, c)
        hlo = k.sb(nm("hlo"), [P, 4, T], F32R, c)
        yf = k.sb(nm("yf"), [P, C, DM, T], F32, c)
        S = lambda s: k.sem(nm(s))
        w_split, w13_done, w2_done = S("w_split"), S("w13_done"), S("w2_done")
        g_ready, u_ready, c_ready, y_done = S("g_ready"), S("u_ready"), S("c_ready"), S("y_done")
        silu_done, cb_done, um_done, h_done, hi_done, lo_done = (
            S("silu_done"), S("cb_done"), S("um_done"), S("h_done"), S("hi_done"), S("lo_done"))
        yf_done, yT_ready, x_done, x_out = S("yf_done"), S("yT_ready"), S("x_done"), S("x_out")
        block = c.enter_context(nc.Block())
        PER = tiles // groups
        PEEL = 2 + PER % 2

        def each_tile(eng, half, body):
            for group in range(groups):
                first = group * PER
                base = half * tiles + first
                for t in range(PEEL):
                    body(first + t, base + t, (base + t) % 2, group)
                with eng.Fori(0, (PER - PEEL) // 2) as pair:
                    for j in range(2):
                        t = pair * 2 + (PEEL + j)
                        body(first + t, base + t, (base + PEEL + j) % 2, group)

        def spreads(t):
            return groups == 1 or (isinstance(t, int) and t % PER == 0)

        def spread_count(half, group, n, j):
            return n + 1 if groups == 1 else (half * groups + group) * C + j + 1

        @block.sync
        def _(sp):
            def load(t, g, par, group):
                if not (isinstance(g, int) and g < 2):
                    sp.wait_ge(w2_done, g - 1)
                    weights.load(sp, w, t, par)
            for half in range(HALVES):
                each_tile(sp, half, load)
                if half == 0 and prefetch is not None:
                    prefetch(sp)
            if out is not None:
                for half in range(HALVES):
                    for i in range(2 * C):
                        sp.wait_ge(x_done, 2 * C * half + i + 1)
                        tiles_out = slice(8 * half + 2 * i, 8 * half + 2 * i + 2)
                        sp.dma_start(out.rearrange("(t p) d -> p t d", p=P)[:, tiles_out], k.X[:, tiles_out, :]).then_inc(x_out, 16)
                sp.wait_ge(x_out, HALVES * 2 * C * 16)

        @block.gpsimd
        def _(pool):
            def split(t, g, par, group):
                count = (g - par) * 8 + 16
                for lo, hi, free, done in ((0, WC, c_ready if groups == 1 else u_ready, w13_done), (WC, WALL, y_done, w2_done)):
                    if lo == 0:
                        pool.wait_ge(w_in[par], count)
                    wait(pool, free, 2 * g - 2)
                    pool.tensor_tensor(wlo[:, par, W13:W13 + 1], wst[:, par, 0:1], wst[:, par, 1:2], ALU.mult).then_inc(w_split, 1)
                    pool.tensor_scalar(whi[:, par, lo:hi], wst[:, par, lo:hi], 1.0, 1.0, ALU.mult, ALU.mult).then_inc(w_split, 1)
                    pool.wait_ge(w_split, g * 4 + (2 if lo == 0 else 4))
                    end = min(hi, W13) if lo == 0 else hi
                    pool.tensor_tensor(wlo[:, par, lo:end], wst[:, par, lo:end], f32(whi[:, par, lo:end]), ALU.subtract).then_inc(done, 1)
            for half in range(HALVES):
                each_tile(pool, half, split)

        @block.scalar
        def _(act):
            def split_h(n, s):
                wait(act, h_done, n + 1)
                wait(act, y_done, n - 3)
                act.activation(hhi[:, s % 4, :], hf[:, s % 2, :], ACT.Copy).then_inc(hi_done, 1)

            def steps(t, g, par, group):
                for j in range(C):
                    n, s = 2 * g + j, 2 * par + j
                    if not (isinstance(t, int) and t == 0 and j == 0):
                        split_h(n - 1, s - 1)
                    wait(act, g_ready, n + 1)
                    wait(act, h_done, n - 1)
                    act.activation(sg[:, s % 2, :], k.PS[:, 3 * s % 4, :], ACT.Silu).then_inc(silu_done, 1)
                    if spreads(t):
                        wait(act, c_ready, spread_count(half, group, n, j))
                        wait(act, um_done, n - 1)
                        act.activation(cb[:, j, :], k.PS[:, (3 * s + 2) % 4, :], ACT.Copy).then_inc(cb_done, 1)
            for half in range(HALVES):
                each_tile(act, half, steps)
                N = C * tiles * (half + 1)
                split_h(N - 1, N - 1)
                act.wait_ge(y_done, N)
                for j in range(C):
                    for m in range(DM):
                        if half:
                            act.wait_ge(yT_ready, 4 * half)
                        act.activation(yf[:, j, m, :], k.PS[:, 4 + 2 * j + m, :], ACT.Copy,
                                       scale=k.modc[:, layer, GB, m, C * half + j:C * half + j + 1]).then_inc(yf_done, 1)

        @block.vector
        def _(dve):
            def split_h(n, s):
                wait(dve, hi_done, n + 1)
                wait(dve, y_done, n - 3)
                dve.tensor_tensor(hlo[:, s % 4, :], hf[:, s % 2, :], f32(hhi[:, s % 4, :]), ALU.subtract).then_inc(lo_done, 1)

            def residual(half):
                for i in range(2 * C):
                    dve.wait_ge(yT_ready, 4 * half + i + 1)
                    x = k.X[:, 8 * half + 2 * i:8 * half + 2 * i + 2, :]
                    dve.tensor_tensor(x, k.PS[:, 4 + i, :].rearrange("p (t d) -> p t d", t=2), x, ALU.add).then_inc(x_done, 1)

            def steps(t, g, par, group):
                for j in range(C):
                    n, s = 2 * g + j, 2 * par + j
                    if not (isinstance(t, int) and t == 0 and j == 0):
                        split_h(n - 1, s - 1)
                    wait(dve, u_ready, n + 1)
                    wait(dve, cb_done, spread_count(half, group, n, j))
                    dve.tensor_tensor(um[:, s % 2, :], k.PS[:, (3 * s + 1) % 4, :], cb[:, j, :], ALU.mult).then_inc(um_done, 1)
                    wait(dve, um_done, n + 1)
                    wait(dve, silu_done, n + 1)
                    wait(dve, lo_done, n - 1)
                    dve.tensor_tensor(hf[:, s % 2, :], um[:, s % 2, :], sg[:, s % 2, :], ALU.mult).then_inc(h_done, 1)
                if isinstance(t, int) and t == 0 and half:
                    residual(half - 1)
            for half in range(HALVES):
                each_tile(dve, half, steps)
                N = C * tiles * (half + 1)
                split_h(N - 1, N - 1)
            residual(HALVES - 1)

        @block.tensor
        def _(pe):
            def rows(half):
                for j in range(C):
                    pe.wait_ge(yf_done, 4 * half + 2 * j + 2)
                    for i in range(2):
                        for t in (2 * i, 2 * i + 1):
                            for m in range(DM):
                                ins = pe.transpose(k.PS[:, 4 + 2 * j + i, (t % 2) * D + m * P:(t % 2) * D + m * P + P],
                                                   yf[:, j, m, t * P:(t + 1) * P], k.ident[:])
                        ins.then_inc(yT_ready, 1)

            def into_y(half, t, g, par, j, last=False):
                n, s = 2 * g + j, 2 * par + j
                wait(pe, lo_done, n + 1)
                first = isinstance(t, int) and t == 0
                if j == 0:
                    wait(pe, w2_done, g + 1)
                if first and half:
                    pe.wait_ge(x_done, 4 * half)
                for m in range(DM):
                    ins = split3(pe, k.PS[:, 4 + 2 * j + m, :], whi[:, par, WC + m * P:WC + (m + 1) * P],
                                 wlo[:, par, WC + m * P:WC + (m + 1) * P], hhi[:, s % 4, :], hlo[:, s % 4, :], first, last)
                ins.then_inc(y_done, 1)

            for half in range(HALVES):
                def steps(t, g, par, group):
                    start = isinstance(t, int) and t == 0
                    for j in range(C):
                        n, s = 2 * g + j, 2 * par + j
                        chunk = slice((C * half + j) * T, (C * half + j + 1) * T)
                        if j == 0:
                            wait(pe, w13_done, g + 1)

                        def spread():
                            wait(pe, um_done, n)
                            pe.matmul(k.PS[:, (3 * s + 2) % 4, :], whi[:, par, W13:WC], combT[:, chunk], start=True, stop=True).then_inc(c_ready, 1)
                        if groups > 1 and spreads(t):
                            spread()
                        for i, (done, count) in enumerate(((um_done, n - 1), (silu_done, n))):
                            wait(pe, done, count)
                            for d in range(DM):
                                at = (i * DM + d) * P
                                ins = split3(pe, k.PS[:, (3 * s + i) % 4, :], whi[:, par, at:at + P], wlo[:, par, at:at + P],
                                             hT[0][:, d, chunk], hT[1][:, d, chunk], d == 0, d == DM - 1)
                            ins.then_inc((g_ready, u_ready)[i], 1)
                        if groups == 1:
                            spread()
                        if not start:
                            into_y(half, t - 1, g - 1, 1 - par, j)
                    if start and half:
                        rows(half - 1)
                each_tile(pe, half, steps)
                g = (half + 1) * tiles - 1
                for j in range(C):
                    into_y(half, tiles - 1, g, g % 2, j, True)
            rows(HALVES - 1)


class ConvWeights:

    def __init__(self, k, c, w_in, w_out, taps):
        self.arrays = w_in.rearrange("(m p) n -> p m n", p=P), w_out.rearrange("(e p) n -> p e n", p=P), taps
        self.wi = k.sb("c_wi_st", [P, DM, 2 * INNER], F32, c)
        self.wo = k.sb("c_wo_st", [P, IT, D], F32, c)
        self.tap = k.sb("c_tap", [P, IT, TAPS + 1], F32, c)
        self.w_in = k.sem("c_w_in")

    def load(self, sp):
        for tile, array in zip((self.wi, self.wo, self.tap), self.arrays):
            sp.dma_start(tile[:], array).then_inc(self.w_in, 16)


def gated_conv(k, H, hT, weights):
    nc = k.nc
    with ExitStack() as c:
        n = lambda s: f"c_{s}"
        wi_st, wo_st, tap, w_in = weights.wi, weights.wo, weights.tap, weights.w_in
        wi_hi = k.sb(n("wi_hi"), [P, DM, 2 * INNER], F32R, c)
        wi_lo = k.sb(n("wi_lo"), [P, DM, 2 * INNER], F32R, c)
        wo_hi = k.sb(n("wo_hi"), [P, IT, D], F32R, c)
        wo_lo = k.sb(n("wo_lo"), [P, IT, D], F32R, c)
        stats = k.sb(n("stats"), [P, TT, 6], F32, c)
        mv = k.sb(n("mv"), [P, TT, 2], F32, c)
        var, rs = k.sb(n("var"), [P, 3, TT], F32, c), k.sb(n("rs"), [P, 3, TT], F32, c)
        ss, sq = k.sb(n("ss"), [P, 2, TT], F32, c), k.sb(n("sq"), [P, 2, TT, D], F32, c)
        hn = k.sb(n("hn"), [P, 2, TT, D], F32, c)
        rhi, rlo = k.sb(n("rhi"), [P, 2, DM, T], F32R, c), k.sb(n("rlo"), [P, 2, DM, T], F32R, c)
        acc = k.sb(n("acc"), [P, 2, T], F32, c)
        sx, sz = k.sb(n("sx"), [P, 2, T], F32, c), k.sb(n("sz"), [P, 2, T], F32, c)
        yv = k.sb(n("yv"), [P, IT, T], F32, c)
        yhi, ylo = k.sb(n("yhi"), [P, IT, T], F32R, c), k.sb(n("ylo"), [P, IT, T], F32R, c)
        yf = k.sb(n("yf"), [P, DM, T], F32, c)
        S = lambda s: k.sem(n(s))
        w_hi, w_lo, own_dve = S("w_hi"), S("w_lo"), S("dve")
        LN, IN, OUT = 0, 1, 2
        var_ready, root_done = [S(f"var_ready{i}") for i in range(3)], [S(f"root_done{i}") for i in range(3)]
        h_ready, h_added = S("h_ready"), S("h_added")
        ss_done, hn_ready, rT_ready = ([S(f"{s}{i}") for i in range(2)] for s in ("ss_done", "hn_ready", "rT_ready"))
        rhi_done, rlo_done = ([S(f"{s}{i}") for i in range(2)] for s in ("rhi_done", "rlo_done"))
        p_ready, z_ready, conv_done, sx_done, sz_done = S("p_ready"), S("z_ready"), S("conv_done"), S("sx_done"), S("sz_done")
        yv_done, yhi_done, ylo_done, o_done = S("yv_done"), S("yhi_done"), S("ylo_done"), S("o_done")
        yf_done, yT_ready = S("yf_done"), S("yT_ready")
        block = c.enter_context(nc.Block())

        turns = []
        wavefront((2, lambda b: turns.append(("rows", b))), (0, lambda b: turns.append((IN, b))),
                  (2, lambda b: turns.append((OUT, b))))

        def wait_turn(pe, kind, b):
            at = turns.index((kind, b))
            if at:
                before, bb = turns[at - 1]
                pe.wait_ge(h_added if before == "rows" else rlo_done[before - 1], DM * (bb + 1))

        @block.gpsimd
        def _(pool):
            def root(kind):
                def stage(b):
                    pool.wait_ge(var_ready[kind], b + 1)
                    pool.tensor_tensor(rs[:, kind], var[:, kind], k.mhalf[:, 0:TT], ALU.pow).then_inc(root_done[kind], 1)
                    if b == 0 and kind != OUT:
                        lo, st, hi = ((wi_lo, wi_st, wi_hi), (wo_lo, wo_st, wo_hi))[kind]
                        pool.wait_ge(w_hi, kind + 1)
                        pool.tensor_tensor(lo[:], st[:], f32(hi[:]), ALU.subtract).then_inc(w_lo, 1)
                return stage

            def gate(e):
                def stage(b):
                    i = b * IT + e
                    pool.wait_ge(sx_done, i + 1)
                    pool.wait_ge(sz_done, i + 1)
                    if b:
                        pool.wait_ge(ylo_done, i - IT + 1)
                    pool.tensor_tensor(yv[:, e, :], sx[:, i % 2, :], sz[:, i % 2, :], ALU.mult).then_inc(yv_done, 1)
                return stage
            def split_y(e):
                def stage(b):
                    i = b * IT + e
                    pool.wait_ge(yhi_done, i + 1)
                    pool.tensor_tensor(ylo[:, e, :], yv[:, e, :], f32(yhi[:, e, :]), ALU.subtract).then_inc(ylo_done, 1)
                return stage
            wavefront((1, gate(0)), (2, split_y(3)), (0, root(LN)), (1, gate(1)), (1, split_y(0)), (0, root(IN)), (1, gate(2)),
                      (1, split_y(1)), (2, root(OUT)), (1, gate(3)), (1, split_y(2)))

        @block.scalar
        def _(act):
            def y_out(b):
                act.wait_ge(o_done, (b + 1) * IT)
                if b:
                    act.wait_ge(yT_ready, 2 * b)
                for m in range(DM):
                    act.activation(yf[:, m, :], k.PS[:, 6 + m, :], ACT.Copy).then_inc(yf_done, 1)

            def silu_z(e):
                def stage(b):
                    i = b * IT + e
                    act.wait_ge(z_ready, i + 1)
                    if i >= 2:
                        act.wait_ge(yv_done, i - 1)
                    act.activation(sz[:, i % 2, :], k.PS[:, 3 + 2 * (i % 2), :], ACT.Silu).then_inc(sz_done, 1)
                return stage

            def silu_x(e):
                def stage(b):
                    i = b * IT + e
                    act.wait_ge(conv_done, i + 1)
                    act.activation(sx[:, i % 2, :], acc[:, i % 2, :], ACT.Silu).then_inc(sx_done, 1)
                return stage

            def split_y(e):
                def stage(b):
                    i = b * IT + e
                    act.wait_ge(yv_done, i + 1)
                    if b:
                        act.wait_ge(o_done, i - IT + 1)
                    act.activation(yhi[:, e, :], yv[:, e, :], ACT.Copy).then_inc(yhi_done, 1)
                return stage

            def squares(i):
                def stage(b):
                    act.wait_ge((h_ready, h_added)[i], (1, 2)[i] * (b + 1))
                    if b:
                        act.wait_ge(var_ready[1 + i], b)
                    for t in range(TT):
                        act.activation(sq[:, i, t, :], H[:, b * TT + t, :], ACT.Square,
                                       accum_out=ss[:, i, t:t + 1]).then_inc(ss_done[i], 1)
                return stage

            def hi(i):
                def stage(b):
                    for m in range(DM):
                        act.wait_ge(rT_ready[i], b * DM + m + 1)
                        if i == 0 and b >= 2:
                            act.wait_ge(z_ready, (b - 1) * IT)
                        out = rhi[:, b % 2, m, :] if i == 0 else hT[0][:, m, b * T:(b + 1) * T]
                        act.activation(out, k.PS[:, m, :], ACT.Copy).then_inc(rhi_done[i], 1)
                return stage

            act.wait_ge(w_in, 48)
            act.activation(wi_hi[:], wi_st[:], ACT.Copy).then_inc(w_hi, 1)
            act.activation(wo_hi[:], wo_st[:], ACT.Copy).then_inc(w_hi, 1)
            wavefront((1, silu_z(0)), (3, hi(1)), (1, silu_x(0)), (2, split_y(3)), (1, silu_z(1)), (1, silu_x(1)),
                      (1, split_y(0)), (0, squares(0)), (2, y_out), (1, silu_z(2)), (1, silu_x(2)), (1, split_y(1)),
                      (2, squares(1)), (1, silu_z(3)), (0, hi(0)), (1, silu_x(3)), (1, split_y(2)))

        @block.vector
        def _(dve):
            own = Chain(dve, own_dve)

            def stats_of(b):
                row_stats(own, dve, lambda t: k.X[:, b * TT + t, :], stats, mv)
                dve.tensor_scalar(var[:, LN], mv[:, :, 1], EPS, None, ALU.add).then_inc(var_ready[LN], 1)

            def layer_norm(b):
                dve.wait_ge(root_done[LN], b + 1)
                h = H[:, b * TT:(b + 1) * TT, :]
                for t in range(TT):
                    own.link(dve.tensor_scalar(H[:, b * TT + t, :], k.X[:, b * TT + t, :], mv[:, t, 0:1], rs[:, LN, t:t + 1],
                                               ALU.subtract, ALU.mult))
                own.wait()
                row = lambda part: k.rows[:, 1, part, b, :].unsqueeze(1).to_broadcast([P, TT, D])
                own.link(dve.tensor_tensor(h, h, row(CA), ALU.mult))
                own.wait()
                dve.tensor_tensor(h, h, row(SA), ALU.add).then_inc(h_ready, 1)

            def rms_var(i):
                def stage(b):
                    dve.wait_ge(ss_done[i], (b + 1) * TT)
                    dve.tensor_scalar(var[:, 1 + i], ss[:, i], 1e-24, 1.0 / D, ALU.max, ALU.mult).then_inc(var_ready[1 + i], 1)
                return stage

            def rms(i):
                def stage(b):
                    dve.wait_ge(root_done[1 + i], b + 1)
                    if b:
                        dve.wait_ge(rT_ready[i], b * DM)
                    for t in range(TT):
                        dve.tensor_scalar(hn[:, i, t, :], H[:, b * TT + t, :], rs[:, 1 + i, t:t + 1], None,
                                          ALU.mult).then_inc(hn_ready[i], 1)
                return stage

            def lo(i):
                def stage(b):
                    cols = slice(b * T, (b + 1) * T)
                    for m in range(DM):
                        dve.wait_ge(rhi_done[i], b * DM + m + 1)
                        hi, out = (rhi[:, b % 2, m, :], rlo[:, b % 2, m, :]) if i == 0 else (hT[0][:, m, cols], hT[1][:, m, cols])
                        dve.tensor_tensor(out, k.PS[:, m, :], f32(hi), ALU.subtract).then_inc(rlo_done[i], 1)
                return stage

            def conv(e):
                def stage(b):
                    i = b * IT + e
                    p, a = k.PS[:, 2 + 2 * (i % 2), :], acc[:, i % 2, :]
                    dve.wait_ge(p_ready, i + 1)
                    if i >= 2:
                        dve.wait_ge(sx_done, i - 1)
                    own.link(dve.tensor_scalar(a, p, tap[:, e, TAPS - 1:TAPS], tap[:, e, TAPS:TAPS + 1], ALU.mult, ALU.add))
                    for j in range(1, TAPS):
                        own.wait()
                        ins = dve.scalar_tensor_tensor(out=a[:, j:T], in0=p[:, 0:T - j], scalar=tap[:, e, TAPS - 1 - j:TAPS - j],
                                                       in1=a[:, j:T], op0=ALU.mult, op1=ALU.add)
                        if j < TAPS - 1:
                            own.link(ins)
                    ins.then_inc(conv_done, 1)
                return stage

            def add(b):
                for g in range(2):
                    dve.wait_ge(yT_ready, b * 2 + g + 1)
                    x = H[:, b * TT + 2 * g:b * TT + 2 * g + 2, :]
                    dve.tensor_tensor(x, k.PS[:, g, :].rearrange("p (t d) -> p t d", t=2), x, ALU.add).then_inc(h_added, 1)
            wavefront((1, conv(0)), (3, lo(1)), (0, stats_of), (1, conv(1)), (0, layer_norm), (1, conv(2)), (0, rms_var(0)),
                      (2, add), (0, rms(0)), (1, conv(3)), (2, rms_var(1)), (0, lo(0)), (2, rms(1)))

        @block.tensor
        def _(pe):
            def columns(i):
                def stage(b):
                    wait_turn(pe, 1 + i, b)
                    for m in range(DM):
                        for t in range(TT):
                            pe.wait_ge(hn_ready[i], b * TT + t + 1)
                            last = pe.transpose(k.PS[:, m, t * P:(t + 1) * P], hn[:, i, t, m * P:(m + 1) * P], k.ident[:])
                        last.then_inc(rT_ready[i], 1)
                return stage

            def up(e):
                def stage(b):
                    i = b * IT + e
                    if i == 0:
                        pe.wait_ge(w_lo, 1)
                    if e == 0:
                        pe.wait_ge(rlo_done[0], (b + 1) * DM)
                    for part, (free, done) in enumerate(((conv_done, p_ready), (sz_done, z_ready))):
                        if i >= 2:
                            pe.wait_ge(free, i - 1)
                        for d in range(DM):
                            at = part * INNER + e * P
                            last = split3(pe, k.PS[:, 2 + 2 * (i % 2) + part, :], wi_hi[:, d, at:at + P], wi_lo[:, d, at:at + P],
                                          rhi[:, b % 2, d, :], rlo[:, b % 2, d, :], d == 0, d == DM - 1)
                        last.then_inc(done, 1)
                return stage

            def down(e):
                def stage(b):
                    i = b * IT + e
                    if e == 0 and b:
                        pe.wait_ge(yf_done, b * DM)
                    if i == 0:
                        pe.wait_ge(w_lo, 2)
                    pe.wait_ge(ylo_done, i + 1)
                    for m in range(DM):
                        last = split3(pe, k.PS[:, 6 + m, :], wo_hi[:, e, m * P:(m + 1) * P], wo_lo[:, e, m * P:(m + 1) * P],
                                      yhi[:, e, :], ylo[:, e, :], e == 0, e == IT - 1)
                    last.then_inc(o_done, 1)
                return stage

            def rows(b):
                wait_turn(pe, "rows", b)
                pe.wait_ge(yf_done, (b + 1) * DM)
                for g in range(2):
                    for t in (2 * g, 2 * g + 1):
                        for m in range(DM):
                            last = pe.transpose(k.PS[:, g, (t % 2) * D + m * P:(t % 2) * D + m * P + P],
                                                yf[:, m, t * P:(t + 1) * P], k.ident[:])
                    last.then_inc(yT_ready, 1)
            wavefront((2, down(2)), (1, up(1)), (2, down(3)), (1, up(2)), (2, rows), (1, down(0)), (1, up(3)),
                      (0, columns(0)), (1, down(1)), (0, up(0)), (2, columns(1)))


def mlp_and_route(k, H, hT, w_d, combT, gate_w, expert_weights, w):
    nc = k.nc
    WM = DM * P
    STAGED = 4
    with ExitStack() as c:
        n = lambda s: f"m_{s}"
        wst = k.sb(n("wst"), [P, STAGED, WM + D], F32, c)
        whi = k.sb(n("whi"), [P, MLP_T, WM + D], F32R, c)
        wlo = k.sb(n("wlo"), [P, MLP_T, WM + D], F32R, c)
        hi, lo = k.sb(n("hi"), [P, 4, T], F32R, c), k.sb(n("lo"), [P, 4, T], F32R, c)
        yf = k.sb(n("yf"), [P, DM, T], F32, c)
        S = lambda s: k.sem(n(s))
        w_in = [S(f"w_in{i}") for i in range(STAGED)]
        whi_done, wlo_done = S("whi_done"), S("wlo_done")
        u_ready, hi_done, lo_done, o_done = S("u_ready"), S("hi_done"), S("lo_done"), S("o_done")
        yf_done, yT_ready, x_done, own_dve = S("yf_done"), S("yT_ready"), S("x_done"), S("dve")
        r = Route(k, 1, hT, combT, L1_EXPERTS, 1, 1, lambda b: 6, c)
        block = c.enter_context(nc.Block())

        def interleave(tile, *others):
            for b in range(B + 2):
                for i in range(MLP_T):
                    if b < B:
                        tile(b, i)
                    for back, at, stage in others:
                        if at == i and 0 <= b - back < B:
                            stage(b - back)

        def split_weights(b, i, split):
            if b == 0:
                for j in range(0 if i == 0 else i + 2, min(i + 3, MLP_T)):
                    split(j)

        @block.sync
        def _(sp):
            for i in range(MLP_T):
                if i >= STAGED:
                    sp.wait_ge(wlo_done, i - STAGED + 1)
                sp.dma_start(wst[:, i % STAGED, :], w_d[i]).then_inc(w_in[i % STAGED], 16)
            r.load(sp, gate_w)
            for tile in range(2):
                expert_weights.load(sp, w, tile, tile)

        @block.gpsimd
        def _(pool):
            r.fill(pool)
            wavefront((0, lambda b: r.root(pool, b)))

        @block.scalar
        def _(act):
            def split(i):
                act.wait_ge(w_in[i % STAGED], 16 * (i // STAGED + 1))
                act.activation(whi[:, i, :], wst[:, i % STAGED, :], ACT.Copy).then_inc(whi_done, 1)

            def tile(b, i):
                split_weights(b, i, split)
                act.wait_ge(u_ready, b * MLP_T + i + 1)
                wait(act, o_done, b * MLP_T + i - 3)
                act.activation(hi[:, i % 4, :], k.PS[:, i % 4, :], ACT.Relu).then_inc(hi_done, 1)

            def result(b):
                act.wait_ge(o_done, (b + 1) * MLP_T)
                if b:
                    act.wait_ge(yT_ready, b * 2)
                for m in range(DM):
                    act.activation(yf[:, m, :], k.PS[:, 4 + m, :], ACT.Copy, scale=k.modc[:, 1, GA, m, b:b + 1]).then_inc(yf_done, 1)
            interleave(tile, (0, 7, result), (1, 0, lambda b: r.act_gate(act) if b == 0 else None),
                       (1, 5, lambda b: r.act_columns(act, b)), (1, 6, lambda b: r.act_logits(act, b)),
                       (1, 7, lambda b: r.act_exp(act, b)), (2, 1, lambda b: r.act_weights(act, b)))

        @block.vector
        def _(dve):
            own = Chain(dve, own_dve)

            def split(i):
                dve.wait_ge(whi_done, i + 1)
                dve.tensor_tensor(wlo[:, i, :], wst[:, i % STAGED, :], f32(whi[:, i, :]), ALU.subtract).then_inc(wlo_done, 1)

            def tile(b, i):
                split_weights(b, i, split)
                dve.wait_ge(hi_done, b * MLP_T + i + 1)
                wait(dve, o_done, b * MLP_T + i - 3)
                dve.scalar_tensor_tensor(out=lo[:, i % 4, :], in0=k.PS[:, i % 4, :], scalar=0.0, in1=f32(hi[:, i % 4, :]),
                                         op0=ALU.max, op1=ALU.subtract).then_inc(lo_done, 1)

            def add_h(b):
                h, x = H[:, b * TT:(b + 1) * TT, :], k.X[:, b * TT:(b + 1) * TT, :]
                own.link(dve.tensor_tensor(h, h, k.rows[:, 1, GA, b, :].unsqueeze(1).to_broadcast([P, TT, D]), ALU.mult))
                own.wait()
                own.link(dve.tensor_tensor(x, x, h, ALU.add))
                own.wait()

            def residual(b):
                for g in range(2):
                    dve.wait_ge(yT_ready, b * 2 + g + 1)
                    x = k.X[:, b * TT + 2 * g:b * TT + 2 * g + 2, :]
                    dve.tensor_tensor(x, k.PS[:, 6 + g, :].rearrange("p (t d) -> p t d", t=2), x, ALU.add).then_inc(x_done, 1)
                dve.wait_ge(x_done, b * 2 + 2)
                if b == 0:
                    r.dve_gate(dve)
                r.dve_stats(dve, b)
            interleave(tile, (0, 5, add_h), (1, 2, residual), (1, 4, lambda b: r.dve_norm(dve, b)), (1, 5, lambda b: r.dve_lo(dve, b)),
                       (1, 7, lambda b: r.dve_center(dve, b)), (2, 0, lambda b: r.dve_choose(dve, b)),
                       (2, 1, lambda b: r.dve_weights_lo(dve, b)))

        @block.tensor
        def _(pe):
            def up(b, i):
                if b == 0:
                    pe.wait_ge(wlo_done, i + 1)
                wait(pe, lo_done, b * MLP_T + i - 3)
                for d in range(DM):
                    cols = slice(b * T, (b + 1) * T)
                    last = split3(pe, k.PS[:, i % 4, :], whi[:, i, d * P:(d + 1) * P], wlo[:, i, d * P:(d + 1) * P],
                                  hT[0][:, d, cols], hT[1][:, d, cols], d == 0, d == DM - 1)
                last.then_inc(u_ready, 1)

            def down(i):
                def stage(b):
                    if i == 0 and b:
                        pe.wait_ge(yf_done, b * DM)
                    pe.wait_ge(lo_done, b * MLP_T + i + 1)
                    for m in range(DM):
                        last = split3(pe, k.PS[:, 4 + m, :], whi[:, i, WM + m * P:WM + (m + 1) * P], wlo[:, i, WM + m * P:WM + (m + 1) * P],
                                      hi[:, i % 4, :], lo[:, i % 4, :], i == 0, i == MLP_T - 1)
                    last.then_inc(o_done, 1)
                return stage

            def rows(b):
                pe.wait_ge(yf_done, (b + 1) * DM)
                if b:
                    pe.wait_ge(r.cf_done, 2 * b)
                for g in range(2):
                    for t in (2 * g, 2 * g + 1):
                        for m in range(DM):
                            last = pe.transpose(k.PS[:, 6 + g, (t % 2) * D + m * P:(t % 2) * D + m * P + P],
                                                yf[:, m, t * P:(t + 1) * P], k.ident[:])
                    last.then_inc(yT_ready, 1)
            interleave(up, (2, 1, lambda b: r.pe_weights(pe, b)), (1, 2, rows), (1, 5, lambda b: r.pe_columns(pe, b)),
                       (1, 6, lambda b: r.pe_logits(pe, b)), (1, 7, lambda b: r.pe_rows(pe, b)),
                       *((0, i + 2, down(i)) for i in range(MLP_T - 2)), (0, 7, down(MLP_T - 2)), (0, 7, down(MLP_T - 1)))


def layout(a):
    import numpy as np

    def cols(*vs):
        return np.ascontiguousarray(np.stack([v.reshape(DM, P) for v in vs]).transpose(2, 0, 1))

    o = {"x": a["L0_attn_X"].reshape(B * T, D)}
    o["cT"] = np.ascontiguousarray(np.stack([a["L0_c"], a["L1_c"]]).reshape(2, B, DM, P).transpose(3, 0, 2, 1))
    o["wmod0"], o["wmod1"] = a["L0_wmod"], a["L1_wmod"]
    o["wqkv"] = np.stack([a["L0_attn_Wq"], a["L0_attn_Wk"], a["L0_attn_Wv"]])
    o["ln_gb"] = cols(a["L0_attn_ln_g"], a["L0_attn_ln_b"])
    o["bqk"] = cols(a["L0_attn_bq"], a["L0_attn_bk"])
    o["bv"] = a["L0_attn_bv"]
    o["wo"] = a["L0_attn_Wo"]
    o["bo"] = np.ascontiguousarray(a["L0_attn_bo"].reshape(DM, P).T)

    def gate(g):
        full = np.zeros((P, DM, P), np.float32)
        full[:, :, :g.shape[0]] = g.reshape(-1, DM, P).transpose(2, 1, 0)
        return full

    def blocks(w1, w3, w2, experts, ff, tiles):
        full = np.zeros((tiles, P, WALL), np.float32)
        up = np.zeros((2, tiles * P, D), np.float32)
        up[0, :w1.shape[0]], up[1, :w3.shape[0]] = w1, w3
        full[:, :, :W13] = up.reshape(2, tiles, P, DM, P).transpose(1, 4, 0, 3, 2).reshape(tiles, P, W13)
        row = np.minimum(np.arange(tiles * P) // ff, experts)
        row[row == experts] = ONE
        for part in (0, GROW):
            sel = np.zeros((tiles * P, P), np.float32)
            sel[np.arange(tiles * P), row + part] = 1.0
            full[:, :, W13:WC] += sel.reshape(tiles, P, P).transpose(0, 2, 1)
        down = np.zeros((tiles * P, D), np.float32)
        down[:w2.shape[1]] = w2.T
        full[:, :, WC:] = down.reshape(tiles, P, D)
        return full

    o["gate0"], o["gate1"] = gate(a["L0_ffn_Wg"]), gate(a["L1_ffn_gate_w"])
    flat = lambda v: v.reshape(-1, D)
    down = lambda v: v.transpose(1, 0, 2).reshape(D, -1)
    o["ffn0"] = blocks(np.concatenate([flat(a["L0_ffn_W1"]), a["L0_ffn_W1s"]]), np.concatenate([flat(a["L0_ffn_W3"]), a["L0_ffn_W3s"]]),
                       np.concatenate([down(a["L0_ffn_W2"]), a["L0_ffn_W2s"]], 1), L0_EXPERTS, L0_FF, L0_TILES)
    o["ffn1"] = blocks(flat(a["L1_ffn_w_gate"]), flat(a["L1_ffn_w_up"]), down(a["L1_ffn_w_down"]), L1_EXPERTS, L1_FF, L1_TILES)
    o["conv_in"] = np.ascontiguousarray(a["L1_attn_W_in"].T)
    o["conv_out"] = np.ascontiguousarray(a["L1_attn_W_out"].T)
    o["taps"] = np.ascontiguousarray(np.concatenate([a["L1_attn_conv_w"][:, 0], a["L1_attn_conv_b"][:, None]], 1)
                                     .reshape(IT, P, TAPS + 1).transpose(1, 0, 2))
    o["mlp"] = np.concatenate([a["L1_attn_W_mlp1"].reshape(MLP_T, P, DM, P).transpose(0, 3, 2, 1).reshape(MLP_T, P, D),
                               a["L1_attn_W_mlp2"].T.reshape(MLP_T, P, D)], 2)
    return o


def program(nc, a, out):
    with ExitStack() as ctx:
        k = Core(nc, ctx)
        with ExitStack() as layer0:
            with ExitStack() as c:
                with ExitStack() as att:
                    heads = Heads(k, att)
                    setup(k, heads, a["x"], a["cT"], a["wmod0"], a["wmod1"])
                    attention_inputs(k, heads, a["wqkv"], a["ln_gb"], a["bqk"], a["bv"])
                    OT = [k.sb(f"OT{i}", [P, B * QUADS, T], F32R, c) for i in range(2)]
                    out_weights = OutputWeights(k, c)
                    attention(k, heads, OT, out_weights, a["wo"])
                hT = [k.sb(f"hT{i}", [P, DM, B * T], F32R, side="right") for i in range(2)]
                combT = k.sb("combT", [P, B * T], F32R, side="right")
                weights = ExpertWeights(k, 0, layer0)
                attention_output_and_route(k, OT, out_weights, a["bo"], hT, combT, a["gate0"], weights, a["ffn0"])
            k.recycle()
            with ExitStack() as c:
                conv = ConvWeights(k, c, a["conv_in"], a["conv_out"], a["taps"])
                H = k.sb("H", [P, NT, D], F32, c)
                experts(k, 0, hT, combT, weights, a["ffn0"], L0_TILES, 1, None, conv.load)
                layer0.close()
                gated_conv(k, H, hT, conv)
                weights = ExpertWeights(k, 1, ctx)
                mlp_and_route(k, H, hT, a["mlp"], combT, a["gate1"], weights, a["ffn1"])
        experts(k, 1, hT, combT, weights, a["ffn1"], L1_TILES, L1_EXPERTS, out)


def kernel(**inputs):
    import numpy as np
    import concourse.bacc as bacc
    from concourse.bass_utils import run_bass_kernel_spmd

    nc = bacc.Bacc("TRN2", target_bir_lowering=False, num_devices=1)
    arrays = {f"in_{n}": np.ascontiguousarray(v) for n, v in layout(inputs).items()}
    aps = {n[3:]: nc.dram_tensor(n, v.shape, mybir.dt.from_np(v.dtype), kind="ExternalInput").ap() for n, v in arrays.items()}
    out = nc.dram_tensor("out", (B * T, D), F32, kind="ExternalOutput").ap()
    program(nc, aps, out)
    got = run_bass_kernel_spmd(nc, [arrays], core_ids=[0])
    return got.results[0]["out"].reshape(B, T, D)
```
